# Optimizing a Trainium2 kernel written in Bass

```python
import numpy as np
import jax
import jax.numpy as jnp

def _softmax(x, axis=-1):
    return jax.nn.softmax(x, axis=axis)

def _gelu(x):
    return jax.nn.gelu(x, approximate=True)

def _silu(x):
    return jax.nn.silu(x)

def _sigmoid(x):
    return jax.nn.sigmoid(x)

def _layernorm(x, axis=-1, eps=1e-05):
    m = jnp.mean(x, axis=axis, keepdims=True)
    v = jnp.var(x, axis=axis, keepdims=True)
    return (x - m) / jnp.sqrt(v + eps)

def _scatter_add(tgt, idx, src, axis=0):
    return tgt.at[idx].add(src)

def _segment_sum(src, seg, n):
    return jax.ops.segment_sum(src, seg, n)
kernel_name = 'mk_macaron_d2_jaxref_r8_d55bcf'

def setup_inputs(seed: int=0):
    np.random.seed(seed)
    _w = jnp.asarray

    def _L0_attn_setup():
        import jax, jax.numpy as jnp
        import numpy as np
        B, S, D_MODEL, H, D = (2, 256, 128, 16, 64)
        SCALE = 1.0 / float(np.sqrt(D))

        def _rope(t, c, s):
            d2 = t.shape[-1] // 2
            t1, t2 = (t[..., :d2], t[..., d2:])
            return jnp.concatenate([t1 * c - t2 * s, t1 * s + t2 * c], axis=-1)
        key = jax.random.key(seed)
        ks = jax.random.split(key, 5)
        x = jax.random.normal(ks[0], (B, S, D_MODEL), jnp.float32)
        qkv_w = jax.random.normal(ks[1], (3 * H * D, D_MODEL), jnp.float32) * 0.02
        out_w = jax.random.normal(ks[2], (D_MODEL, H * D), jnp.float32) * 0.02
        bias_p = jax.random.uniform(ks[3], (H, 1, 1), jnp.float32) * 2.0
        bias_a = jax.random.uniform(ks[4], (H, 1, 1), jnp.float32)
        rope_freqs = 10000.0 ** (-jnp.arange(D // 2, dtype=jnp.float32) / (D // 2))
        return {'x': x, 'qkv_w': qkv_w, 'out_w': out_w, 'bias_p': bias_p, 'bias_a': bias_a, 'rope_freqs': rope_freqs}
    _L0_attn_in = _L0_attn_setup()

    def _L0_ffn_setup():
        import jax, jax.numpy as jnp
        import numpy as np
        B, S, D = (2, 256, 128)
        E, K, F = (16, 2, 64)
        FS = 128
        key = jax.random.key(seed)
        ks = jax.random.split(key, 8)

        def w(k, shape, fan_in):
            return jax.random.normal(k, shape, jnp.float32) / np.sqrt(fan_in).astype(np.float32)
        return {'x': jax.random.normal(ks[0], (B, S, D), jnp.float32), 'Wr': w(ks[1], (D, E), D), 'Wg': w(ks[2], (E, D, F), D), 'Wu': w(ks[3], (E, D, F), D), 'Wd': w(ks[4], (E, F, D), F), 'Sg': w(ks[5], (D, FS), D), 'Su': w(ks[6], (D, FS), D), 'Sd': w(ks[7], (FS, D), FS)}
    _L0_ffn_in = _L0_ffn_setup()

    def _L1_attn_setup():
        import jax, jax.numpy as jnp
        import numpy as np
        H = 16

        def _kernel(x, gamma, beta):
            mean = x.mean(axis=-1, keepdims=True)
            std = jnp.std(x, axis=-1, ddof=1, keepdims=True)
            xn = (x - mean) / (std + 1e-06)
            return jnp.square(gamma * xn + beta)
        key = jax.random.key(seed)
        ks = jax.random.split(key, 9)
        B, T, C = (2, 256, 128)
        x = jax.random.normal(ks[0], (B, T, C), jnp.float32)
        Wqkv = jax.random.normal(ks[1], (C, 3 * C), jnp.float32) * 0.02
        bqkv = jnp.zeros((3 * C,), jnp.float32)
        gamma_q = jax.random.uniform(ks[2], (C,), jnp.float32)
        beta_q = jax.random.uniform(ks[3], (C,), jnp.float32)
        gamma_k = jax.random.uniform(ks[4], (C,), jnp.float32)
        beta_k = jax.random.uniform(ks[5], (C,), jnp.float32)
        Wo = jax.random.normal(ks[6], (C, C), jnp.float32) * 0.02
        bo = jnp.zeros((C,), jnp.float32)
        return {'x': x, 'Wqkv': Wqkv, 'bqkv': bqkv, 'gamma_q': gamma_q, 'beta_q': beta_q, 'gamma_k': gamma_k, 'beta_k': beta_k, 'Wo': Wo, 'bo': bo}
    _L1_attn_in = _L1_attn_setup()

    def _L1_ffn_setup():
        import jax, jax.numpy as jnp
        import numpy as np
        DIM = 128
        DEPTH = 2
        HEADS = 8
        DIM_HEAD = 64
        WINDOW = 64
        INNER = HEADS * DIM_HEAD
        HID = int(DIM * 4 * 2 / 3)
        B, N = (2, 1024)
        QK_SCALE = 8.0

        def shift_token(t):
            t1, t2 = jnp.split(t, 2, axis=-1)
            t2 = jnp.pad(t2, ((0, 0), (1, 0), (0, 0)))[:, :-1]
            return jnp.concatenate([t1, t2], axis=-1)

        def l2norm(t):
            return t / jnp.clip(jnp.linalg.norm(t, axis=-1, keepdims=True), 1e-12)

        def rotate_half(x):
            x1, x2 = jnp.split(x, 2, axis=-1)
            return jnp.concatenate([-x2, x1], axis=-1)

        def rotary_xpos(q, k):
            n = q.shape[-2]
            half_idx = jnp.arange(0, DIM_HEAD, 2, dtype=jnp.float32)
            inv_freq = 1.0 / 10000.0 ** (half_idx / DIM_HEAD)
            t = jnp.arange(n, dtype=jnp.float32)
            freqs = t[:, None] * inv_freq[None, :]
            freqs = jnp.concatenate([freqs, freqs], axis=-1)
            base = (half_idx + 0.4 * DIM_HEAD) / (1.4 * DIM_HEAD)
            power = (t - n // 2) / float(WINDOW // 2)
            scale = base[None, :] ** power[:, None]
            scale = jnp.concatenate([scale, scale], axis=-1)
            cos, sin = (jnp.cos(freqs), jnp.sin(freqs))
            q = q * cos * scale + rotate_half(q) * sin * scale
            k = k * cos / scale + rotate_half(k) * sin / scale
            return (q, k)

        def local_attention(q, k, v):
            b, h, n, d = q.shape
            w = n // WINDOW
            bq = q.reshape(b, h, w, WINDOW, d) * QK_SCALE
            bk = k.reshape(b, h, w, WINDOW, d)
            bv = v.reshape(b, h, w, WINDOW, d)

            def look_around(t):
                p = jnp.pad(t, ((0, 0), (0, 0), (1, 0), (0, 0), (0, 0)))
                return jnp.concatenate([p[:, :, :w], p[:, :, 1:]], axis=3)
            bk, bv = (look_around(bk), look_around(bv))
            bt = jnp.arange(n).reshape(w, WINDOW)
            btp = jnp.pad(bt, ((1, 0), (0, 0)), constant_values=-1)
            btk = jnp.concatenate([btp[:w], btp[1:]], axis=1)
            sim = jnp.einsum('bhwid,bhwjd->bhwij', bq, bk)
            i = bt[:, :, None]
            j = btk[:, None, :]
            mask = (i < j) | (i > j + WINDOW) | (j == -1)
            sim = jnp.where(mask, -jnp.finfo(sim.dtype).max, sim)
            attn = jax.nn.softmax(sim, axis=-1)
            out = jnp.einsum('bhwij,bhwjd->bhwid', attn, bv)
            return out.reshape(b, h, n, d)

        def _layer(x, wqkv, qs, ksc, wo, lg, lb, w1, b1, w2, b2):
            b, n, _ = x.shape
            h = shift_token(x)
            qkv = h @ wqkv
            q, k, v = jnp.split(qkv, 3, axis=-1)
            to_heads = lambda t: t.reshape(b, n, HEADS, DIM_HEAD).transpose(0, 2, 1, 3)
            q, k, v = (to_heads(q), to_heads(k), to_heads(v))
            q = l2norm(q) * qs
            k = l2norm(k) * ksc
            q, k = rotary_xpos(q, k)
            o = local_attention(q, k, v)
            o = o.transpose(0, 2, 1, 3).reshape(b, n, INNER)
            x = x + o @ wo
            h = shift_token(x)
            mu = h.mean(-1, keepdims=True)
            var = h.var(-1, keepdims=True)
            h = (h - mu) / jnp.sqrt(var + 1e-05) * lg + lb
            h = h @ w1 + b1
            a, g = jnp.split(h, 2, axis=-1)
            h = a * jax.nn.gelu(g, approximate=False)
            x = x + h @ w2 + b2
            return x
        key = jax.random.key(seed)
        ks = jax.random.split(key, 6)
        return {'x': jax.random.normal(ks[0], (B, N, DIM), jnp.float32), 'wqkv': jax.random.normal(ks[1], (DEPTH, DIM, 3 * INNER), jnp.float32) * 0.02, 'q_scale': jnp.ones((DEPTH, DIM_HEAD), jnp.float32), 'k_scale': jnp.ones((DEPTH, DIM_HEAD), jnp.float32), 'wo': jax.random.normal(ks[2], (DEPTH, INNER, DIM), jnp.float32) * 0.02, 'ln_g': jnp.ones((DEPTH, DIM), jnp.float32), 'ln_b': jnp.zeros((DEPTH, DIM), jnp.float32), 'w1': jax.random.normal(ks[3], (DEPTH, DIM, 2 * HID), jnp.float32) * 0.02, 'b1': jnp.zeros((DEPTH, 2 * HID), jnp.float32), 'w2': jax.random.normal(ks[4], (DEPTH, HID, DIM), jnp.float32) * 0.02, 'b2': jnp.zeros((DEPTH, DIM), jnp.float32)}
    _L1_ffn_in = _L1_ffn_setup()
    _d = {'L0_attn_x': _L0_attn_in['x'], 'L0_attn_qkv_w': _L0_attn_in['qkv_w'], 'L0_attn_out_w': _L0_attn_in['out_w'], 'L0_attn_bias_p': _L0_attn_in['bias_p'], 'L0_attn_bias_a': _L0_attn_in['bias_a'], 'L0_attn_rope_freqs': _L0_attn_in['rope_freqs'], 'L0_ffn_Wr': _L0_ffn_in['Wr'], 'L0_ffn_Wg': _L0_ffn_in['Wg'], 'L0_ffn_Wu': _L0_ffn_in['Wu'], 'L0_ffn_Wd': _L0_ffn_in['Wd'], 'L0_ffn_Sg': _L0_ffn_in['Sg'], 'L0_ffn_Su': _L0_ffn_in['Su'], 'L0_ffn_Sd': _L0_ffn_in['Sd'], 'L1_attn_Wqkv': _L1_attn_in['Wqkv'], 'L1_attn_bqkv': _L1_attn_in['bqkv'], 'L1_attn_gamma_q': _L1_attn_in['gamma_q'], 'L1_attn_beta_q': _L1_attn_in['beta_q'], 'L1_attn_gamma_k': _L1_attn_in['gamma_k'], 'L1_attn_beta_k': _L1_attn_in['beta_k'], 'L1_attn_Wo': _L1_attn_in['Wo'], 'L1_attn_bo': _L1_attn_in['bo'], 'L1_ffn_wqkv': _L1_ffn_in['wqkv'], 'L1_ffn_q_scale': _L1_ffn_in['q_scale'], 'L1_ffn_k_scale': _L1_ffn_in['k_scale'], 'L1_ffn_wo': _L1_ffn_in['wo'], 'L1_ffn_ln_g': _L1_ffn_in['ln_g'], 'L1_ffn_ln_b': _L1_ffn_in['ln_b'], 'L1_ffn_w1': _L1_ffn_in['w1'], 'L1_ffn_b1': _L1_ffn_in['b1'], 'L1_ffn_w2': _L1_ffn_in['w2'], 'L1_ffn_b2': _L1_ffn_in['b2']}
    _x0 = _d['L0_attn_x']
    _d['L0_attn_x'] = jax.random.normal(jax.random.fold_in(jax.random.key(seed), 1), (2, 1024, 128), dtype=_x0.dtype)
    del _x0
    return _d

def reference(L0_attn_x, L0_attn_qkv_w, L0_attn_out_w, L0_attn_bias_p, L0_attn_bias_a, L0_attn_rope_freqs, L0_ffn_Wr, L0_ffn_Wg, L0_ffn_Wu, L0_ffn_Wd, L0_ffn_Sg, L0_ffn_Su, L0_ffn_Sd, L1_attn_Wqkv, L1_attn_bqkv, L1_attn_gamma_q, L1_attn_beta_q, L1_attn_gamma_k, L1_attn_beta_k, L1_attn_Wo, L1_attn_bo, L1_ffn_wqkv, L1_ffn_q_scale, L1_ffn_k_scale, L1_ffn_wo, L1_ffn_ln_g, L1_ffn_ln_b, L1_ffn_w1, L1_ffn_b1, L1_ffn_w2, L1_ffn_b2):

    def _L0_attn_ref(x, qkv_w, out_w, bias_p, bias_a, rope_freqs):
        import jax, jax.numpy as jnp
        import numpy as np
        B, S, D_MODEL, H, D = (2, 256, 128, 16, 64)
        SCALE = 1.0 / float(np.sqrt(D))

        def _rope(t, c, s):
            d2 = t.shape[-1] // 2
            t1, t2 = (t[..., :d2], t[..., d2:])
            return jnp.concatenate([t1 * c - t2 * s, t1 * s + t2 * c], axis=-1)
        Bb, Ss, _ = x.shape
        qkv = (x @ qkv_w.T).reshape(Bb, Ss, 3, H, D)
        q = qkv[:, :, 0].transpose(0, 2, 1, 3)
        k = qkv[:, :, 1].transpose(0, 2, 1, 3)
        v = qkv[:, :, 2].transpose(0, 2, 1, 3)
        pos = jnp.arange(Ss, dtype=jnp.float32)
        ang = pos[:, None] * rope_freqs[None, :]
        c = jnp.cos(ang)[None, None]
        s = jnp.sin(ang)[None, None]
        q = _rope(q, c, s)
        k = _rope(k, c, s)
        scores = jnp.einsum('bhqd,bhkd->bhqk', q, k) * SCALE
        p = jnp.maximum(bias_p, 0.01)
        a = jnp.maximum(bias_a, 0.01)
        dist = jnp.abs(pos[None, :] - pos[:, None])
        kb = -p * jnp.log1p(a * dist)
        attn = jax.nn.softmax(scores + kb[None], axis=-1)
        out = jnp.einsum('bhqk,bhkd->bhqd', attn, v)
        out = out.transpose(0, 2, 1, 3).reshape(Bb, Ss, H * D)
        return out @ out_w.T

    def _L0_ffn_ref(x, Wr, Wg, Wu, Wd, Sg, Su, Sd):
        import jax, jax.numpy as jnp
        import numpy as np
        B, S, D = (2, 256, 128)
        E, K, F = (16, 2, 64)
        FS = 128
        b, s, d = x.shape
        T = b * s
        xf = x.reshape(T, d)
        shared = jax.nn.silu(xf @ Sg) * (xf @ Su) @ Sd
        probs = jax.nn.softmax(xf @ Wr, axis=-1)
        topk_p, topk_i = jax.lax.top_k(probs, K)
        n_exp = Wr.shape[1]
        cw = jnp.zeros((T, n_exp), x.dtype).at[jnp.arange(T)[:, None], topk_i].add(topk_p)

        def step(acc, ew):
            wg, wu, wd, c = ew
            y = jax.nn.silu(xf @ wg) * (xf @ wu) @ wd
            return (acc + y * c[:, None], None)
        routed, _ = jax.lax.scan(step, jnp.zeros_like(xf), (Wg, Wu, Wd, cw.T))
        return (routed + shared).reshape(b, s, d)

    def _L1_attn_ref(x, Wqkv, bqkv, gamma_q, beta_q, gamma_k, beta_k, Wo, bo):
        import jax, jax.numpy as jnp
        import numpy as np
        H = 16

        def _kernel(x, gamma, beta):
            mean = x.mean(axis=-1, keepdims=True)
            std = jnp.std(x, axis=-1, ddof=1, keepdims=True)
            xn = (x - mean) / (std + 1e-06)
            return jnp.square(gamma * xn + beta)
        B, T, C = x.shape
        D = C // H
        qkv = x @ Wqkv + bqkv
        q, k, v = jnp.split(qkv, 3, axis=2)
        kerq = _kernel(q, gamma_q, beta_q)
        kerk = _kernel(k, gamma_k, beta_k)
        kerq = kerq.reshape(B, T, H, D).transpose(0, 2, 1, 3)
        kerk = kerk.reshape(B, T, H, D).transpose(0, 2, 1, 3)
        vh = v.reshape(B, T, H, D).transpose(0, 2, 1, 3)
        kv = jnp.cumsum(jnp.einsum('bhtf,bhtg->bhtfg', kerk, vh), axis=2)
        out = jnp.einsum('bhtf,bhtfg->bhtg', kerq, kv)
        Z = 1.0 / (jnp.einsum('bhtf,bhtf->bht', kerq, jnp.cumsum(kerk, axis=2)) + 1e-06)
        out = out * Z[..., None]
        out = out.transpose(0, 2, 1, 3).reshape(B, T, C)
        return out @ Wo + bo

    def _L1_ffn_ref(x, wqkv, q_scale, k_scale, wo, ln_g, ln_b, w1, b1, w2, b2):
        import jax, jax.numpy as jnp
        import numpy as np
        DIM = 128
        DEPTH = 2
        HEADS = 8
        DIM_HEAD = 64
        WINDOW = 64
        INNER = HEADS * DIM_HEAD
        HID = int(DIM * 4 * 2 / 3)
        B, N = (2, 1024)
        QK_SCALE = 8.0

        def shift_token(t):
            t1, t2 = jnp.split(t, 2, axis=-1)
            t2 = jnp.pad(t2, ((0, 0), (1, 0), (0, 0)))[:, :-1]
            return jnp.concatenate([t1, t2], axis=-1)

        def l2norm(t):
            return t / jnp.clip(jnp.linalg.norm(t, axis=-1, keepdims=True), 1e-12)

        def rotate_half(x):
            x1, x2 = jnp.split(x, 2, axis=-1)
            return jnp.concatenate([-x2, x1], axis=-1)

        def rotary_xpos(q, k):
            n = q.shape[-2]
            half_idx = jnp.arange(0, DIM_HEAD, 2, dtype=jnp.float32)
            inv_freq = 1.0 / 10000.0 ** (half_idx / DIM_HEAD)
            t = jnp.arange(n, dtype=jnp.float32)
            freqs = t[:, None] * inv_freq[None, :]
            freqs = jnp.concatenate([freqs, freqs], axis=-1)
            base = (half_idx + 0.4 * DIM_HEAD) / (1.4 * DIM_HEAD)
            power = (t - n // 2) / float(WINDOW // 2)
            scale = base[None, :] ** power[:, None]
            scale = jnp.concatenate([scale, scale], axis=-1)
            cos, sin = (jnp.cos(freqs), jnp.sin(freqs))
            q = q * cos * scale + rotate_half(q) * sin * scale
            k = k * cos / scale + rotate_half(k) * sin / scale
            return (q, k)

        def local_attention(q, k, v):
            b, h, n, d = q.shape
            w = n // WINDOW
            bq = q.reshape(b, h, w, WINDOW, d) * QK_SCALE
            bk = k.reshape(b, h, w, WINDOW, d)
            bv = v.reshape(b, h, w, WINDOW, d)

            def look_around(t):
                p = jnp.pad(t, ((0, 0), (0, 0), (1, 0), (0, 0), (0, 0)))
                return jnp.concatenate([p[:, :, :w], p[:, :, 1:]], axis=3)
            bk, bv = (look_around(bk), look_around(bv))
            bt = jnp.arange(n).reshape(w, WINDOW)
            btp = jnp.pad(bt, ((1, 0), (0, 0)), constant_values=-1)
            btk = jnp.concatenate([btp[:w], btp[1:]], axis=1)
            sim = jnp.einsum('bhwid,bhwjd->bhwij', bq, bk)
            i = bt[:, :, None]
            j = btk[:, None, :]
            mask = (i < j) | (i > j + WINDOW) | (j == -1)
            sim = jnp.where(mask, -jnp.finfo(sim.dtype).max, sim)
            attn = jax.nn.softmax(sim, axis=-1)
            out = jnp.einsum('bhwij,bhwjd->bhwid', attn, bv)
            return out.reshape(b, h, n, d)

        def _layer(x, wqkv, qs, ksc, wo, lg, lb, w1, b1, w2, b2):
            b, n, _ = x.shape
            h = shift_token(x)
            qkv = h @ wqkv
            q, k, v = jnp.split(qkv, 3, axis=-1)
            to_heads = lambda t: t.reshape(b, n, HEADS, DIM_HEAD).transpose(0, 2, 1, 3)
            q, k, v = (to_heads(q), to_heads(k), to_heads(v))
            q = l2norm(q) * qs
            k = l2norm(k) * ksc
            q, k = rotary_xpos(q, k)
            o = local_attention(q, k, v)
            o = o.transpose(0, 2, 1, 3).reshape(b, n, INNER)
            x = x + o @ wo
            h = shift_token(x)
            mu = h.mean(-1, keepdims=True)
            var = h.var(-1, keepdims=True)
            h = (h - mu) / jnp.sqrt(var + 1e-05) * lg + lb
            h = h @ w1 + b1
            a, g = jnp.split(h, 2, axis=-1)
            h = a * jax.nn.gelu(g, approximate=False)
            x = x + h @ w2 + b2
            return x
        for l in range(DEPTH):
            x = _layer(x, wqkv[l], q_scale[l], k_scale[l], wo[l], ln_g[l], ln_b[l], w1[l], b1[l], w2[l], b2[l])
        return x
    x = L0_attn_x
    x = x + 0.5 * _L0_ffn_ref(_layernorm(x, axis=-1), L0_ffn_Wr, L0_ffn_Wg, L0_ffn_Wu, L0_ffn_Wd, L0_ffn_Sg, L0_ffn_Su, L0_ffn_Sd)
    x = x + _L0_attn_ref(_layernorm(x, axis=-1), L0_attn_qkv_w, L0_attn_out_w, L0_attn_bias_p, L0_attn_bias_a, L0_attn_rope_freqs)
    x = x + 0.5 * _L0_ffn_ref(_layernorm(x, axis=-1), L0_ffn_Wr, L0_ffn_Wg, L0_ffn_Wu, L0_ffn_Wd, L0_ffn_Sg, L0_ffn_Su, L0_ffn_Sd)
    x = x + 0.5 * _L1_ffn_ref(_layernorm(x, axis=-1), L1_ffn_wqkv, L1_ffn_q_scale, L1_ffn_k_scale, L1_ffn_wo, L1_ffn_ln_g, L1_ffn_ln_b, L1_ffn_w1, L1_ffn_b1, L1_ffn_w2, L1_ffn_b2)
    x = x + _L1_attn_ref(_layernorm(x, axis=-1), L1_attn_Wqkv, L1_attn_bqkv, L1_attn_gamma_q, L1_attn_beta_q, L1_attn_gamma_k, L1_attn_beta_k, L1_attn_Wo, L1_attn_bo)
    x = x + 0.5 * _L1_ffn_ref(_layernorm(x, axis=-1), L1_ffn_wqkv, L1_ffn_q_scale, L1_ffn_k_scale, L1_ffn_wo, L1_ffn_ln_g, L1_ffn_ln_b, L1_ffn_w1, L1_ffn_b1, L1_ffn_w2, L1_ffn_b2)
    return x

_drawn_inputs = setup_inputs


def setup_inputs(seed=0):
    import zlib

    import numpy as np

    out = dict(_drawn_inputs(seed))
    spreads = {'L1_attn_bqkv': (0.0, 0.651),
     'L1_attn_bo': (0.0, 0.407),
     'L1_ffn_q_scale': (1.0, 0.6),
     'L1_ffn_k_scale': (1.0, 0.6),
     'L1_ffn_ln_g': (1.0, 0.6),
     'L1_ffn_ln_b': (0.0, 0.8),
     'L1_ffn_b1': (0.0, 0.8),
     'L1_ffn_b2': (0.0, 0.312)}
    factors = {'L0_attn_bias_p': 3.109,
     'L0_attn_bias_a': 3.793,
     'L0_attn_rope_freqs': 64.0,
     'L1_attn_Wqkv': 8.0,
     'L1_attn_gamma_q': 59.549,
     'L1_attn_beta_q': 61.93,
     'L1_attn_gamma_k': 39.062,
     'L1_attn_beta_k': 39.449,
     'L1_attn_Wo': 4.328,
     'L1_ffn_wqkv': 3.494,
     'L1_ffn_wo': 3.549,
     'L1_ffn_w1': 6.219,
     'L1_ffn_w2': 6.096}
    for name, (base, spread) in spreads.items():
        noise = np.random.default_rng([zlib.crc32(name.encode()), seed]).standard_normal(out[name].shape)
        drawn = base * np.exp(spread * noise) if base else spread * noise
        out[name] = jnp.asarray(drawn.astype(out[name].dtype))
    for name, factor in factors.items():
        out[name] = (out[name] * factor).astype(out[name].dtype)
    return out
```

```python
B, S, D = 2, 1024, 128
P = 128
NT = B * S // P
TB = S // P
EPS = 1e-5

E, F, FS = 16, 64, 128
HC = (E * F + FS) // P
EC = E * F // P
BT = 4
NB = NT // BT

H0, D0 = 16, 64
PAIRS = H0 // 2
BIASW = 2 * S - P

DEPTH, H1, D1, WIN = 2, 8, 64, 64
INNER = H1 * D1
KEYS = WIN + P
HID = int(D * 4 * 2 / 3)
HIDC = [(c, min(P, HID - c)) for c in range(0, HID, P)]
MASKED = -1e30

H2 = 16
D2 = D // H2
VA = D2 + 1


def build(nc, a, out):
    import numpy as np
    import concourse.bass as bass
    from concourse import mybir
    from contextlib import ExitStack

    f32, bf16 = mybir.dt.float32, mybir.dt.bfloat16
    ALU, ACT, AX = mybir.AluOpType, mybir.ActivationFunctionType, mybir.AxisListType.X
    names = [0]

    class Space:
        def __init__(self, ctx):
            self.ctx = ctx
            names[0] += 1
            self.n = names[0]
            self.sems = []
            ctx.callback(self.clear)

        def clear(self):
            if self.sems and self.n > 1:
                with nc.Block() as block:
                    @block.sync
                    def _(sp):
                        for sem in self.sems:
                            sp.sem_clear(sem)

        def sb(self, name, shape, dt=f32):
            return self.ctx.enter_context(nc.sbuf_tensor(f"{name}_{self.n}", shape, dt))

        def ps(self, name, shape, dt=f32):
            return self.ctx.enter_context(nc.psum_tensor(f"{name}_{self.n}", shape, dt))

        def sem(self, name):
            handle = self.ctx.enter_context(nc.semaphore(f"{name}_{self.n}"))
            self.sems.append(handle)
            return handle

    class Chain:
        def __init__(self, eng, sem, per):
            self.eng, self.sem, self.per, self.k, self.base = eng, sem, per, 0, 0

        def turn(self, i):
            self.base, self.k = i * self.per, 0

        def link(self, ins):
            ins.then_inc(self.sem, 1)
            self.k += 1
            self.eng.wait_ge(self.sem, self.base + self.k)

    def layernorm_stats(sp, src, dst_mean, dst_rstd):
        stats, mv, tmp = sp.sb("stats", [P, NT, 6]), sp.sb("mv", [P, NT, 2]), sp.sb("tmp", [P, NT])
        c, s = sp.sem("ln_chain"), sp.sem("ln_std")
        with nc.Block() as block:
            @block.vector
            def _(dve):
                for t in range(NT):
                    last = nc.vector.bn_stats(stats[:, t, :], src[:, t, :])
                last.then_inc(c, 1)
                dve.wait_ge(c, 1)
                for t in range(NT):
                    last = nc.vector.bn_aggr(mv[:, t, :], stats[:, t, :])
                last.then_inc(c, 1)
                dve.wait_ge(c, 2)
                nc.vector.tensor_copy(dst_mean[:, :], mv[:, :, 0])
                nc.vector.tensor_scalar_add(tmp[:, :], mv[:, :, 1], EPS).then_inc(c, 1)
                dve.wait_ge(s, 1)
                nc.vector.reciprocal(dst_rstd[:, :], tmp[:, :]).then_inc(c, 1)
                dve.wait_ge(c, 4)

            @block.scalar
            def _(act):
                act.wait_ge(c, 3)
                nc.scalar.activation(tmp[:, :], tmp[:, :], ACT.Sqrt).then_inc(s, 1)
                act.wait_ge(s, 1)

    def bc(ap, shape):
        return ap.broadcast_to(shape)

    ctx = ExitStack()
    with ctx:
        g = Space(ctx)
        x = g.sb("x", [P, NT, D])
        mean, rstd = g.sb("mean", [P, NT]), g.sb("rstd", [P, NT])
        ident, identb = g.sb("ident", [P, P]), g.sb("identb", [P, P], bf16)
        ones = g.sb("ones", [1, P])
        gatebuf = g.sb("gatebuf", [P, 4])
        xd = a["L0_attn_x"].rearrange("b (t p) d -> p (b t) d", p=P)
        s_load, s_const = g.sem("load"), g.sem("const")
        with nc.Block() as block:
            @block.sync
            def _(sp):
                sp.dma_start(x[:, :, :], xd).then_inc(s_load, 16)
                sp.dma_start(ident[:, :], a["c_ident"]).then_inc(s_load, 16)
                sp.wait_ge(s_load, 32)

            @block.vector
            def _(dve):
                nc.vector.memset(ones[:, :], 1.0).then_inc(s_const, 1)
                nc.vector.memset(gatebuf[:, :], 0.0).then_inc(s_const, 1)
                dve.wait_ge(s_load, 32)
                nc.vector.tensor_copy(identb[:, :], ident[:, :]).then_inc(s_const, 1)
                dve.wait_ge(s_const, 3)

        def moe():
            with ExitStack() as c:
                s = Space(c)
                wg, wu = s.sb("wg", [P, HC * P]), s.sb("wu", [P, HC * P])
                wd, wr = s.sb("wd", [P, HC, D]), s.sb("wr", [P, E])
                self32, sel = s.sb("self32", [P, EC, P]), s.sb("sel", [P, EC, P], bf16)
                rank = s.sb("rank", [P, E])
                hn, hT = s.sb("hn", [P, BT, D]), s.sb("hT", [P, BT * P])
                xc = s.sb("xc", [P, BT, D])
                sg, hid, act_ = s.sb("sg", [P, 2, BT * P]), s.sb("hid", [P, 2, BT * P]), s.sb("act", [P, HC, BT * P])
                G = [P, BT, E]
                d, e, p, p2, t1, t2, s1, cw, rest = (s.sb(n, G) for n in
                    ("d", "e", "p", "p2", "t1", "t2", "s1", "cw", "rest"))
                m4, r4 = s.sb("m4", [P, BT]), s.sb("r4", [P, BT])
                cw3, cwT = s.sb("cw3", [P, BT, P // E, E], bf16), s.sb("cwT", [P, BT * P], bf16)
                pA = s.ps("pA", [P, BT * P])
                pAb = s.ps("pAb", [P, BT * P], bf16)
                pY = pA
                pg, pu, pc = (s.ps(n, [P, 2, BT * P]) for n in ("pg", "pu", "pc"))
                s_hid = s.sem("half_hidden")
                w_in = s.sem("weights"); sel_ok = s.sem("sel_ok")
                hn_ready, hT_psum, hT_ready = s.sem("hn_ready"), s.sem("hT_psum"), s.sem("hT_ready")
                logits, e_in, e_ready, cw_ready, cT_psum, cwT_ready = (s.sem(n) for n in
                    ("logits", "e_in", "e_ready", "cw_ready", "cT_psum", "cwT_ready"))
                gate_psum, up_psum, silu_ready, hid_ready = (s.sem(n) for n in ("gate_psum", "up_psum", "silu_ready", "hid_ready"))
                y_psum, x_new, chain = s.sem("y_psum"), s.sem("x_new"), s.sem("chain")
                layernorm_stats(s, x, mean, rstd)
                L = pA[:, 0:BT * E].rearrange("p (t e) -> p t e", e=E)

                with nc.Block() as block:
                    @block.sync
                    def _(sp):
                        sp.dma_start(wg[:, 0:E * F].rearrange("p (e f) -> p e f", e=E), a["L0_ffn_Wg"].rearrange("e d f -> d e f")).then_inc(w_in, 16)
                        sp.dma_start(wu[:, 0:E * F].rearrange("p (e f) -> p e f", e=E), a["L0_ffn_Wu"].rearrange("e d f -> d e f")).then_inc(w_in, 16)
                        sp.dma_start(wg[:, E * F:], a["L0_ffn_Sg"]).then_inc(w_in, 16)
                        sp.dma_start(wu[:, E * F:], a["L0_ffn_Su"]).then_inc(w_in, 16)
                        sp.dma_start(wd[:, 0:EC, :], a["L0_ffn_Wd"].rearrange("(c two) f d -> (two f) c d", two=2)).then_inc(w_in, 16)
                        sp.dma_start(wd[:, EC, :], a["L0_ffn_Sd"]).then_inc(w_in, 16)
                        sp.dma_start(wr[:, :], a["L0_ffn_Wr"]).then_inc(w_in, 16)
                        sp.dma_start(self32[:, :, :], a["c_sel"]).then_inc(w_in, 16)
                        sp.dma_start(rank[:, :], a["c_rank"]).then_inc(w_in, 16)
                        sp.wait_ge(w_in, 144)

                    @block.tensor
                    def _(pe):
                        def front(i):
                            pe.wait_ge(hn_ready, i + 1)
                            for j in range(BT):
                                last = nc.tensor.transpose(pA[:, j * P:(j + 1) * P], hn[:, j, :], ident[:, :])
                            last.then_inc(hT_psum, 1)
                            pe.wait_ge(hT_ready, i + 1)
                            for j in range(BT):
                                last = nc.tensor.matmul(L[:, j, :], hT[:, j * P:(j + 1) * P], wr[:, :], start=True, stop=True)
                            last.then_inc(logits, 1)

                        def weights(i):
                            pe.wait_ge(cw_ready, i + 1)
                            for j in range(BT):
                                last = nc.tensor.transpose(pAb[:, j * P:(j + 1) * P],
                                                           cw3[:, j, :, :].rearrange("p a b -> p (a b)"), identb[:, :])
                            last.then_inc(cT_psum, 1)

                        def up(i):
                            pe.wait_ge(cwT_ready, i + 1)
                            for c in range(HC):
                                if c >= 2:
                                    pe.wait_ge(silu_ready, i * HC + c - 1)
                                nc.tensor.matmul(pg[:, c % 2, :], wg[:, c * P:(c + 1) * P], hT[:, :], start=True, stop=True).then_inc(gate_psum, 1)
                                if c >= 2:
                                    pe.wait_ge(hid_ready, i * HC + c - 1)
                                last = nc.tensor.matmul(pu[:, c % 2, :], wu[:, c * P:(c + 1) * P], hT[:, :], start=True, stop=True)
                                if c < EC:
                                    last = nc.tensor.matmul(pc[:, c % 2, :], sel[:, c, :], cwT[:, :], start=True, stop=True)
                                last.then_inc(up_psum, 1)

                        def down(i):
                            pe.wait_ge(hid_ready, i * HC + HC)
                            for j in range(BT):
                                for c in range(HC):
                                    last = nc.tensor.matmul(pY[:, j * D:(j + 1) * D], act_[:, c, j * P:(j + 1) * P], wd[:, c, :],
                                                            start=(c == 0), stop=(c == HC - 1))
                            last.then_inc(y_psum, 1)

                        pe.wait_ge(w_in, 144)
                        pe.wait_ge(sel_ok, 2)
                        with pe.Fori(0, NB) as i:
                            front(i)
                            weights(i)
                            up(i)
                            down(i)

                    @block.scalar
                    def _(act):
                        with act.Fori(0, NB) as i:
                            act.wait_ge(hT_psum, i + 1)
                            nc.scalar.copy(hT[:, :], pA[:, :]).then_inc(hT_ready, 1)
                            act.wait_ge(e_in, i + 1)
                            nc.scalar.activation(e[:, :, :], d[:, :, :], ACT.Exp).then_inc(e_ready, 1)
                            for c in range(HC):
                                act.wait_ge(gate_psum, i * HC + c + 1)
                                if c >= 2:
                                    act.wait_ge(hid_ready, i * HC + c - 1)
                                nc.scalar.activation(sg[:, c % 2, :], pg[:, c % 2, :], ACT.Silu).then_inc(silu_ready, 1)

                    @block.vector
                    def _(dve):
                        dve.wait_ge(w_in, 144)
                        nc.vector.tensor_copy(sel[:, :, :], self32[:, :, :]).then_inc(sel_ok, 1)
                        nc.vector.memset(cw3[:, :, :, :], 0.0).then_inc(sel_ok, 1)
                        dve.wait_ge(sel_ok, 2)
                        ch = Chain(dve, chain, 22)
                        rk = bc(rank[:, None, :], G)
                        with dve.Fori(0, NB) as i:
                            ch.turn(i)
                            ch.link(nc.vector.tensor_tensor(xc[:, :, :], x[:, bass.ds(i * BT, BT), :], bc(mean[:, bass.ds(i * BT, BT), None], [P, BT, D]), ALU.subtract))
                            nc.vector.tensor_tensor(hn[:, :, :], xc[:, :, :], bc(rstd[:, bass.ds(i * BT, BT), None], [P, BT, D]), ALU.mult).then_inc(hn_ready, 1)
                            dve.wait_ge(logits, i + 1)
                            ch.link(nc.vector.tensor_reduce(m4[:, :], L, AX, ALU.max))
                            nc.vector.tensor_tensor(d[:, :, :], L, bc(m4[:, :, None], G), ALU.subtract).then_inc(e_in, 1)
                            dve.wait_ge(e_ready, i + 1)
                            ch.link(nc.vector.reduce_sum(r4[:, :], e[:, :, :], AX))
                            ch.link(nc.vector.reciprocal(m4[:, :], r4[:, :]))
                            ch.link(nc.vector.tensor_tensor(p[:, :, :], e[:, :, :], bc(m4[:, :, None], G), ALU.mult))

                            def pick(src, dst):
                                ch.link(nc.vector.tensor_reduce(m4[:, :], src[:, :, :], AX, ALU.max))
                                ch.link(nc.vector.tensor_tensor(t1[:, :, :], src[:, :, :], bc(m4[:, :, None], G), ALU.is_ge))
                                ch.link(nc.vector.tensor_tensor(t2[:, :, :], t1[:, :, :], rk, ALU.mult))
                                ch.link(nc.vector.tensor_reduce(r4[:, :], t2[:, :, :], AX, ALU.max))
                                ch.link(nc.vector.tensor_tensor(dst[:, :, :], t2[:, :, :], bc(r4[:, :, None], G), ALU.is_equal))
                            pick(p, s1)
                            ch.link(nc.vector.scalar_tensor_tensor(p2[:, :, :], s1[:, :, :], -2.0, p[:, :, :], ALU.mult, ALU.add))
                            pick(p2, d)
                            ch.link(nc.vector.tensor_tensor(t1[:, :, :], s1[:, :, :], d[:, :, :], ALU.add))
                            ch.link(nc.vector.tensor_tensor(cw[:, :, :], t1[:, :, :], p[:, :, :], ALU.mult))
                            ch.link(nc.vector.tensor_copy(cw3[:, :, 0, :], cw[:, :, :]))
                            ch.link(nc.vector.tensor_tensor(rest[:, :, :], cw[:, :, :], cw3[:, :, 0, :], ALU.subtract))
                            ch.link(nc.vector.tensor_copy(cw3[:, :, 1, :], rest[:, :, :]))
                            ch.link(nc.vector.tensor_tensor(t1[:, :, :], rest[:, :, :], cw3[:, :, 1, :], ALU.subtract))
                            nc.vector.tensor_copy(cw3[:, :, 2, :], t1[:, :, :]).then_inc(cw_ready, 1)
                            dve.wait_ge(cT_psum, i + 1)
                            nc.vector.tensor_copy(cwT[:, :], pAb[:, :]).then_inc(cwT_ready, 1)
                            for c in range(HC):
                                dve.wait_ge(up_psum, i * HC + c + 1)
                                dve.wait_ge(silu_ready, i * HC + c + 1)
                                if c < EC:
                                    nc.vector.tensor_tensor(hid[:, c % 2, :], sg[:, c % 2, :], pu[:, c % 2, :], ALU.mult).then_inc(s_hid, 1)
                                    dve.wait_ge(s_hid, i * EC + c + 1)
                                    nc.vector.tensor_tensor(act_[:, c, :], hid[:, c % 2, :], pc[:, c % 2, :], ALU.mult).then_inc(hid_ready, 1)
                                else:
                                    nc.vector.tensor_tensor(act_[:, c, :], sg[:, c % 2, :], pu[:, c % 2, :], ALU.mult).then_inc(hid_ready, 1)
                            dve.wait_ge(y_psum, i + 1)
                            xi = x[:, bass.ds(i * BT, BT), :]
                            nc.vector.scalar_tensor_tensor(xi, pY.rearrange("p (t d) -> p t d", d=D), 0.5, xi, ALU.mult, ALU.add).then_inc(x_new, 1)
                        assert ch.k == ch.per, ch.k
                        dve.wait_ge(x_new, NB)

        def layer(l, zin, zmid, zout):
            with ExitStack() as c:
                s = Space(c)
                NC = len(HIDC)
                wqkv, wo = s.sb("wqkv", [P, 3 * INNER]), s.sb("wo", [P, INNER // P, D])
                w1, w2 = s.sb("w1", [P, 2 * HID]), s.sb("w2", [P, NC, D])
                b1a, b1g, b2 = s.sb("b1a", [P, NC]), s.sb("b1g", [P, NC]), s.sb("b2", [1, D])
                lg, lb = s.sb("lg", [P, 1]), s.sb("lb", [P, 1])
                qk, qks = s.sb("qk", [P, 2, D1]), s.sb("qks", [P, 2, D1])
                cosT, sinT = s.sb("cosT", [P, TB, 2, D1]), s.sb("sinT", [P, TB, 2, D1])
                maskf, mask = s.sb("maskf", [P, TB, KEYS]), s.sb("mask", [P, TB, KEYS], bf16)
                two = range(B)
                both = lambda name, shape: [s.sb(f"{name}{b}", shape) for b in two]
                hs1, hT, sq, ra, rb = both("hs1", [P, D]), both("hT", [P, P]), both("sq", [P, 2 * INNER]), both("ra", [P, 2 * INNER]), both("rb", [P, 2 * INNER])
                ss, rn = both("ss", [P, 2 * H1]), both("rn", [P, 2 * H1])
                qT, kT = both("qT", [P, H1 // 2, P]), both("kT", [P, H1 // 2, KEYS])
                V = both("V", [P, TB + 1, H1, D1 + 1])
                mx, diff, pr = both("mx", [P, H1]), both("diff", [P, H1, KEYS]), both("pr", [P, H1, 2 * P])
                pT = both("pT", [P, 2 * H1, P])
                rs, on, oT = both("rs", [P, H1]), both("on", [P, INNER]), both("oT", [P, INNER // P, P])
                hs2, st, mv, rv, hn = both("hs2", [P, D]), both("st", [P, 6]), both("mv", [P, 2]), both("rv", [P, 1]), both("hn", [P, D])
                h2T, gg, uT = s.sb("h2T", [P, B * P]), s.sb("gg", [P, NC, B * P]), s.sb("uT", [P, NC, B * P])
                R = [s.ps(f"R{b}", [P, 4, 512]) for b in two]
                Sv = [R[b][:, :, :].rearrange("p k (s n) -> p (k s) n", s=2)[:, :, 0:KEYS] for b in two]
                slot = lambda h: 2 * (2 * (h // 4) + h % 2) + (h // 2) % 2
                w_in, setup = s.sem("weights"), s.sem("setup")
                hs1_in, hs2_in = [s.sem(f"hs1_in{b}") for b in two], [s.sem(f"hs2_in{b}") for b in two]
                (h1T_psum, hT_ready, qkv_psum, sq_ready, v_ready, ss_ready, norm_ready, rn_ready, ab_ready, rot_sum, rot_ready,
                 qkT_psum, qT_ready, kT_ready, s_psum, d_ready, exp_ready, pT_psum, pTa_ready, pTb_ready, o_psum, on_ready,
                 oT_psum, oT_ready, y_psum, zmid_ready, var_ready, std_ready, hn_ready, h2T_psum, h2T_ready, up_psum,
                 gelu_ready, u_ready, y2_psum, zout_ready, chain) = (s.sem(n) for n in (
                 "h1T_psum hT_ready qkv_psum sq_ready v_ready ss_ready norm_ready rn_ready ab_ready rot_sum rot_ready "
                 "qkT_psum qT_ready kT_ready s_psum d_ready exp_ready pT_psum pTa_ready pTb_ready o_psum on_ready "
                 "oT_psum oT_ready y_psum zmid_ready var_ready std_ready hn_ready h2T_psum h2T_ready up_psum "
                 "gelu_ready u_ready y2_psum zout_ready chain").split())
                at = lambda t, b: t * B + b + 1

                with nc.Block() as block:
                    @block.sync
                    def _(sp):
                        bcast = lambda ap, n: ap.broadcast_to([P, n])
                        qs, ks = a["L1_ffn_q_scale"], a["L1_ffn_k_scale"]
                        hf = D1 // 2
                        loads = [(wqkv[:, :], a["L1_ffn_wqkv"][l]), (wo[:, :, :], a["L1_ffn_wo"][l].rearrange("(c p) d -> p c d", p=P)),
                                 (w1[:, :], a["L1_ffn_w1"][l]), (b2[:, :], a["L1_ffn_b2"][l:l + 1, :]),
                                 (lg[:, :], a["L1_ffn_ln_g"][l].rearrange("(p o) -> p o", o=1)), (lb[:, :], a["L1_ffn_ln_b"][l].rearrange("(p o) -> p o", o=1)),
                                 (qk[:, 0, :], bcast(qs[l:l + 1, :], D1)), (qk[:, 1, :], bcast(ks[l:l + 1, :], D1)),
                                 (qks[:, 0, 0:hf], bcast(qs[l:l + 1, hf:], hf)), (qks[:, 0, hf:], bcast(qs[l:l + 1, 0:hf], hf)),
                                 (qks[:, 1, 0:hf], bcast(ks[l:l + 1, hf:], hf)), (qks[:, 1, hf:], bcast(ks[l:l + 1, 0:hf], hf)),
                                 (cosT[:, :, :, :], a["c_cos"]), (sinT[:, :, :, :], a["c_sin"]), (maskf[:, :, :], a["c_mask"])]
                        for k, (r, n) in enumerate(HIDC):
                            loads += [(w2[0:n, k, :], a["L1_ffn_w2"][l, r:r + n, :]),
                                      (b1a[0:n, k:k + 1], a["L1_ffn_b1"][l, r:r + n].rearrange("(p o) -> p o", o=1)),
                                      (b1g[0:n, k:k + 1], a["L1_ffn_b1"][l, HID + r:HID + r + n].rearrange("(p o) -> p o", o=1))]
                        for dst, src in loads:
                            sp.dma_start(dst, src).then_inc(w_in, 16)
                        sp.wait_ge(w_in, 16 * len(loads))

                    @block.gpsimd
                    def _(pool):
                        for b in two:
                            nc.gpsimd.memset(V[b][:, :, :, :], 1.0).then_inc(setup, 1)
                            nc.gpsimd.memset(pr[b][:, :, :], 0.0).then_inc(setup, 1)
                        pool.wait_ge(setup, 4)

                    @block.vector
                    def _(dve):
                        for b in two:
                            nc.vector.memset(kT[b][:, :, :], 0.0).then_inc(chain, 1)
                            nc.vector.memset(zmid[:, b, 0, :], 0.0).then_inc(chain, 1)
                        dve.wait_ge(w_in, 16 * (15 + 3 * NC))
                        nc.vector.tensor_tensor(cosT[:, :, :, :], cosT[:, :, :, :], bc(qk[:, None, :, :], [P, TB, 2, D1]), ALU.mult).then_inc(chain, 1)
                        nc.vector.tensor_tensor(sinT[:, :, :, :], sinT[:, :, :, :], bc(qks[:, None, :, :], [P, TB, 2, D1]), ALU.mult).then_inc(chain, 1)
                        nc.vector.tensor_copy(mask[:, :, :], maskf[:, :, :]).then_inc(chain, 1)
                        dve.sem_inc(zout_ready, B)
                        dve.wait_ge(chain, 2 * B + 3)

                chain = s.sem("steps")
                with nc.Block() as block:
                    def shifted(sp, dst, src, b, t, sem):
                        sp.dma_start(dst[:, 0:D // 2], src[:, b, t + 1, 0:D // 2]).then_inc(sem, 16)
                        sp.dma_start(dst[1:P, D // 2:], src[0:P - 1, b, t + 1, D // 2:]).then_inc(sem, 16)
                        sp.dma_start(dst[0:1, D // 2:], src[P - 1:P, b, t, D // 2:]).then_inc(sem, 16)

                    @block.sync
                    def _(sp):
                        def second(t):
                            for b in two:
                                sp.wait_ge(zmid_ready, at(t, b))
                                shifted(sp, hs2[b], zmid, b, t, hs2_in[b])
                        for b in two:
                            shifted(sp, hs1[b], zin, b, 0, hs1_in[b])
                        with sp.Fori(0, TB - 1) as t:
                            for b in two:
                                sp.wait_ge(h1T_psum, at(t, b))
                                shifted(sp, hs1[b], zin, b, t + 1, hs1_in[b])
                            second(t)
                        second(TB - 1)

                    @block.tensor
                    def _(pe):
                        with pe.Fori(0, TB) as t:
                            for b in two:
                                pe.wait_ge(hs1_in[b], 48 * t + 48)
                                nc.tensor.transpose(R[b][:, 3, 0:P], hs1[b][:, :], ident[:, :]).then_inc(h1T_psum, 1)
                            for b in two:
                                pe.wait_ge(zout_ready, at(t, b))
                                pe.wait_ge(hT_ready, at(t, b))
                                for k in range(3):
                                    last = nc.tensor.matmul(R[b][:, k, :], hT[b][:, :], wqkv[:, k * INNER:(k + 1) * INNER], start=True, stop=True)
                                last.then_inc(qkv_psum, 1)
                            for b in two:
                                pe.wait_ge(rot_ready, at(t, b))
                                for k in range(H1):
                                    bank = 3 if k < H1 // 2 else 0
                                    last = nc.tensor.transpose(R[b][:, bank, (k % 4) * P:(k % 4 + 1) * P], ra[b][:, k * P:(k + 1) * P], ident[:, :])
                                last.then_inc(qkT_psum, 1)
                            for b in two:
                                pe.wait_ge(v_ready, at(t, b))
                                pe.wait_ge(qT_ready, at(t, b))
                                pe.wait_ge(kT_ready, at(t, b))
                                for k in range(4):
                                    nc.tensor.matmul(Sv[b][:, 2 * k:2 * k + 2, :], identb[:, :], bc(mask[:, bass.ds(t, 1), :], [P, 2, KEYS]), start=True, stop=False)
                                for h in range(H1):
                                    r = (h % 2) * D1
                                    last = nc.tensor.matmul(Sv[b][:, slot(h), :], qT[b][r:r + D1, h // 2, :], kT[b][r:r + D1, h // 2, :],
                                                            start=False, stop=(slot(h) % 2 == 1))
                                last.then_inc(s_psum, 1)
                            for b in two:
                                pe.wait_ge(exp_ready, at(t, b))
                                for k in range(2 * H1):
                                    last = nc.tensor.transpose(R[b][:, k // 4, (k % 4) * P:(k % 4 + 1) * P], pr[b][:, k // 2, (k % 2) * P:(k % 2 + 1) * P], ident[:, :])
                                last.then_inc(pT_psum, 1)
                            for b in two:
                                pe.wait_ge(pTa_ready, at(t, b))
                                pe.wait_ge(pTb_ready, at(t, b))
                                for h in range(H1):
                                    O = R[b][:, h // 4, (h % 4) * (D1 + 1):(h % 4 + 1) * (D1 + 1)]
                                    nc.tensor.matmul(O, pT[b][:, 2 * slot(h), :], V[b][:, t, h, :], start=True, stop=False)
                                    last = nc.tensor.matmul(O, pT[b][:, 2 * slot(h) + 1, :], V[b][:, t + 1, h, :], start=False, stop=True)
                                last.then_inc(o_psum, 1)
                            for b in two:
                                pe.wait_ge(on_ready, at(t, b))
                                for k in range(INNER // P):
                                    last = nc.tensor.transpose(R[b][:, 2, k * P:(k + 1) * P], on[b][:, k * P:(k + 1) * P], ident[:, :])
                                last.then_inc(oT_psum, 1)
                            for b in two:
                                pe.wait_ge(oT_ready, at(t, b))
                                for k in range(INNER // P):
                                    last = nc.tensor.matmul(R[b][:, 3, 0:D], oT[b][:, k, :], wo[:, k, :], start=(k == 0), stop=(k == INNER // P - 1))
                                last.then_inc(y_psum, 1)
                            for b in two:
                                pe.wait_ge(hn_ready, at(t, b))
                                nc.tensor.transpose(R[b][:, 0, 0:P], hn[b][:, :], ident[:, :]).then_inc(h2T_psum, 1)
                            pe.wait_ge(h2T_ready, B * t + B)
                            for k, (r, n) in enumerate(HIDC):
                                for half in two:
                                    last = nc.tensor.matmul(R[half][0:n, 1 + k // 2, (k % 2) * 256:(k % 2) * 256 + B * P],
                                                            w1[:, half * HID + r:half * HID + r + n], h2T[:, :], start=True, stop=True)
                            last.then_inc(up_psum, 1)
                            pe.wait_ge(u_ready, t + 1)
                            for b in two:
                                for k, (r, n) in enumerate(HIDC):
                                    nc.tensor.matmul(R[b][:, 2, 0:D], uT[0:n, k, b * P:(b + 1) * P], w2[0:n, k, :], start=(k == 0), stop=False)
                                nc.tensor.matmul(R[b][:, 2, 0:D], ones[:, :], b2[:, :], start=False, stop=True).then_inc(y2_psum, 1)

                    @block.scalar
                    def _(act):
                        with act.Fori(0, TB) as t:
                            for b in two:
                                act.wait_ge(h1T_psum, at(t, b))
                                nc.scalar.copy(hT[b][:, :], R[b][:, 3, 0:P]).then_inc(hT_ready, 1)
                            for b in two:
                                act.wait_ge(qkv_psum, at(t, b))
                                nc.scalar.activation(sq[b][:, :], R[b][:, 0:2, :].rearrange("p k n -> p (k n)"), ACT.Square).then_inc(sq_ready, 1)
                                nc.scalar.copy(V[b][:, t + 1, :, 0:D1], R[b][:, 2, :].rearrange("p (h d) -> p h d", h=H1)).then_inc(v_ready, 1)
                            for b in two:
                                act.wait_ge(ss_ready, at(t, b))
                                nc.scalar.activation(ss[b][:, :], ss[b][:, :], ACT.Sqrt).then_inc(norm_ready, 1)
                            for b in two:
                                act.wait_ge(qkT_psum, at(t, b))
                                nc.scalar.copy(qT[b][:, :, :], R[b][:, 3, :].rearrange("p (k n) -> p k n", n=P)).then_inc(qT_ready, 1)
                            for b in two:
                                act.wait_ge(d_ready, at(t, b))
                                nc.scalar.activation(pr[b][:, :, P - WIN:], diff[b][:, :, :], ACT.Exp).then_inc(exp_ready, 1)
                            for b in two:
                                act.wait_ge(pT_psum, at(t, b))
                                nc.scalar.copy(pT[b][:, 0:H1, :], R[b][:, 0:2, :].rearrange("p k (m n) -> p (k m) n", n=P)).then_inc(pTa_ready, 1)
                            for b in two:
                                act.wait_ge(oT_psum, at(t, b))
                                nc.scalar.copy(oT[b][:, :, :], R[b][:, 2, :].rearrange("p (k n) -> p k n", n=P)).then_inc(oT_ready, 1)
                            for b in two:
                                act.wait_ge(var_ready, at(t, b))
                                nc.scalar.activation(rv[b][:, :], rv[b][:, :], ACT.Sqrt).then_inc(std_ready, 1)
                            for b in two:
                                act.wait_ge(h2T_psum, at(t, b))
                                nc.scalar.activation(h2T[:, b * P:(b + 1) * P], R[b][:, 0, 0:P], ACT.Identity, bias=lb[:, 0:1], scale=lg[:, 0:1]).then_inc(h2T_ready, 1)
                            act.wait_ge(up_psum, t + 1)
                            for k, (r, n) in enumerate(HIDC):
                                nc.scalar.activation(gg[0:n, k, :], R[1][0:n, 1 + k // 2, (k % 2) * 256:(k % 2) * 256 + B * P], ACT.Gelu,
                                                     bias=b1g[0:n, k:k + 1]).then_inc(gelu_ready, 1)

                    @block.gpsimd
                    def _(pool):
                        with pool.Fori(0, TB) as t:
                            for b in two:
                                pool.wait_ge(ab_ready, at(t, b))
                                nc.gpsimd.tensor_tensor(sq[b][:, :], ra[b][:, :], rb[b][:, :], ALU.add).then_inc(rot_sum, 1)
                                pool.wait_ge(rn_ready, at(t, b))
                                pool.wait_ge(rot_sum, at(t, b))
                                nc.gpsimd.tensor_tensor(ra[b][:, :].rearrange("p (h d) -> p h d", d=D1), sq[b][:, :].rearrange("p (h d) -> p h d", d=D1),
                                                        bc(rn[b][:, :, None], [P, 2 * H1, D1]), ALU.mult).then_inc(rot_ready, 1)

                    @block.vector
                    def _(dve):
                        ch = Chain(dve, chain, 14)
                        gate = lambda: nc.vector.memset(gatebuf[:, :], 0.0)
                        hf = D1 // 2
                        with dve.Fori(0, TB) as t:
                            ch.turn(t)
                            for b in two:
                                dve.wait_ge(sq_ready, at(t, b))
                                nc.vector.reduce_sum(ss[b][:, :], sq[b][:, :].rearrange("p (h d) -> p h d", d=D1), AX).then_inc(ss_ready, 1)
                                for j in range(2):
                                    src = R[b][:, j, :].rearrange("p (h d) -> p h d", d=D1)
                                    d3 = lambda buf: buf[b][:, j * INNER:(j + 1) * INNER].rearrange("p (h d) -> p h d", d=D1)
                                    nc.vector.tensor_tensor(d3(ra), src, bc(cosT[:, bass.ds(t, 1), j, :], [P, H1, D1]), ALU.mult)
                                    for k in range(2):
                                        last = nc.vector.tensor_tensor(d3(rb)[:, :, k * hf:(k + 1) * hf], src[:, :, (1 - k) * hf:(2 - k) * hf],
                                                                       bc(sinT[:, bass.ds(t, 1), j, k * hf:(k + 1) * hf], [P, H1, hf]), ALU.mult)
                                last.then_inc(ab_ready, 1)
                            for b in two:
                                dve.wait_ge(norm_ready, at(t, b))
                                ch.link(nc.vector.tensor_scalar_max(ss[b][:, :], ss[b][:, :], 1e-12))
                                nc.vector.reciprocal(rn[b][:, :], ss[b][:, :]).then_inc(rn_ready, 1)
                            for b in two:
                                dve.wait_ge(qkT_psum, at(t, b))
                                ch.link(nc.vector.tensor_copy(kT[b][:, :, 0:WIN], kT[b][:, :, P:KEYS]))
                                nc.vector.tensor_copy(kT[b][:, :, WIN:KEYS], R[b][:, 0, :].rearrange("p (k n) -> p k n", n=P)).then_inc(kT_ready, 1)
                            for b in two:
                                dve.wait_ge(s_psum, at(t, b))
                                ch.link(nc.vector.tensor_reduce(mx[b][:, :], Sv[b], AX, ALU.max))
                                nc.vector.tensor_tensor(diff[b][:, :, :], Sv[b], bc(mx[b][:, :, None], [P, H1, KEYS]), ALU.subtract).then_inc(d_ready, 1)
                            for b in two:
                                dve.wait_ge(pT_psum, at(t, b))
                                nc.vector.tensor_copy(pT[b][:, H1:, :], R[b][:, 2:4, :].rearrange("p k (m n) -> p (k m) n", n=P)).then_inc(pTb_ready, 1)
                            for b in two:
                                dve.wait_ge(o_psum, at(t, b))
                                O = R[b][:, 0:2, 0:4 * (D1 + 1)].rearrange("p k (h d) -> p k h d", d=D1 + 1)
                                ch.link(nc.vector.reciprocal(rs[b][:, :].rearrange("p (k h) -> p k h", k=2), O[:, :, :, D1]))
                                for k in range(2):
                                    last = nc.vector.tensor_tensor(on[b][:, k * 256:(k + 1) * 256].rearrange("p (h d) -> p h d", d=D1), O[:, k, :, 0:D1],
                                                                   bc(rs[b][:, 4 * k:4 * k + 4, None], [P, 4, D1]), ALU.mult)
                                last.then_inc(on_ready, 1)
                            for b in two:
                                dve.wait_ge(y_psum, at(t, b))
                                nc.vector.tensor_tensor(zmid[:, b, t + 1, :], R[b][:, 3, 0:D], zin[:, b, t + 1, :], ALU.add).then_inc(zmid_ready, 1)
                            for b in two:
                                dve.wait_ge(hs2_in[b], 48 * t + 48)
                                ch.link(nc.vector.bn_stats(st[b][:, :], hs2[b][:, :]))
                                gate()
                                ch.link(nc.vector.bn_aggr(mv[b][:, :], st[b][:, :]))
                                nc.vector.tensor_scalar_add(rv[b][:, :], mv[b][:, 1:2], EPS).then_inc(var_ready, 1)
                            for b in two:
                                dve.wait_ge(std_ready, at(t, b))
                                ch.link(nc.vector.reciprocal(rv[b][:, :], rv[b][:, :]))
                                nc.vector.tensor_scalar(hn[b][:, :], hs2[b][:, :], mv[b][:, 0:1], rv[b][:, :], ALU.subtract, ALU.mult).then_inc(hn_ready, 1)
                            for k, (r, n) in enumerate(HIDC):
                                dve.wait_ge(gelu_ready, NC * t + k + 1)
                                last = nc.vector.scalar_tensor_tensor(uT[0:n, k, :], R[0][0:n, 1 + k // 2, (k % 2) * 256:(k % 2) * 256 + B * P], b1a[0:n, k:k + 1],
                                                                      gg[0:n, k, :], ALU.add, ALU.mult)
                            last.then_inc(u_ready, 1)
                            for b in two:
                                dve.wait_ge(y2_psum, at(t, b))
                                nc.vector.tensor_tensor(zout[:, b, t + 1, :], R[b][:, 2, 0:D], zmid[:, b, t + 1, :], ALU.add).then_inc(zout_ready, 1)
                        assert ch.k == ch.per, ch.k

        def windowed():
            with ExitStack() as c:
                s = Space(c)
                z0, z1, z2 = (s.sb(n, [P, B, TB + 1, D]) for n in ("z0", "z1", "z2"))
                layernorm_stats(s, x, mean, rstd)
                zs, done = s.sem("z_set"), s.sem("x_new")
                with nc.Block() as block:
                    @block.vector
                    def _(dve):
                        nc.vector.memset(z0[:, :, 0, :], 0.0)
                        nc.vector.memset(z2[:, :, 0, :], 0.0)
                        for b in range(B):
                            v = x[:, b * TB:(b + 1) * TB, :]
                            nc.vector.tensor_tensor(z0[:, b, 1:, :], v, bc(mean[:, b * TB:(b + 1) * TB, None], [P, TB, D]), ALU.subtract).then_inc(zs, 1)
                            dve.wait_ge(zs, 2 * b + 1)
                            nc.vector.tensor_tensor(z0[:, b, 1:, :], z0[:, b, 1:, :], bc(rstd[:, b * TB:(b + 1) * TB, None], [P, TB, D]), ALU.mult).then_inc(zs, 1)
                            dve.wait_ge(zs, 2 * b + 2)
                layer(0, z0, z1, z2)
                layer(1, z2, z1, z0)
                with nc.Block() as block:
                    @block.vector
                    def _(dve):
                        for b in range(B):
                            v = x[:, b * TB:(b + 1) * TB, :]
                            nc.vector.scalar_tensor_tensor(v, z0[:, b, 1:, :], 0.5, v, ALU.mult, ALU.add).then_inc(done, 1)
                        dve.wait_ge(done, B)

        def linear():
            with ExitStack() as c:
                s = Space(c)
                two = range(B)
                both = lambda name, shape: [s.sb(f"{name}{b}", shape) for b in two]
                wqkv, wo = s.sb("wqkv", [P, 3 * D]), s.sb("wo", [P, D])
                bqkv, bo = s.sb("bqkv", [P, 3 * D]), s.sb("bo", [1, D])
                gam, bet = s.sb("gam", [P, 2 * D]), s.sb("bet", [P, 2 * D])
                headm, causal, blockm = s.sb("headm", [P, H2]), s.sb("causal", [P, P]), s.sb("blockm", [P, H2 * VA])
                xc, hn, hT = both("xc", [P, D]), both("hn", [P, D]), both("hT", [P, P])
                qk, V = both("qk", [P, 2 * D]), both("V", [P, H2, VA])
                st, mv, sd = both("st", [P, 2, 6]), both("mv", [P, 2, 2]), both("sd", [P, 2])
                xn, ga, gb, ker = both("xn", [P, 2 * D]), both("ga", [P, 2 * D]), both("gb", [P, 2 * D]), both("ker", [P, 2 * D])
                kqT, qm, Am = both("kqT", [P, 2, P]), both("qm", [P, H2, P]), both("Am", [P, H2, P])
                state, cross = both("state", [P, H2 * VA]), both("cross", [P, H2 * VA])
                den, o, oT = both("den", [P, H2]), both("o", [P, D]), both("oT", [P, P])
                R = [s.ps(f"R{b}", [P, 4, 512]) for b in two]
                w_in, setup, chain, xs = s.sem("weights"), s.sem("setup"), s.sem("steps"), s.sem("xc")
                (hn_ready, hT_psum, hT_ready, qkv_psum, var_ready, std_ready, xn_ready, scaled, shifted_, ker_ready, kqT_psum,
                 kqT_ready, qm_ready, a_psum, am_ready, o_psum, cross_psum, state_ready, on_ready, oT_psum, oT_ready,
                 y_psum, x_new) = (s.sem(n) for n in (
                 "hn_ready hT_psum hT_ready qkv_psum var_ready std_ready xn_ready scaled shifted ker_ready kqT_psum "
                 "kqT_ready qm_ready a_psum am_ready o_psum cross_psum state_ready on_ready oT_psum oT_ready "
                 "y_psum x_new").split())
                at = lambda t, b: t * B + b + 1
                layernorm_stats(s, x, mean, rstd)
                with nc.Block() as block:
                    @block.sync
                    def _(sp):
                        row = lambda n: a[n].rearrange("(o n) -> o n", o=1)
                        loads = [(wqkv[:, :], a["L1_attn_Wqkv"]), (wo[:, :], a["L1_attn_Wo"]), (bqkv[:, :], row("L1_attn_bqkv").broadcast_to([P, 3 * D])),
                                 (bo[:, :], row("L1_attn_bo")), (headm[:, :], a["c_headm"]), (causal[:, :], a["c_causal"]), (blockm[:, :], a["c_blockm"])]
                        for k, n in enumerate("qk"):
                            loads += [(gam[:, k * D:(k + 1) * D], row(f"L1_attn_gamma_{n}").broadcast_to([P, D])),
                                      (bet[:, k * D:(k + 1) * D], row(f"L1_attn_beta_{n}").broadcast_to([P, D]))]
                        for dst, src in loads:
                            sp.dma_start(dst, src).then_inc(w_in, 16)
                        sp.wait_ge(w_in, 16 * len(loads))

                    @block.vector
                    def _(dve):
                        for b in two:
                            nc.vector.memset(V[b][:, :, :], 1.0).then_inc(setup, 1)
                            nc.vector.memset(state[b][:, :], 0.0).then_inc(setup, 1)
                        dve.wait_ge(setup, 2 * B)

                with nc.Block() as block:
                    @block.tensor
                    def _(pe):
                        with pe.Fori(0, TB) as t:
                            for b in two:
                                pe.wait_ge(hn_ready, at(t, b))
                                nc.tensor.transpose(R[b][:, 0, 0:P], hn[b][:, :], ident[:, :]).then_inc(hT_psum, 1)
                            for b in two:
                                pe.wait_ge(hT_ready, at(t, b))
                                nc.tensor.matmul(R[b][:, 1, 0:3 * D], hT[b][:, :], wqkv[:, :], start=True, stop=True).then_inc(qkv_psum, 1)
                            for b in two:
                                pe.wait_ge(ker_ready, at(t, b))
                                for k in range(2):
                                    last = nc.tensor.transpose(R[b][:, 2, k * P:(k + 1) * P], ker[b][:, k * D:(k + 1) * D], ident[:, :])
                                last.then_inc(kqT_psum, 1)
                            for b in two:
                                pe.wait_ge(qm_ready, at(t, b))
                                for k in range(4):
                                    last = nc.tensor.matmul(R[b][:, k, :], kqT[b][:, 1, :], qm[b][:, 4 * k:4 * k + 4, :], start=True, stop=True)
                                last.then_inc(a_psum, 1)
                            for b in two:
                                pe.wait_ge(am_ready, at(t, b))
                                nc.tensor.matmul(R[b][:, 0, 0:H2 * VA], kqT[b][:, 0, :], state[b][:, :], start=True, stop=False)
                                for h in range(H2):
                                    last = nc.tensor.matmul(R[b][:, 0, h * VA:(h + 1) * VA], Am[b][:, h, :], V[b][:, h, :], start=False, stop=(h == H2 - 1))
                                last.then_inc(o_psum, 1)
                                nc.tensor.matmul(R[b][:, 1, 0:H2 * VA], ker[b][:, D:], V[b][:, :, :], start=True, stop=True).then_inc(cross_psum, 1)
                            for b in two:
                                pe.wait_ge(on_ready, at(t, b))
                                nc.tensor.transpose(R[b][:, 2, 0:P], o[b][:, :], ident[:, :]).then_inc(oT_psum, 1)
                            for b in two:
                                pe.wait_ge(oT_ready, at(t, b))
                                nc.tensor.matmul(R[b][:, 3, 0:D], oT[b][:, :], wo[:, :], start=True, stop=False)
                                nc.tensor.matmul(R[b][:, 3, 0:D], ones[:, :], bo[:, :], start=False, stop=True).then_inc(y_psum, 1)

                    @block.scalar
                    def _(act):
                        with act.Fori(0, TB) as t:
                            for b in two:
                                act.wait_ge(hT_psum, at(t, b))
                                nc.scalar.copy(hT[b][:, :], R[b][:, 0, 0:P]).then_inc(hT_ready, 1)
                            for b in two:
                                act.wait_ge(var_ready, at(t, b))
                                nc.scalar.activation(sd[b][:, :], mv[b][:, :, 1], ACT.Sqrt, scale=D / (D - 1)).then_inc(std_ready, 1)
                            for b in two:
                                act.wait_ge(shifted_, at(t, b))
                                nc.scalar.activation(ker[b][:, :], gb[b][:, :], ACT.Square).then_inc(ker_ready, 1)
                            for b in two:
                                act.wait_ge(kqT_psum, at(t, b))
                                nc.scalar.copy(kqT[b][:, :, :], R[b][:, 2, 0:2 * P].rearrange("p (k n) -> p k n", k=2)).then_inc(kqT_ready, 1)
                            for b in two:
                                act.wait_ge(oT_psum, at(t, b))
                                nc.scalar.copy(oT[b][:, :], R[b][:, 2, 0:P]).then_inc(oT_ready, 1)

                    @block.gpsimd
                    def _(pool):
                        with pool.Fori(0, TB) as t:
                            for b in two:
                                pool.wait_ge(xn_ready, at(t, b))
                                nc.gpsimd.tensor_tensor(ga[b][:, :], xn[b][:, :], gam[:, :], ALU.mult).then_inc(scaled, 1)
                                pool.wait_ge(scaled, at(t, b))
                                nc.gpsimd.tensor_tensor(gb[b][:, :], ga[b][:, :], bet[:, :], ALU.add).then_inc(shifted_, 1)

                    @block.vector
                    def _(dve):
                        ch = Chain(dve, chain, 18)
                        gate = lambda: nc.vector.memset(gatebuf[:, :], 0.0)
                        with dve.Fori(0, TB) as t:
                            ch.turn(t)
                            for b in two:
                                xt = x[:, bass.ds(t + b * TB, 1), :]
                                ch.link(nc.vector.tensor_tensor(xc[b][:, :], xt, bc(mean[:, bass.ds(t + b * TB, 1)], [P, D]), ALU.subtract))
                                nc.vector.tensor_tensor(hn[b][:, :], xc[b][:, :], bc(rstd[:, bass.ds(t + b * TB, 1)], [P, D]), ALU.mult).then_inc(hn_ready, 1)
                            for b in two:
                                dve.wait_ge(qkv_psum, at(t, b))
                                qkv = R[b][:, 1, 0:3 * D]
                                nc.vector.tensor_tensor(V[b][:, :, 0:D2], qkv[:, 2 * D:].rearrange("p (h d) -> p h d", d=D2),
                                                        bqkv[:, 2 * D:].rearrange("p (h d) -> p h d", d=D2), ALU.add)
                                ch.link(nc.vector.tensor_tensor(qk[b][:, :], qkv[:, 0:2 * D], bqkv[:, 0:2 * D], ALU.add))
                                for k in range(2):
                                    if k == 0:
                                        last = nc.vector.bn_stats(st[b][:, k, :], qk[b][:, k * D:(k + 1) * D])
                                    else:
                                        ch.link(nc.vector.bn_stats(st[b][:, k, :], qk[b][:, k * D:(k + 1) * D]))
                                gate()
                                for k in range(2):
                                    last = nc.vector.bn_aggr(mv[b][:, k, :], st[b][:, k, :])
                                last.then_inc(var_ready, 1)
                            for b in two:
                                dve.wait_ge(std_ready, at(t, b))
                                ch.link(nc.vector.tensor_scalar_add(sd[b][:, :], sd[b][:, :], 1e-6))
                                ch.link(nc.vector.reciprocal(sd[b][:, :], sd[b][:, :]))
                                for k in range(2):
                                    last = nc.vector.tensor_scalar(xn[b][:, k * D:(k + 1) * D], qk[b][:, k * D:(k + 1) * D], mv[b][:, k, 0:1], sd[b][:, k:k + 1],
                                                                   ALU.subtract, ALU.mult)
                                last.then_inc(xn_ready, 1)
                            for b in two:
                                dve.wait_ge(kqT_ready, at(t, b))
                                nc.vector.tensor_tensor(qm[b][:, :, :], bc(kqT[b][:, 0:1, :], [P, H2, P]), bc(headm[:, :, None], [P, H2, P]), ALU.mult).then_inc(qm_ready, 1)
                            for b in two:
                                dve.wait_ge(a_psum, at(t, b))
                                nc.vector.tensor_tensor(Am[b][:, :, :], R[b][:, :, :].rearrange("p k (h n) -> p (k h) n", n=P),
                                                        bc(causal[:, None, :], [P, H2, P]), ALU.mult).then_inc(am_ready, 1)
                            for b in two:
                                dve.wait_ge(o_psum, at(t, b))
                                O = R[b][:, 0, 0:H2 * VA].rearrange("p (h d) -> p h d", d=VA)
                                ch.link(nc.vector.tensor_scalar_add(den[b][:, :], O[:, :, D2], 1e-6))
                                ch.link(nc.vector.reciprocal(den[b][:, :], den[b][:, :]))
                                nc.vector.tensor_tensor(o[b][:, :].rearrange("p (h d) -> p h d", d=D2), O[:, :, 0:D2], bc(den[b][:, :, None], [P, H2, D2]), ALU.mult).then_inc(on_ready, 1)
                            for b in two:
                                dve.wait_ge(cross_psum, at(t, b))
                                ch.link(nc.vector.tensor_tensor(cross[b][:, :], R[b][:, 1, 0:H2 * VA], blockm[:, :], ALU.mult))
                                ch.link(nc.vector.tensor_tensor(state[b][:, :], state[b][:, :], cross[b][:, :], ALU.add))
                            for b in two:
                                dve.wait_ge(y_psum, at(t, b))
                                xt = x[:, bass.ds(t + b * TB, 1), :]
                                nc.vector.tensor_tensor(xt, R[b][:, 3, 0:D], xt, ALU.add).then_inc(x_new, 1)
                        assert ch.k == ch.per, ch.k
                        dve.wait_ge(x_new, NT)

        def attention():
            with ExitStack() as c:
                s = Space(c)
                hT = s.sb("hT", [P, NT * P])
                cosq, sinq, cosk, sink = (s.sb(n, [P, S]) for n in ("cosq", "sinq", "cosk", "sink"))
                dist = s.sb("dist", [P, BIASW])
                slope, amp, sgn = s.sb("slope", [P, H0]), s.sb("amp", [P, H0]), s.sb("sgn", [P, 2])
                O_all = s.sb("O_all", [P, NT, H0 * D0])
                prepare(s, hT, cosq, sinq, cosk, sink, dist, slope, amp, sgn)
                heads(hT, cosq, sinq, cosk, sink, dist, slope, amp, O_all)
                project(O_all)

        def prepare(s, hT, cosq, sinq, cosk, sink, dist, slope, amp, sgn):
            layernorm_stats(s, x, mean, rstd)
            with ExitStack() as c:
                s = Space(c)
                xc, hn = s.sb("xc", [P, NT, D]), s.sb("hn", [P, NT, D])
                freq, ang, turns, r, over = s.sb("freq", [P, 1]), s.sb("ang", [P, S]), s.sb("turns", [P, S]), s.sb("r", [P, S]), s.sb("over", [P, S])
                T4 = [s.ps(f"T{k}", [P, 512]) for k in range(4)]
                w_in, iotas, hn_ready, hT_psum, chain, r_ready, sin_ready = (s.sem(n) for n in ("weights", "iotas", "hn_ready", "hT_psum", "chain", "r_ready", "sin_ready"))
                hT_ready = s.sem("hT_ready")
                PI = 3.1415925
                TWO_PI = 6.283185307179586
                MAGIC = 12582912.0
                C1 = 6.28125
                C2 = 1014 / 2 ** 19
                C3 = TWO_PI - C1 - C2
                with nc.Block() as block:
                    @block.sync
                    def _(sp):
                        nf = D0 // 2
                        for k in range(P // nf):
                            sp.dma_start(freq[k * nf:(k + 1) * nf, :], a["L0_attn_rope_freqs"].rearrange("(p o) -> p o", o=1)).then_inc(w_in, 16)
                        sp.dma_start(slope[:, :], a["L0_attn_bias_a"].rearrange("h a b -> (a b) h").broadcast_to([P, H0])).then_inc(w_in, 16)
                        sp.dma_start(amp[:, :], a["L0_attn_bias_p"].rearrange("h a b -> (a b) h").broadcast_to([P, H0])).then_inc(w_in, 16)
                        sp.dma_start(sgn[:, :], a["c_sgn"]).then_inc(w_in, 16)
                        sp.wait_ge(w_in, 16 * 7)

                    @block.gpsimd
                    def _(pool):
                        nc.gpsimd.iota(ang[:, :], pattern=[[1, S]], base=0, channel_multiplier=0, allow_small_or_imprecise_dtypes=True).then_inc(iotas, 1)
                        nc.gpsimd.iota(dist[:, :], pattern=[[1, BIASW]], base=P - S, channel_multiplier=-1, allow_small_or_imprecise_dtypes=True).then_inc(iotas, 1)
                        pool.wait_ge(iotas, 2)

                    @block.tensor
                    def _(pe):
                        for t in range(NT):
                            if t % 4 == 0:
                                pe.wait_ge(hn_ready, t // 4 + 1)
                            last = nc.tensor.transpose(T4[t // 4][:, (t % 4) * P:(t % 4 + 1) * P], hn[:, t, :], ident[:, :])
                            if t % 4 == 3:
                                last.then_inc(hT_psum, 1)

                    @block.scalar
                    def _(act):
                        for k in range(4):
                            act.wait_ge(hT_psum, k + 1)
                            nc.scalar.copy(hT[:, k * 512:(k + 1) * 512], T4[k][:, :]).then_inc(hT_ready, 1)
                        act.wait_ge(r_ready, 1)
                        nc.scalar.activation(sink[:, :], r[:, :], ACT.Sin).then_inc(sin_ready, 1)
                        act.wait_ge(r_ready, 2)
                        nc.scalar.activation(cosk[:, :], over[:, :], ACT.Sin).then_inc(sin_ready, 1)
                        act.wait_ge(hT_ready, 4)
                        act.wait_ge(sin_ready, 2)

                    @block.vector
                    def _(dve):
                        ch = Chain(dve, chain, 0)
                        for k in range(4):
                            sl = slice(4 * k, 4 * k + 4)
                            ch.link(nc.vector.tensor_tensor(xc[:, sl, :], x[:, sl, :], bc(mean[:, sl, None], [P, 4, D]), ALU.subtract))
                            nc.vector.tensor_tensor(hn[:, sl, :], xc[:, sl, :], bc(rstd[:, sl, None], [P, 4, D]), ALU.mult).then_inc(hn_ready, 1)
                        dve.wait_ge(w_in, 16 * 7)
                        dve.wait_ge(iotas, 2)
                        ch.link(nc.vector.scalar_tensor_tensor(dist[:, :], dist[:, :], -1.0, dist[:, :], ALU.mult, ALU.max))
                        ch.link(nc.vector.tensor_scalar_max(slope[:, :], slope[:, :], 0.01))
                        ch.link(nc.vector.tensor_scalar_max(amp[:, :], amp[:, :], 0.01))
                        ch.link(nc.vector.tensor_scalar(ang[:, :], ang[:, :], freq[:, :], None, ALU.mult))
                        ch.link(nc.vector.tensor_scalar(turns[:, :], ang[:, :], 1 / TWO_PI, MAGIC, ALU.mult, ALU.add))
                        ch.link(nc.vector.tensor_scalar(turns[:, :], turns[:, :], MAGIC, None, ALU.subtract))
                        ch.link(nc.vector.scalar_tensor_tensor(r[:, :], turns[:, :], -C1, ang[:, :], ALU.mult, ALU.add))
                        ch.link(nc.vector.scalar_tensor_tensor(r[:, :], turns[:, :], -C2, r[:, :], ALU.mult, ALU.add))
                        ch.link(nc.vector.scalar_tensor_tensor(r[:, :], turns[:, :], -C3, r[:, :], ALU.mult, ALU.add))

                        def wrap(v, tmp):
                            ch.link(nc.vector.tensor_scalar(tmp[:, :], v[:, :], PI, -TWO_PI, ALU.is_gt, ALU.mult))
                            ch.link(nc.vector.tensor_tensor(v[:, :], v[:, :], tmp[:, :], ALU.add))
                            ch.link(nc.vector.tensor_scalar(tmp[:, :], v[:, :], -PI, TWO_PI, ALU.is_lt, ALU.mult))
                            ch.link(nc.vector.tensor_tensor(v[:, :], v[:, :], tmp[:, :], ALU.add))
                            return nc.vector.tensor_scalar(v[:, :], v[:, :], PI, -PI, ALU.min, ALU.max)
                        wrap(r, turns).then_inc(r_ready, 1)
                        dve.wait_ge(r_ready, 1)
                        ch.link(nc.vector.tensor_scalar_add(over[:, :], r[:, :], TWO_PI / 4))
                        wrap(over, turns).then_inc(r_ready, 1)
                        dve.wait_ge(sin_ready, 2)
                        nc.vector.tensor_scalar(sinq[:, :], sink[:, :], sgn[:, 1:2], None, ALU.mult)
                        ch.link(nc.vector.tensor_scalar(cosq[:, :], cosk[:, :], -1.0 / D0 ** 0.5, None, ALU.mult))
                        ch.link(nc.vector.tensor_scalar(sink[:, :], sink[:, :], sgn[:, 0:1], None, ALU.mult))

        def heads(hT, cosq, sinq, cosk, sink, dist, slope, amp, O_all):
            with ExitStack() as c:
                s = Space(c)
                w = s.sb("w", [P, 5, P])
                ab = s.sb("ab", [P, 4])
                qT, kT = s.sb("qT", [P, NT * P]), s.sb("kT", [P, NT * P])
                m1, m2 = s.sb("m1", [P, 2, 512]), s.sb("m2", [P, 2, 512])
                V = s.sb("V", [P, NT, 2, D0 + 1])
                bias = s.sb("bias", [P, 2, BIASW])
                y, pr, pT = s.sb("y", [P, 2, S]), s.sb("pr", [P, 2, S]), s.sb("pT", [P, 2, TB, P])
                U = 2 * NT
                low, rz = s.sb("low", [P, U]), s.sb("rz", [P, 2])
                Sp = [s.ps(f"S{k}", [P, S]) for k in range(2)]
                Tp = s.ps("Tp", [P, 2, 512])
                Op = [s.ps(f"O{k}", [P, 512]) for k in range(2)]
                (w_in, setup, ab_ready, ln_ready, bias_ready, proj_psum, m_ready, rot_ready, v_psum, v_ready, s_psum, y_ready, exp_ready,
                 ta_psum, tb_psum, ta_ready, tb_ready, o_psum, r_ready, o_ready) = (s.sem(n) for n in (
                 "weights setup ab_ready ln_ready bias_ready proj_psum m_ready rot_ready v_psum v_ready s_psum y_ready exp_ready "
                 "ta_psum tb_psum ta_ready tb_ready o_psum r_ready o_ready").split())
                LAST = U + 3
                tile, head, batch = (lambda v: v // 2), (lambda v: v % 2), (lambda v: v // 2 // TB)

                with nc.Block() as block:
                    @block.vector
                    def _(dve):
                        nc.vector.memset(V[:, :, :, :], 1.0).then_inc(setup, 1)
                        dve.wait_ge(setup, 1)

                with nc.Block() as block:
                    @block.sync
                    def _(sp):
                        wsrc = a["L0_attn_w5"]
                        sp.dma_start(w[:, :, :], wsrc[0]).then_inc(w_in, 16)
                        with sp.Fori(0, PAIRS - 1) as i:
                            sp.wait_ge(v_psum, 4 * i + 4)
                            sp.dma_start(w[:, :, :], wsrc[bass.ds(i + 1, 1)].rearrange("o p k n -> p (o k) n")).then_inc(w_in, 16)

                    @block.tensor
                    def _(pe):
                        with pe.Fori(0, PAIRS) as i:
                            pe.wait_ge(w_in, 16 * i + 16)
                            for j in range(8):
                                if j >= 2:
                                    pe.wait_ge(m_ready, 8 * i + j - 1)
                                for k in range(2):
                                    last = nc.tensor.matmul(Sp[j % 2][:, k * 512:(k + 1) * 512], w[:, 2 * (j % 2) + k, :],
                                                            hT[:, (j // 2) * 512:(j // 2 + 1) * 512], start=True, stop=True)
                                last.then_inc(proj_psum, 1)
                            for k in range(4):
                                if k >= 2:
                                    pe.wait_ge(v_ready, 4 * i + k - 1)
                                for t in range(4):
                                    last = nc.tensor.matmul(Tp[:, k % 2, t * P:(t + 1) * P], hT[:, (4 * k + t) * P:(4 * k + t + 1) * P], w[:, 4, :],
                                                            start=True, stop=True)
                                last.then_inc(v_psum, 1)
                            pe.wait_ge(rot_ready, 8 * i + 8)
                            pe.wait_ge(v_ready, 4 * i + 4)
                            for n in range(LAST):
                                v = n
                                if v < U:
                                    if v >= 2:
                                        pe.wait_ge(y_ready, U * i + v - 1)
                                    r = head(v) * D0
                                    for k in range(2):
                                        last = nc.tensor.matmul(Sp[v % 2][:, k * 512:(k + 1) * 512], qT[r:r + D0, tile(v) * P:(tile(v) + 1) * P],
                                                                kT[r:r + D0, batch(v) * S + k * 512:batch(v) * S + (k + 1) * 512], start=True, stop=True)
                                    last.then_inc(s_psum, 1)
                                v = n - 2
                                if 0 <= v < U:
                                    pe.wait_ge(exp_ready, U * i + v + 1)
                                    for k in range(TB):
                                        if v >= 1 and k == 0:
                                            pe.wait_ge(ta_ready, U * i + v)
                                        if v >= 1 and k == 4:
                                            pe.wait_ge(tb_ready, U * i + v)
                                        last = nc.tensor.transpose(Tp[:, k // 4, (k % 4) * P:(k % 4 + 1) * P], pr[:, v % 2, k * P:(k + 1) * P], ident[:, :])
                                        if k == 3:
                                            last.then_inc(ta_psum, 1)
                                    last.then_inc(tb_psum, 1)
                                v = n - 3
                                if 0 <= v < U:
                                    if v >= 2:
                                        pe.wait_ge(o_ready, U * i + v - 1)
                                    pe.wait_ge(ta_ready, U * i + v + 1)
                                    pe.wait_ge(tb_ready, U * i + v + 1)
                                    for k in range(TB):
                                        last = nc.tensor.matmul(Op[v % 2][:, 0:D0 + 1], pT[:, v % 2, k, :], V[:, batch(v) * TB + k, head(v), :],
                                                                start=(k == 0), stop=(k == TB - 1))
                                    last.then_inc(o_psum, 1)

                    @block.scalar
                    def _(act):
                        with act.Fori(0, PAIRS) as i:
                            act.wait_ge(ab_ready, i + 1)
                            for h in range(2):
                                nc.scalar.activation(bias[:, h, :], dist[:, :], ACT.Ln, bias=1.0, scale=ab[:, h:h + 1]).then_inc(ln_ready, 1)
                            for k in range(4):
                                act.wait_ge(v_psum, 4 * i + k + 1)
                                nc.scalar.copy(V[:, 4 * k:4 * k + 4, :, 0:D0], Tp[:, k % 2, :].rearrange("p (t h d) -> p t h d", t=4, h=2)).then_inc(v_ready, 1)
                            for n in range(LAST):
                                v = n - 2
                                if 0 <= v < U:
                                    act.wait_ge(tb_psum, U * i + v + 1)
                                    nc.scalar.copy(pT[:, v % 2, 4:, :], Tp[:, 1, :].rearrange("p (k n) -> p k n", n=P)).then_inc(tb_ready, 1)
                                v = n
                                if v < U:
                                    act.wait_ge(y_ready, U * i + v + 1)
                                    if v >= 2:
                                        act.wait_ge(tb_psum, U * i + v - 1)
                                    nc.scalar.activation(pr[:, v % 2, :], y[:, v % 2, :], ACT.Exp, bias=low[:, v:v + 1], scale=-1.0).then_inc(exp_ready, 1)

                    @block.gpsimd
                    def _(pool):
                        with pool.Fori(0, PAIRS) as i:
                            for j in range(8):
                                pool.wait_ge(m_ready, 8 * i + j + 1)
                                dst = (qT, kT)[j % 2]
                                nc.gpsimd.tensor_tensor(dst[:, (j // 2) * 512:(j // 2 + 1) * 512], m1[:, j % 2, :], m2[:, j % 2, :], ALU.add).then_inc(rot_ready, 1)

                    @block.vector
                    def _(dve):
                        with dve.Fori(0, PAIRS) as i:
                            nc.vector.tensor_copy(ab[:, 0:2], slope[:, bass.ds(2 * i, 2)])
                            nc.vector.tensor_copy(ab[:, 2:4], amp[:, bass.ds(2 * i, 2)]).then_inc(ab_ready, 1)
                            for j in range(8):
                                cs, sn = ((cosq, sinq), (cosk, sink))[j % 2]
                                pos = slice((j // 2 % 2) * 512, (j // 2 % 2 + 1) * 512)
                                if j >= 2:
                                    dve.wait_ge(rot_ready, 8 * i + j - 1)
                                dve.wait_ge(proj_psum, 8 * i + j + 1)
                                nc.vector.tensor_tensor(m1[:, j % 2, :], Sp[j % 2][:, 0:512], cs[:, pos], ALU.mult)
                                nc.vector.tensor_tensor(m2[:, j % 2, :], Sp[j % 2][:, 512:], sn[:, pos], ALU.mult).then_inc(m_ready, 1)
                            dve.wait_ge(ln_ready, 2 * i + 2)
                            dve.wait_ge(ab_ready, i + 1)
                            for h in range(2):
                                nc.vector.tensor_scalar(bias[:, h, :], bias[:, h, :], ab[:, 2 + h:3 + h], None, ALU.mult).then_inc(bias_ready, 1)
                            dve.wait_ge(bias_ready, 2 * i + 2)
                            for n in range(LAST):
                                v = n
                                if v < U:
                                    dve.wait_ge(s_psum, U * i + v + 1)
                                    if v >= 2:
                                        dve.wait_ge(exp_ready, U * i + v - 1)
                                    nc.vector.memset(gatebuf[:, v % 4:v % 4 + 1], 0.0)
                                    off = S - P - (tile(v) % TB) * P
                                    nc.vector.tensor_tensor_reduce(out=y[:, v % 2, :], in0=Sp[v % 2][:, :], in1=bias[:, head(v), off:off + S], scale=1.0, scalar=3e38,
                                                                   op0=ALU.add, op1=ALU.min, accum_out=low[:, v:v + 1]).then_inc(y_ready, 1)
                                v = n - 2
                                if 0 <= v < U:
                                    dve.wait_ge(ta_psum, U * i + v + 1)
                                    nc.vector.tensor_copy(pT[:, v % 2, 0:4, :], Tp[:, 0, :].rearrange("p (k n) -> p k n", n=P)).then_inc(ta_ready, 1)
                                v = n - 3
                                if 0 <= v < U:
                                    dve.wait_ge(o_psum, U * i + v + 1)
                                    nc.vector.reciprocal(rz[:, v % 2:v % 2 + 1], Op[v % 2][:, D0:D0 + 1]).then_inc(r_ready, 1)
                                    dve.wait_ge(r_ready, U * i + v + 1)
                                    nc.vector.tensor_scalar(O_all[:, tile(v), bass.ds(2 * D0 * i + head(v) * D0, D0)], Op[v % 2][:, 0:D0],
                                                            rz[:, v % 2:v % 2 + 1], None, ALU.mult).then_inc(o_ready, 1)

        def project(O_all):
            with ExitStack() as c:
                s = Space(c)
                KC = H0 * D0 // P
                wo = s.sb("wo", [P, KC, D])
                stage, oT = s.sb("stage", [P, 2, H0 * D0]), s.sb("oT", [P, 2, KC, P])
                Tp = [s.ps(f"T{k}", [P, 2, 512]) for k in range(2)]
                Y = [s.ps(f"Y{k}", [P, 512]) for k in range(2)]
                w_in, staged, t_psum, oT_ready, y_psum, x_new = (s.sem(n) for n in ("weights", "staged", "t_psum", "oT_ready", "y_psum", "x_new"))
                with nc.Block() as block:
                    @block.sync
                    def _(sp):
                        sp.dma_start(wo[:, :, :], a["L0_attn_out_w"].rearrange("(k p) d -> p k d", p=P)).then_inc(w_in, 16)
                        sp.wait_ge(w_in, 16)

                    @block.tensor
                    def _(pe):
                        pe.wait_ge(w_in, 16)
                        with pe.Fori(0, NT // 2) as i:
                            for k in range(2):
                                pe.wait_ge(staged, 2 * i + k + 1)
                                for n in range(KC):
                                    last = nc.tensor.transpose(Tp[k][:, n // 4, (n % 4) * P:(n % 4 + 1) * P], stage[:, k, n * P:(n + 1) * P], ident[:, :])
                                last.then_inc(t_psum, 1)
                            for k in range(2):
                                pe.wait_ge(oT_ready, 2 * i + k + 1)
                                for n in range(KC):
                                    last = nc.tensor.matmul(Y[k][:, 0:D], oT[:, k, n, :], wo[:, n, :], start=(n == 0), stop=(n == KC - 1))
                                last.then_inc(y_psum, 1)

                    @block.scalar
                    def _(act):
                        with act.Fori(0, NT // 2) as i:
                            for k in range(2):
                                act.wait_ge(t_psum, 2 * i + k + 1)
                                nc.scalar.copy(oT[:, k, :, :], Tp[k][:, :, :].rearrange("p a (b n) -> p (a b) n", n=P)).then_inc(oT_ready, 1)

                    @block.vector
                    def _(dve):
                        with dve.Fori(0, NT // 2) as i:
                            for k in range(2):
                                nc.vector.tensor_scalar(stage[:, k, :], O_all[:, bass.ds(2 * i + k, 1), :].rearrange("p o n -> p (o n)"), 1.0, None, ALU.mult).then_inc(staged, 1)
                            for k in range(2):
                                dve.wait_ge(y_psum, 2 * i + k + 1)
                                xt = x[:, bass.ds(2 * i + k, 1), :]
                                nc.vector.tensor_tensor(xt, Y[k][:, 0:D], xt, ALU.add).then_inc(x_new, 1)
                        dve.wait_ge(x_new, NT)

        moe()
        attention()
        moe()
        windowed()
        linear()
        windowed()
        s_out = g.sem("s_out")
        with nc.Block() as block:
            @block.sync
            def _(sp):
                sp.dma_start(out.rearrange("b (t p) d -> p (b t) d", p=P), x[:, :, :]).then_inc(s_out, 16)
                sp.wait_ge(s_out, 16)


def constants():
    import numpy as np
    c = {"c_ident": np.eye(P)}
    r, m = np.arange(P)[:, None, None], np.arange(P)[None, None, :]
    ch = np.arange(EC)[None, :, None]
    c["c_sel"] = (r % E == 2 * ch + m // F) & (r < 3 * E)
    c["c_rank"] = np.tile(E - np.arange(E), (P, 1))
    half = np.arange(0, D1, 2, dtype=np.float32)
    inv = (np.float32(1.0) / np.float32(10000.0) ** (half / np.float32(D1))).astype(np.float32)
    t = np.arange(S, dtype=np.float32)
    ang = (t[:, None] * inv[None, :]).astype(np.float32).astype(np.float64)
    base = (half + np.float32(0.4 * D1)) / np.float32(1.4 * D1)
    scale = base[None, :].astype(np.float64) ** ((t - S // 2) / (WIN // 2))[:, None].astype(np.float64)
    cos, sin = np.cos(ang), np.sin(ang)
    co = np.stack([np.tile(8.0 * cos * scale, 2), np.tile(cos / scale, 2)], 1)
    si = np.stack([np.concatenate([-8.0 * sin * scale, 8.0 * sin * scale], 1), np.concatenate([-sin / scale, sin / scale], 1)], 1)
    c["c_cos"], c["c_sin"] = (v.reshape(TB, P, 2, D1).transpose(1, 0, 2, 3) for v in (co, si))
    q, tt, j = np.arange(P)[:, None, None], np.arange(TB)[None, :, None], np.arange(KEYS)[None, None, :] - WIN
    c["c_mask"] = np.where((j > q) | (q > j + WIN) | (tt * P + j < 0), MASKED, 0.0)
    p = np.arange(P)
    first = p % D0 < D0 // 2
    c["c_sgn"] = np.stack([np.where(first, -1.0, 1.0), np.where(first, 1.0, -1.0) / D0 ** 0.5], 1)
    c["c_headm"] = p[:, None] // D2 == np.arange(H2)[None, :]
    c["c_causal"] = p[:, None] <= p[None, :]
    c["c_blockm"] = p[:, None] // D2 == np.arange(H2 * VA)[None, :] // VA
    return {k: np.ascontiguousarray(v, dtype=np.float32) for k, v in c.items()}


def kernel(**inputs):
    import numpy as _np
    import concourse.bacc as _bacc
    from concourse import mybir as _mybir
    from concourse.bass_utils import run_bass_kernel_spmd as _run

    nc = _bacc.Bacc("TRN2", target_bir_lowering=False, num_devices=1)
    arrays, args = {}, {}
    data = dict(inputs)
    w = _np.asarray(data.pop("L0_attn_qkv_w")).reshape(3, PAIRS, 2, 2, D0 // 2, D)
    q, k, v = w
    data["L0_attn_w5"] = _np.stack([m.reshape(PAIRS, P, D) for m in (q, q[:, :, ::-1], k, k[:, :, ::-1], v)], 1).transpose(0, 3, 1, 2)
    data["L0_attn_out_w"] = _np.ascontiguousarray(_np.asarray(data["L0_attn_out_w"]).T)
    data.update(constants())
    for name, v in data.items():
        v = _np.ascontiguousarray(v)
        arrays[f"in_{name}"] = v
        args[name] = nc.dram_tensor(f"in_{name}", v.shape, _mybir.dt.from_np(v.dtype), kind="ExternalInput").ap()
    out = nc.dram_tensor("out_0_dram", (B, S, D), _mybir.dt.float32, kind="ExternalOutput").ap()
    build(nc, args, out)
    r = _run(nc, [arrays], core_ids=[0])
    return r.results[0]["out_0_dram"]
```

```python
B, S, D = 2, 1024, 128
P = 128
NT = B * S // P
TB = S // P
EPS = 1e-5

E, F, FS = 16, 64, 128
HC = (E * F + FS) // P
EC = E * F // P
BT = 4
NB = NT // BT

H0, D0 = 16, 64
PAIRS = H0 // 2
BIASW = 2 * S - P

DEPTH, H1, D1, WIN = 2, 8, 64, 64
INNER = H1 * D1
KEYS = WIN + P
HID = int(D * 4 * 2 / 3)
HIDC = [(c, min(P, HID - c)) for c in range(0, HID, P)]
MASKED = -1e30

H2 = 16
D2 = D // H2
VA = D2 + 1


def build(nc, a, out):
    import numpy as np
    import concourse.bass as bass
    from concourse import mybir
    from contextlib import ExitStack

    f32, bf16 = mybir.dt.float32, mybir.dt.bfloat16
    ALU, ACT, AX = mybir.AluOpType, mybir.ActivationFunctionType, mybir.AxisListType.X
    names = [0]

    class Space:
        def __init__(self, ctx):
            self.ctx = ctx
            names[0] += 1
            self.n = names[0]
            self.sems = []
            ctx.callback(self.clear)

        def clear(self):
            if self.sems and self.n > 1:
                with nc.Block() as block:
                    @block.sync
                    def _(sp):
                        for sem in self.sems:
                            sp.sem_clear(sem)

        def sb(self, name, shape, dt=f32):
            return self.ctx.enter_context(nc.sbuf_tensor(f"{name}_{self.n}", shape, dt))

        def ps(self, name, shape, dt=f32):
            return self.ctx.enter_context(nc.psum_tensor(f"{name}_{self.n}", shape, dt))

        def sem(self, name):
            handle = self.ctx.enter_context(nc.semaphore(f"{name}_{self.n}"))
            self.sems.append(handle)
            return handle

    class Chain:
        def __init__(self, eng, sem, per):
            self.eng, self.sem, self.per, self.k, self.base = eng, sem, per, 0, 0

        def turn(self, i):
            self.base, self.k = i * self.per, 0

        def link(self, ins):
            ins.then_inc(self.sem, 1)
            self.k += 1
            self.eng.wait_ge(self.sem, self.base + self.k)

    def layernorm_stats(sp, src, dst_mean, dst_rstd):
        stats, mv, tmp = sp.sb("stats", [P, NT, 6]), sp.sb("mv", [P, NT, 2]), sp.sb("tmp", [P, NT])
        c, s = sp.sem("ln_chain"), sp.sem("ln_std")
        with nc.Block() as block:
            @block.vector
            def _(dve):
                for t in range(NT):
                    last = nc.vector.bn_stats(stats[:, t, :], src[:, t, :])
                last.then_inc(c, 1)
                dve.wait_ge(c, 1)
                for t in range(NT):
                    last = nc.vector.bn_aggr(mv[:, t, :], stats[:, t, :])
                last.then_inc(c, 1)
                dve.wait_ge(c, 2)
                nc.vector.tensor_copy(dst_mean[:, :], mv[:, :, 0])
                nc.vector.tensor_scalar_add(tmp[:, :], mv[:, :, 1], EPS).then_inc(c, 1)
                dve.wait_ge(s, 1)
                nc.vector.reciprocal(dst_rstd[:, :], tmp[:, :]).then_inc(c, 1)
                dve.wait_ge(c, 4)

            @block.scalar
            def _(act):
                act.wait_ge(c, 3)
                nc.scalar.activation(tmp[:, :], tmp[:, :], ACT.Sqrt).then_inc(s, 1)
                act.wait_ge(s, 1)

    def bc(ap, shape):
        return ap.broadcast_to(shape)

    ctx = ExitStack()
    with ctx:
        g = Space(ctx)
        x = g.sb("x", [P, NT, D])
        mean, rstd = g.sb("mean", [P, NT]), g.sb("rstd", [P, NT])
        ident, identb = g.sb("ident", [P, P]), g.sb("identb", [P, P], bf16)
        ones = g.sb("ones", [1, P])
        gatebuf = g.sb("gatebuf", [P, 4])
        xd = a["L0_attn_x"].rearrange("b (t p) d -> p (b t) d", p=P)
        s_load, s_const = g.sem("load"), g.sem("const")
        with nc.Block() as block:
            @block.sync
            def _(sp):
                sp.dma_start(x[:, :, :], xd).then_inc(s_load, 16)
                sp.dma_start(ident[:, :], a["c_ident"]).then_inc(s_load, 16)
                sp.wait_ge(s_load, 32)

            @block.vector
            def _(dve):
                nc.vector.memset(ones[:, :], 1.0).then_inc(s_const, 1)
                nc.vector.memset(gatebuf[:, :], 0.0).then_inc(s_const, 1)
                dve.wait_ge(s_load, 32)
                nc.vector.tensor_copy(identb[:, :], ident[:, :]).then_inc(s_const, 1)
                dve.wait_ge(s_const, 3)

        def moe(prefetch=(), fetched=None):
            with ExitStack() as c:
                s = Space(c)
                wg, wu = s.sb("wg", [P, HC * P]), s.sb("wu", [P, HC * P])
                wd, wr = s.sb("wd", [P, HC, D]), s.sb("wr", [P, E])
                self32, sel = s.sb("self32", [P, EC, P]), s.sb("sel", [P, EC, P], bf16)
                rank = s.sb("rank", [P, E])
                hn, hT = s.sb("hn", [P, BT, D]), s.sb("hT", [P, BT * P])
                xc = s.sb("xc", [P, BT, D])
                sg, hid, act_ = s.sb("sg", [P, 2, BT * P]), s.sb("hid", [P, 2, BT * P]), s.sb("act", [P, HC, BT * P])
                G = [P, BT, E]
                d, e, p, p2, t1, t2, s1, cw, rest = (s.sb(n, G) for n in
                    ("d", "e", "p", "p2", "t1", "t2", "s1", "cw", "rest"))
                m4, r4 = s.sb("m4", [P, BT]), s.sb("r4", [P, BT])
                cw3, cwT = s.sb("cw3", [P, BT, P // E, E], bf16), s.sb("cwT", [P, BT * P], bf16)
                pA = s.ps("pA", [P, BT * P])
                pAb = s.ps("pAb", [P, BT * P], bf16)
                pY = pA
                pg, pu, pc = (s.ps(n, [P, 2, BT * P]) for n in ("pg", "pu", "pc"))
                s_hid = s.sem("half_hidden")
                w_in = s.sem("weights"); sel_ok = s.sem("sel_ok")
                hn_ready, hT_psum, hT_ready = s.sem("hn_ready"), s.sem("hT_psum"), s.sem("hT_ready")
                logits, e_in, e_ready, cw_ready, cT_psum, cwT_ready = (s.sem(n) for n in
                    ("logits", "e_in", "e_ready", "cw_ready", "cT_psum", "cwT_ready"))
                gate_psum, up_psum, silu_ready, hid_ready = (s.sem(n) for n in ("gate_psum", "up_psum", "silu_ready", "hid_ready"))
                y_psum, x_new, chain = s.sem("y_psum"), s.sem("x_new"), s.sem("chain")
                layernorm_stats(s, x, mean, rstd)
                L = pA[:, 0:BT * E].rearrange("p (t e) -> p t e", e=E)

                with nc.Block() as block:
                    @block.sync
                    def _(sp):
                        sp.dma_start(wg[:, 0:E * F].rearrange("p (e f) -> p e f", e=E), a["L0_ffn_Wg"].rearrange("e d f -> d e f")).then_inc(w_in, 16)
                        sp.dma_start(wu[:, 0:E * F].rearrange("p (e f) -> p e f", e=E), a["L0_ffn_Wu"].rearrange("e d f -> d e f")).then_inc(w_in, 16)
                        sp.dma_start(wg[:, E * F:], a["L0_ffn_Sg"]).then_inc(w_in, 16)
                        sp.dma_start(wu[:, E * F:], a["L0_ffn_Su"]).then_inc(w_in, 16)
                        sp.dma_start(wd[:, 0:EC, :], a["L0_ffn_Wd"].rearrange("(c two) f d -> (two f) c d", two=2)).then_inc(w_in, 16)
                        sp.dma_start(wd[:, EC, :], a["L0_ffn_Sd"]).then_inc(w_in, 16)
                        sp.dma_start(wr[:, :], a["L0_ffn_Wr"]).then_inc(w_in, 16)
                        sp.dma_start(self32[:, :, :], a["c_sel"]).then_inc(w_in, 16)
                        sp.dma_start(rank[:, :], a["c_rank"]).then_inc(w_in, 16)
                        for dst, src in prefetch:
                            sp.dma_start(dst, src).then_inc(fetched, 16)
                        sp.wait_ge(w_in, 144)

                    @block.tensor
                    def _(pe):
                        def front(i):
                            pe.wait_ge(hn_ready, i + 1)
                            for j in range(BT):
                                last = nc.tensor.transpose(pA[:, j * P:(j + 1) * P], hn[:, j, :], ident[:, :])
                            last.then_inc(hT_psum, 1)
                            pe.wait_ge(hT_ready, i + 1)
                            for j in range(BT):
                                last = nc.tensor.matmul(L[:, j, :], hT[:, j * P:(j + 1) * P], wr[:, :], start=True, stop=True)
                            last.then_inc(logits, 1)

                        def weights(i):
                            pe.wait_ge(cw_ready, i + 1)
                            for j in range(BT):
                                last = nc.tensor.transpose(pAb[:, j * P:(j + 1) * P],
                                                           cw3[:, j, :, :].rearrange("p a b -> p (a b)"), identb[:, :])
                            last.then_inc(cT_psum, 1)

                        def up(i):
                            pe.wait_ge(cwT_ready, i + 1)
                            for c in range(HC):
                                if c >= 2:
                                    pe.wait_ge(silu_ready, i * HC + c - 1)
                                nc.tensor.matmul(pg[:, c % 2, :], wg[:, c * P:(c + 1) * P], hT[:, :], start=True, stop=True).then_inc(gate_psum, 1)
                                if c >= 2:
                                    pe.wait_ge(hid_ready, i * HC + c - 1)
                                last = nc.tensor.matmul(pu[:, c % 2, :], wu[:, c * P:(c + 1) * P], hT[:, :], start=True, stop=True)
                                if c < EC:
                                    last = nc.tensor.matmul(pc[:, c % 2, :], sel[:, c, :], cwT[:, :], start=True, stop=True)
                                last.then_inc(up_psum, 1)

                        def down(i):
                            pe.wait_ge(hid_ready, i * HC + HC)
                            for j in range(BT):
                                for c in range(HC):
                                    last = nc.tensor.matmul(pY[:, j * D:(j + 1) * D], act_[:, c, j * P:(j + 1) * P], wd[:, c, :],
                                                            start=(c == 0), stop=(c == HC - 1))
                            last.then_inc(y_psum, 1)

                        pe.wait_ge(w_in, 144)
                        pe.wait_ge(sel_ok, 2)
                        with pe.Fori(0, NB) as i:
                            front(i)
                            weights(i)
                            up(i)
                            down(i)

                    @block.scalar
                    def _(act):
                        with act.Fori(0, NB) as i:
                            act.wait_ge(hT_psum, i + 1)
                            nc.scalar.copy(hT[:, :], pA[:, :]).then_inc(hT_ready, 1)
                            act.wait_ge(e_in, i + 1)
                            nc.scalar.activation(e[:, :, :], d[:, :, :], ACT.Exp).then_inc(e_ready, 1)
                            for c in range(HC):
                                act.wait_ge(gate_psum, i * HC + c + 1)
                                if c >= 2:
                                    act.wait_ge(hid_ready, i * HC + c - 1)
                                nc.scalar.activation(sg[:, c % 2, :], pg[:, c % 2, :], ACT.Silu).then_inc(silu_ready, 1)

                    @block.vector
                    def _(dve):
                        dve.wait_ge(w_in, 144)
                        nc.vector.tensor_copy(sel[:, :, :], self32[:, :, :]).then_inc(sel_ok, 1)
                        nc.vector.memset(cw3[:, :, :, :], 0.0).then_inc(sel_ok, 1)
                        dve.wait_ge(sel_ok, 2)
                        ch = Chain(dve, chain, 22)
                        rk = bc(rank[:, None, :], G)
                        with dve.Fori(0, NB) as i:
                            ch.turn(i)
                            ch.link(nc.vector.tensor_tensor(xc[:, :, :], x[:, bass.ds(i * BT, BT), :], bc(mean[:, bass.ds(i * BT, BT), None], [P, BT, D]), ALU.subtract))
                            nc.vector.tensor_tensor(hn[:, :, :], xc[:, :, :], bc(rstd[:, bass.ds(i * BT, BT), None], [P, BT, D]), ALU.mult).then_inc(hn_ready, 1)
                            dve.wait_ge(logits, i + 1)
                            ch.link(nc.vector.tensor_reduce(m4[:, :], L, AX, ALU.max))
                            nc.vector.tensor_tensor(d[:, :, :], L, bc(m4[:, :, None], G), ALU.subtract).then_inc(e_in, 1)
                            dve.wait_ge(e_ready, i + 1)
                            ch.link(nc.vector.reduce_sum(r4[:, :], e[:, :, :], AX))
                            ch.link(nc.vector.reciprocal(m4[:, :], r4[:, :]))
                            ch.link(nc.vector.tensor_tensor(p[:, :, :], e[:, :, :], bc(m4[:, :, None], G), ALU.mult))

                            def pick(src, dst):
                                ch.link(nc.vector.tensor_reduce(m4[:, :], src[:, :, :], AX, ALU.max))
                                ch.link(nc.vector.tensor_tensor(t1[:, :, :], src[:, :, :], bc(m4[:, :, None], G), ALU.is_ge))
                                ch.link(nc.vector.tensor_tensor(t2[:, :, :], t1[:, :, :], rk, ALU.mult))
                                ch.link(nc.vector.tensor_reduce(r4[:, :], t2[:, :, :], AX, ALU.max))
                                ch.link(nc.vector.tensor_tensor(dst[:, :, :], t2[:, :, :], bc(r4[:, :, None], G), ALU.is_equal))
                            pick(p, s1)
                            ch.link(nc.vector.scalar_tensor_tensor(p2[:, :, :], s1[:, :, :], -2.0, p[:, :, :], ALU.mult, ALU.add))
                            pick(p2, d)
                            ch.link(nc.vector.tensor_tensor(t1[:, :, :], s1[:, :, :], d[:, :, :], ALU.add))
                            ch.link(nc.vector.tensor_tensor(cw[:, :, :], t1[:, :, :], p[:, :, :], ALU.mult))
                            ch.link(nc.vector.tensor_copy(cw3[:, :, 0, :], cw[:, :, :]))
                            ch.link(nc.vector.tensor_tensor(rest[:, :, :], cw[:, :, :], cw3[:, :, 0, :], ALU.subtract))
                            ch.link(nc.vector.tensor_copy(cw3[:, :, 1, :], rest[:, :, :]))
                            ch.link(nc.vector.tensor_tensor(t1[:, :, :], rest[:, :, :], cw3[:, :, 1, :], ALU.subtract))
                            nc.vector.tensor_copy(cw3[:, :, 2, :], t1[:, :, :]).then_inc(cw_ready, 1)
                            dve.wait_ge(cT_psum, i + 1)
                            nc.vector.tensor_copy(cwT[:, :], pAb[:, :]).then_inc(cwT_ready, 1)
                            for c in range(HC):
                                dve.wait_ge(up_psum, i * HC + c + 1)
                                dve.wait_ge(silu_ready, i * HC + c + 1)
                                if c < EC:
                                    nc.vector.tensor_tensor(hid[:, c % 2, :], sg[:, c % 2, :], pu[:, c % 2, :], ALU.mult).then_inc(s_hid, 1)
                                    dve.wait_ge(s_hid, i * EC + c + 1)
                                    nc.vector.tensor_tensor(act_[:, c, :], hid[:, c % 2, :], pc[:, c % 2, :], ALU.mult).then_inc(hid_ready, 1)
                                else:
                                    nc.vector.tensor_tensor(act_[:, c, :], sg[:, c % 2, :], pu[:, c % 2, :], ALU.mult).then_inc(hid_ready, 1)
                            dve.wait_ge(y_psum, i + 1)
                            xi = x[:, bass.ds(i * BT, BT), :]
                            nc.vector.scalar_tensor_tensor(xi, pY.rearrange("p (t d) -> p t d", d=D), 0.5, xi, ALU.mult, ALU.add).then_inc(x_new, 1)
                        assert ch.k == ch.per, ch.k
                        dve.wait_ge(x_new, NB)

        def windowed_weights(s):
            hf, NC = D1 // 2, len(HIDC)
            W, loads = [], []
            maskf = s.sb("maskf", [P, TB, KEYS])
            mask = s.sb("mask", [P, TB, KEYS], bf16)
            cosf, sinf = s.sb("cosf", [P, TB, 2, D1]), s.sb("sinf", [P, TB, 2, D1])
            loads += [(cosf[:, :, :, :], a["c_cos"]), (sinf[:, :, :, :], a["c_sin"]), (maskf[:, :, :], a["c_mask"])]
            for l in range(DEPTH):
                w = dict(
                    wqkv=s.sb(f"wqkv{l}", [P, 3 * INNER]), wo=s.sb(f"wo{l}", [P, INNER // P, D]),
                    w1=s.sb(f"w1_{l}", [P, 2 * HID]), w2=s.sb(f"w2_{l}", [P, NC, D]),
                    b1a=s.sb(f"b1a{l}", [P, NC]), b1g=s.sb(f"b1g{l}", [P, NC]), b2=s.sb(f"b2_{l}", [1, D]),
                    lg=s.sb(f"lg{l}", [P, 1]), lb=s.sb(f"lb{l}", [P, 1]),
                    qk=s.sb(f"qk{l}", [P, 2, D1]), qks=s.sb(f"qks{l}", [P, 2, D1]),
                    cosT=s.sb(f"cosT{l}", [P, TB, 2, D1]), sinT=s.sb(f"sinT{l}", [P, TB, 2, D1]), mask=mask)
                W.append(w)
                bcast = lambda ap, n: ap.broadcast_to([P, n])
                qs, ks = a["L1_ffn_q_scale"], a["L1_ffn_k_scale"]
                loads += [(w["wqkv"][:, :], a["L1_ffn_wqkv"][l]), (w["wo"][:, :, :], a["L1_ffn_wo"][l].rearrange("(c p) d -> p c d", p=P)),
                          (w["w1"][:, :], a["L1_ffn_w1"][l]), (w["b2"][:, :], a["L1_ffn_b2"][l:l + 1, :]),
                          (w["lg"][:, :], a["L1_ffn_ln_g"][l].rearrange("(p o) -> p o", o=1)), (w["lb"][:, :], a["L1_ffn_ln_b"][l].rearrange("(p o) -> p o", o=1)),
                          (w["qk"][:, 0, :], bcast(qs[l:l + 1, :], D1)), (w["qk"][:, 1, :], bcast(ks[l:l + 1, :], D1)),
                          (w["qks"][:, 0, 0:hf], bcast(qs[l:l + 1, hf:], hf)), (w["qks"][:, 0, hf:], bcast(qs[l:l + 1, 0:hf], hf)),
                          (w["qks"][:, 1, 0:hf], bcast(ks[l:l + 1, hf:], hf)), (w["qks"][:, 1, hf:], bcast(ks[l:l + 1, 0:hf], hf))]
                for k, (r, n) in enumerate(HIDC):
                    loads += [(w["w2"][0:n, k, :], a["L1_ffn_w2"][l, r:r + n, :]),
                              (w["b1a"][0:n, k:k + 1], a["L1_ffn_b1"][l, r:r + n].rearrange("(p o) -> p o", o=1)),
                              (w["b1g"][0:n, k:k + 1], a["L1_ffn_b1"][l, HID + r:HID + r + n].rearrange("(p o) -> p o", o=1))]
            return W, loads, (maskf, mask, cosf, sinf)

        def windowed_tables(W, n_loads, w_in, maskf, mask, cosf, sinf):
            with ExitStack() as c:
                s = Space(c)
                done = s.sem("tables")
                with nc.Block() as block:
                    @block.vector
                    def _(dve):
                        dve.wait_ge(w_in, 16 * n_loads)
                        for w in W:
                            for dst, src, sc in ((w["cosT"], cosf, w["qk"]), (w["sinT"], sinf, w["qks"])):
                                nc.vector.tensor_tensor(dst[:, :, :, :], src[:, :, :, :], bc(sc[:, None, :, :], [P, TB, 2, D1]), ALU.mult).then_inc(done, 1)
                        nc.vector.tensor_copy(mask[:, :, :], maskf[:, :, :]).then_inc(done, 1)
                        dve.wait_ge(done, 2 * DEPTH + 1)

        def layer(w, zin, zmid, zout):
            with ExitStack() as c:
                s = Space(c)
                NC, HG, HH = len(HIDC), 2, H1 // 2
                wqkv, wo, w1, w2, b1a, b1g, b2 = (w[k] for k in ("wqkv", "wo", "w1", "w2", "b1a", "b1g", "b2"))
                lg, lb, cosT, sinT, mask = (w[k] for k in ("lg", "lb", "cosT", "sinT", "mask"))
                two = range(B)
                both = lambda name, shape: [s.sb(f"{name}{b}", shape) for b in two]
                hs1, hT, sq, ra, rb = both("hs1", [P, D]), both("hT", [P, P]), both("sq", [P, 2 * INNER]), both("ra", [P, 2 * INNER]), both("rb", [P, 2 * INNER])
                ss, rn = both("ss", [P, 2 * H1]), both("rn", [P, 2 * H1])
                qT, kT = both("qT", [P, H1 // 2, P]), both("kT", [P, H1 // 2, KEYS])
                V = both("V", [P, TB + 1, H1, D1 + 1])
                grp = lambda name, shape: [s.sb(f"{name}{g_}", shape) for g_ in range(HG)]
                mx, diff, pr, pT = grp("mx", [P, HH]), grp("diff", [P, HH, KEYS]), grp("pr", [P, HH, 2 * P]), grp("pT", [P, 2 * HH, P])
                rs, on, oT = s.sb("rs", [P, HG, HH]), s.sb("on", [P, INNER]), s.sb("oT", [P, INNER // P, P])
                hs2, st, mv, rv, hn = both("hs2", [P, D]), s.sb("st", [P, 6]), s.sb("mv", [P, 2]), s.sb("rv", [P, 1]), s.sb("hn", [P, D])
                h2T, gg, uT = s.sb("h2T", [P, P]), s.sb("gg", [P, NC, P]), s.sb("uT", [P, NC, P])
                Q = s.ps("Q", [P, 3, 512])
                M = s.ps("M", [P, 512])
                A = [s.ps(f"A{g_}", [P, 2, 512]) for g_ in range(HG)]
                Sv = [A[g_][:, :, :].rearrange("p k (s n) -> p (k s) n", s=2)[:, :, 0:KEYS] for g_ in range(HG)]
                slot = lambda h: 2 * (h % 2) + (h // 2) % 2
                setup = s.sem("setup")
                hs1_in, hs2_in = [s.sem(f"hs1_in{b}") for b in two], [s.sem(f"hs2_in{b}") for b in two]
                (h1T_psum, hT_ready, qkv_psum, sq_ready, v_ready, ss_ready, norm_ready, rn_ready, ab_ready, rot_sum, rot_ready,
                 kT_psum, qT_psum, qT_ready, kT_ready, s_psum, d_ready, exp_ready, pT_psum, pTa_ready, pTb_ready, o_psum, on_ready,
                 oT_psum, oT_ready, y_psum, zmid_ready, var_ready, std_ready, hn_ready, h2T_psum, h2T_ready, up_psum,
                 gelu_ready, u_ready, y2_psum, zout_ready, chain) = (s.sem(n) for n in (
                 "h1T_psum hT_ready qkv_psum sq_ready v_ready ss_ready norm_ready rn_ready ab_ready rot_sum rot_ready "
                 "kT_psum qT_psum qT_ready kT_ready s_psum d_ready exp_ready pT_psum pTa_ready pTb_ready o_psum on_ready "
                 "oT_psum oT_ready y_psum zmid_ready var_ready std_ready hn_ready h2T_psum h2T_ready up_psum "
                 "gelu_ready u_ready y2_psum zout_ready steps").split())
                at = lambda t, b: t * B + b + 1
                atg = lambda t, b, k: HG * (t * B + b) + k + 1

                def steps(eng, body):
                    last = B * TB
                    parts = lambda i: [(n // B, n % B) if 0 <= n < last else None for n in range(i + 1, i - 5, -1)]
                    for i in range(-1, 2 * B):
                        body(*parts(i))
                    with eng.Fori(2, TB - 1) as t:
                        body((t, 1), (t, 0), (t - 1, 1), (t - 1, 0), (t - 2, 1), (t - 2, 0))
                        body((t + 1, 0), (t, 1), (t, 0), (t - 1, 1), (t - 1, 0), (t - 2, 1))
                    for i in range(last - B, last + 4):
                        body(*parts(i))

                with nc.Block() as block:
                    @block.gpsimd
                    def _(pool):
                        for b in two:
                            nc.gpsimd.memset(V[b][:, :, :, :], 1.0).then_inc(setup, 1)
                            nc.gpsimd.memset(pr[b][:, :, :], 0.0).then_inc(setup, 1)
                        pool.wait_ge(setup, 4)

                    @block.vector
                    def _(dve):
                        for b in two:
                            nc.vector.memset(kT[b][:, :, :], 0.0).then_inc(rn_ready, 1)
                            nc.vector.memset(zmid[:, b, 0, :], 0.0).then_inc(ab_ready, 1)
                        dve.wait_ge(rn_ready, 2)
                        dve.wait_ge(ab_ready, 2)
                        dve.sem_clear(rn_ready)
                        dve.sem_clear(ab_ready)

                with nc.Block() as block:
                    def shifted(sp, dst, src, b, t, sem):
                        sp.dma_start(dst[:, 0:D // 2], src[:, b, t + 1, 0:D // 2]).then_inc(sem, 16)
                        sp.dma_start(dst[1:P, D // 2:], src[0:P - 1, b, t + 1, D // 2:]).then_inc(sem, 16)
                        sp.dma_start(dst[0:1, D // 2:], src[P - 1:P, b, t, D // 2:]).then_inc(sem, 16)

                    @block.sync
                    def _(sp):
                        for b in two:
                            shifted(sp, hs1[b], zin, b, 0, hs1_in[b])

                        def step(N, X, R, Y, Z, W):
                            if Z:
                                sp.wait_ge(zmid_ready, at(*Z))
                                shifted(sp, hs2[Z[1]], zmid, Z[1], Z[0], hs2_in[Z[1]])
                            if X and not (isinstance(X[0], int) and X[0] == TB - 1):
                                sp.wait_ge(h1T_psum, at(*X))
                                shifted(sp, hs1[X[1]], zin, X[1], X[0] + 1, hs1_in[X[1]])
                        steps(sp, step)

                    @block.tensor
                    def _(pe):
                        def transpose_in(t, b):
                            pe.wait_ge(hs1_in[b], 48 * t + 48)
                            if not (isinstance(t, int) and t == 0 and b == 0):
                                pe.wait_ge(v_ready, at(t, b) - 1)
                            nc.tensor.transpose(Q[:, 2, 0:P], hs1[b][:, :], ident[:, :]).then_inc(h1T_psum, 1)

                        def project(t, b, k):
                            nc.tensor.matmul(Q[:, k, :], hT[b][:, :], wqkv[:, k * INNER:(k + 1) * INNER], start=True, stop=True).then_inc(qkv_psum, 1)

                        def transpose_qk(t, b):
                            pe.wait_ge(rot_ready, at(t, b))
                            for j, psum in ((1, kT_psum), (0, qT_psum)):
                                for k in range(H1 // 2):
                                    last = nc.tensor.transpose(Q[:, j, k * P:(k + 1) * P], ra[b][:, j * INNER + k * P:j * INNER + (k + 1) * P], ident[:, :])
                                last.then_inc(psum, 1)

                        def scores(t, b, g_):
                            if g_ == 0:
                                pe.wait_ge(v_ready, at(t, b))
                                pe.wait_ge(qT_ready, at(t, b))
                                pe.wait_ge(kT_ready, at(t, b))
                            elif not (isinstance(t, int) and t == 0 and b == 0):
                                pe.wait_ge(zmid_ready, at(t, b) - 1)
                            for k in range(2):
                                nc.tensor.matmul(Sv[g_][:, 2 * k:2 * k + 2, :], identb[:, :], bc(mask[:, bass.ds(t, 1), :], [P, 2, KEYS]), start=True, stop=False)
                            for h in range(HH * g_, HH * g_ + HH):
                                r = (h % 2) * D1
                                last = nc.tensor.matmul(Sv[g_][:, slot(h), :], qT[b][r:r + D1, h // 2, :], kT[b][r:r + D1, h // 2, :],
                                                        start=False, stop=(slot(h) % 2 == 1))
                            last.then_inc(s_psum, 1)

                        def transpose_p(t, b, g_):
                            pe.wait_ge(exp_ready, atg(t, b, g_))
                            for k in range(2 * HH):
                                last = nc.tensor.transpose(A[g_][:, k // 4, (k % 4) * P:(k % 4 + 1) * P], pr[g_][:, k // 2, (k % 2) * P:(k % 2 + 1) * P], ident[:, :])
                            last.then_inc(pT_psum, 1)

                        def values(t, b, g_, halfway=None):
                            pe.wait_ge(pTa_ready, atg(t, b, g_))
                            pe.wait_ge(pTb_ready, atg(t, b, g_))
                            for k in range(HH):
                                if halfway and k == HH // 2:
                                    transpose_ff(*halfway)
                                h = HH * g_ + k
                                O = A[g_][:, 0, k * (D1 + 1):(k + 1) * (D1 + 1)]
                                nc.tensor.matmul(O, pT[g_][:, 2 * slot(h), :], V[b][:, t, h, :], start=True, stop=False)
                                last = nc.tensor.matmul(O, pT[g_][:, 2 * slot(h) + 1, :], V[b][:, t + 1, h, :], start=False, stop=True)
                            last.then_inc(o_psum, 1)

                        def out(t, b):
                            pe.wait_ge(on_ready, atg(t, b, 1))
                            for k in range(INNER // P):
                                last = nc.tensor.transpose(A[0][:, 1, k * P:(k + 1) * P], on[:, k * P:(k + 1) * P], ident[:, :])
                            last.then_inc(oT_psum, 1)

                        def out2(t, b):
                            pe.wait_ge(oT_ready, at(t, b))
                            for k in range(INNER // P):
                                last = nc.tensor.matmul(A[1][:, 1, 0:D], oT[:, k, :], wo[:, k, :], start=(k == 0), stop=(k == INNER // P - 1))
                            last.then_inc(y_psum, 1)

                        def transpose_ff(t, b):
                            if not (isinstance(t, int) and t == 0 and b == 0):
                                pe.wait_ge(zout_ready, at(t, b) - 1)
                            pe.wait_ge(hn_ready, at(t, b))
                            nc.tensor.transpose(M[:, 0:P], hn[:, :], ident[:, :]).then_inc(h2T_psum, 1)

                        def up(t, b):
                            pe.wait_ge(h2T_ready, at(t, b))
                            for k, (r, n) in enumerate(HIDC):
                                nc.tensor.matmul(Q[0:n, 2, k * P:(k + 1) * P], w1[:, r:r + n], h2T[:, :], start=True, stop=True)
                                last = nc.tensor.matmul(M[0:n, k * P:(k + 1) * P], w1[:, HID + r:HID + r + n], h2T[:, :], start=True, stop=True)
                            last.then_inc(up_psum, 1)

                        def down(t, b):
                            for k, (r, n) in enumerate(HIDC):
                                nc.tensor.matmul(M[:, 0:D], uT[0:n, k, :], w2[0:n, k, :], start=(k == 0), stop=False)
                            nc.tensor.matmul(M[:, 0:D], ones[:, :], b2[:, :], start=False, stop=True).then_inc(y2_psum, 1)

                        def step(N, X, R, Y, Z, W):
                            if R:
                                pe.wait_ge(ab_ready, 2 * at(*R))
                                pe.wait_ge(sq_ready, 2 * at(*R))
                            if Y:
                                transpose_qk(*Y)
                            if Z:
                                out2(*Z)
                            if Y:
                                scores(*Y, 0)
                                scores(*Y, 1)
                            if X:
                                pe.wait_ge(hT_ready, at(*X))
                                project(*X, 0)
                                project(*X, 1)
                            if W:
                                pe.wait_ge(u_ready, at(*W))
                            if X:
                                project(*X, 2)
                            if W:
                                down(*W)
                            if Y:
                                transpose_p(*Y, 0)
                                transpose_p(*Y, 1)
                            if N:
                                transpose_in(*N)
                            if Y:
                                values(*Y, 0)
                            if Y:
                                values(*Y, 1, Z)
                            elif Z:
                                transpose_ff(*Z)
                            if X:
                                pe.wait_ge(v_ready, at(*X))
                            if N:
                                pe.wait_ge(hT_ready, at(*N))
                            if Z:
                                up(*Z)
                            if Y:
                                out(*Y)
                        steps(pe, step)

                    @block.scalar
                    def _(act):
                        def step(N, X, R, Y, Z, W):
                            def exp(g_):
                                act.wait_ge(d_ready, atg(*Y, g_))
                                nc.scalar.activation(pr[g_][:, :, P - WIN:], diff[g_][:, :, :], ACT.Exp).then_inc(exp_ready, 1)

                            def square(j):
                                b = X[1]
                                nc.scalar.activation(sq[b][:, j * INNER:(j + 1) * INNER], Q[:, j, :], ACT.Square).then_inc(sq_ready, 1)

                            def copy_p(g_):
                                act.wait_ge(pT_psum, atg(*Y, g_))
                                nc.scalar.copy(pT[g_][:, 0:HH, :], A[g_][:, 0, :].rearrange("p (m n) -> p m n", n=P)).then_inc(pTa_ready, 1)
                            if Y:
                                act.wait_ge(qT_psum, at(*Y))
                                nc.scalar.copy(qT[Y[1]][:, :, :], Q[:, 0, :].rearrange("p (k n) -> p k n", n=P)).then_inc(qT_ready, 1)
                            if W:
                                act.wait_ge(up_psum, at(*W))
                                for k, (r, n) in enumerate(HIDC):
                                    last = nc.scalar.activation(gg[0:n, k, :], M[0:n, k * P:(k + 1) * P], ACT.Gelu, bias=b1g[0:n, k:k + 1])
                                last.then_inc(gelu_ready, 1)
                            if Y:
                                exp(0)
                                exp(1)
                            if X:
                                t, b = X
                                act.wait_ge(qkv_psum, 3 * at(t, b))
                                nc.scalar.copy(V[b][:, t + 1, :, 0:D1], Q[:, 2, :].rearrange("p (h d) -> p h d", h=H1)).then_inc(v_ready, 1)
                            if Y:
                                copy_p(0)
                            if X:
                                square(1)
                            if Y:
                                copy_p(1)
                            if N:
                                act.wait_ge(h1T_psum, at(*N))
                                nc.scalar.copy(hT[N[1]][:, :], Q[:, 2, 0:P]).then_inc(hT_ready, 1)
                            if Z:
                                act.wait_ge(var_ready, at(*Z))
                                nc.scalar.activation(rv[:, :], rv[:, :], ACT.Sqrt).then_inc(std_ready, 1)
                            if X:
                                act.wait_ge(ab_ready, 2 * at(t, b) - 1)
                                square(0)
                            if Z:
                                act.wait_ge(h2T_psum, at(*Z))
                                nc.scalar.activation(h2T[:, :], M[:, 0:P], ACT.Identity, bias=lb[:, 0:1], scale=lg[:, 0:1]).then_inc(h2T_ready, 1)
                            if Y:
                                act.wait_ge(oT_psum, at(*Y))
                                nc.scalar.copy(oT[:, :, :], A[0][:, 1, :].rearrange("p (k n) -> p k n", n=P)).then_inc(oT_ready, 1)
                            if X:
                                act.wait_ge(ss_ready, at(t, b))
                                nc.scalar.activation(ss[b][:, :], ss[b][:, :], ACT.Sqrt).then_inc(norm_ready, 1)
                        steps(act, step)

                    @block.gpsimd
                    def _(pool):
                        def step(N, X, R, Y, Z, W):
                            if R:
                                t, b = R
                                pool.wait_ge(rn_ready, at(t, b))
                                pool.wait_ge(rot_sum, 2 * at(t, b))
                                nc.gpsimd.tensor_tensor(ra[b][:, :].rearrange("p (h d) -> p h d", d=D1), rb[b][:, :].rearrange("p (h d) -> p h d", d=D1),
                                                        bc(rn[b][:, :, None], [P, 2 * H1, D1]), ALU.mult).then_inc(rot_ready, 1)
                            if X:
                                t, b = X
                                for j in range(2):
                                    half = slice(j * INNER, (j + 1) * INNER)
                                    pool.wait_ge(ab_ready, 2 * at(t, b) - 1 + j)
                                    nc.gpsimd.tensor_tensor(rb[b][:, half], ra[b][:, half], rb[b][:, half], ALU.add).then_inc(rot_sum, 1)
                        steps(pool, step)

                    @block.vector
                    def _(dve):
                        hf = D1 // 2
                        LINKS = dict(R=1, Y=5, Z=3)

                        def step(N, X, R, Y, Z, W):
                            before = lambda u: at(*u) - 1 if u else 0 if N else B * TB
                            ch.base, ch.k = LINKS["R"] * before(R) + LINKS["Y"] * before(Y) + LINKS["Z"] * before(Z), 0
                            def soften(g_):
                                dve.wait_ge(s_psum, atg(*Y, g_))
                                ch.link(nc.vector.tensor_reduce(mx[g_][:, :], Sv[g_], AX, ALU.max))
                                nc.vector.tensor_tensor(diff[g_][:, :, :], Sv[g_], bc(mx[g_][:, :, None], [P, HH, KEYS]), ALU.subtract).then_inc(d_ready, 1)

                            def copy_p(g_):
                                dve.wait_ge(pT_psum, atg(*Y, g_))
                                nc.vector.tensor_copy(pT[g_][:, HH:, :], A[g_][:, 1, :].rearrange("p (m n) -> p m n", n=P)).then_inc(pTb_ready, 1)

                            def normalise(g_):
                                dve.wait_ge(o_psum, atg(*Y, g_))
                                O = A[g_][:, 0, 0:HH * (D1 + 1)].rearrange("p (h d) -> p h d", d=D1 + 1)
                                ch.link(nc.vector.reciprocal(rs[:, g_, :], O[:, :, D1]))
                                nc.vector.tensor_tensor(on[:, g_ * HH * D1:(g_ + 1) * HH * D1].rearrange("p (h d) -> p h d", d=D1), O[:, :, 0:D1],
                                                        bc(rs[:, g_, :, None], [P, HH, D1]), ALU.mult).then_inc(on_ready, 1)
                            def rotate(j):
                                t, b = X
                                src = Q[:, j, :].rearrange("p (h d) -> p h d", d=D1)
                                d3 = lambda buf: buf[b][:, j * INNER:(j + 1) * INNER].rearrange("p (h d) -> p h d", d=D1)
                                nc.vector.tensor_tensor(d3(ra), src, bc(cosT[:, bass.ds(t, 1), j, :], [P, H1, D1]), ALU.mult)
                                for k in range(2):
                                    last = nc.vector.tensor_tensor(d3(rb)[:, :, k * hf:(k + 1) * hf], src[:, :, (1 - k) * hf:(2 - k) * hf],
                                                                   bc(sinT[:, bass.ds(t, 1), j, k * hf:(k + 1) * hf], [P, H1, hf]), ALU.mult)
                                last.then_inc(ab_ready, 1)
                            if Y:
                                kb = kT[Y[1]]
                                ch.link(nc.vector.tensor_copy(kb[:, :, 0:WIN], kb[:, :, P:KEYS]))
                                dve.wait_ge(kT_psum, at(*Y))
                                nc.vector.tensor_copy(kb[:, :, WIN:KEYS], Q[:, 1, :].rearrange("p (k n) -> p k n", n=P)).then_inc(kT_ready, 1)
                            if Z:
                                tz, bz = Z
                                dve.wait_ge(y_psum, at(*Z))
                                nc.vector.tensor_tensor(zmid[:, bz, tz + 1, :], A[1][:, 1, 0:D], zin[:, bz, tz + 1, :], ALU.add).then_inc(zmid_ready, 1)
                            if Y:
                                soften(0)
                            if R:
                                br = R[1]
                                dve.wait_ge(norm_ready, at(*R))
                                ch.link(nc.vector.tensor_scalar_max(ss[br][:, :], ss[br][:, :], 1e-12))
                                nc.vector.reciprocal(rn[br][:, :], ss[br][:, :]).then_inc(rn_ready, 1)
                            if W:
                                tw, bw = W
                                dve.wait_ge(gelu_ready, at(*W))
                                for k, (r, n) in enumerate(HIDC):
                                    last = nc.vector.scalar_tensor_tensor(uT[0:n, k, :], Q[0:n, 2, k * P:(k + 1) * P], b1a[0:n, k:k + 1],
                                                                          gg[0:n, k, :], ALU.add, ALU.mult)
                                last.then_inc(u_ready, 1)
                            if Y:
                                soften(1)
                            if Z:
                                dve.wait_ge(hs2_in[bz], 48 * tz + 48)
                                ch.link(nc.vector.bn_stats(st[:, :], hs2[bz][:, :]))
                                nc.vector.memset(gatebuf[:, 0:1], 0.0)
                                ch.link(nc.vector.bn_aggr(mv[:, :], st[:, :]))
                                nc.vector.tensor_scalar_add(rv[:, :], mv[:, 1:2], EPS).then_inc(var_ready, 1)
                            if Y:
                                copy_p(0)
                            if X:
                                t, b = X
                                dve.wait_ge(qkv_psum, 3 * at(t, b) - 1)
                                rotate(0)
                            if Y:
                                copy_p(1)
                            if W:
                                dve.wait_ge(y2_psum, at(*W))
                                nc.vector.tensor_tensor(zout[:, bw, tw + 1, :], M[:, 0:D], zmid[:, bw, tw + 1, :], ALU.add).then_inc(zout_ready, 1)
                            if Z:
                                dve.wait_ge(std_ready, at(*Z))
                                ch.link(nc.vector.reciprocal(rv[:, :], rv[:, :]))
                                nc.vector.tensor_scalar(hn[:, :], hs2[bz][:, :], mv[:, 0:1], rv[:, :], ALU.subtract, ALU.mult).then_inc(hn_ready, 1)
                            if X:
                                dve.wait_ge(sq_ready, 2 * at(t, b) - 1)
                                rotate(1)
                            if Y:
                                normalise(0)
                                normalise(1)
                            if X:
                                dve.wait_ge(sq_ready, 2 * at(t, b))
                                nc.vector.reduce_sum(ss[b][:, :], sq[b][:, :].rearrange("p (h d) -> p h d", d=D1), AX).then_inc(ss_ready, 1)
                            links = LINKS["R"] * bool(R) + LINKS["Y"] * bool(Y) + LINKS["Z"] * bool(Z)
                            assert ch.k == links, ch.k

                        ch = Chain(dve, chain, 0)
                        steps(dve, step)

        def windowed(W):
            with ExitStack() as c:
                s = Space(c)
                z0, z1, z2 = (s.sb(n, [P, B, TB + 1, D]) for n in ("z0", "z1", "z2"))
                layernorm_stats(s, x, mean, rstd)
                zs, done = s.sem("z_set"), s.sem("x_new")
                with nc.Block() as block:
                    @block.vector
                    def _(dve):
                        nc.vector.memset(z0[:, :, 0, :], 0.0)
                        nc.vector.memset(z2[:, :, 0, :], 0.0)
                        for b in range(B):
                            v = x[:, b * TB:(b + 1) * TB, :]
                            nc.vector.tensor_tensor(z0[:, b, 1:, :], v, bc(mean[:, b * TB:(b + 1) * TB, None], [P, TB, D]), ALU.subtract).then_inc(zs, 1)
                            dve.wait_ge(zs, 2 * b + 1)
                            nc.vector.tensor_tensor(z0[:, b, 1:, :], z0[:, b, 1:, :], bc(rstd[:, b * TB:(b + 1) * TB, None], [P, TB, D]), ALU.mult).then_inc(zs, 1)
                            dve.wait_ge(zs, 2 * b + 2)
                layer(W[0], z0, z1, z2)
                layer(W[1], z2, z1, z0)
                with nc.Block() as block:
                    @block.vector
                    def _(dve):
                        for b in range(B):
                            v = x[:, b * TB:(b + 1) * TB, :]
                            nc.vector.scalar_tensor_tensor(v, z0[:, b, 1:, :], 0.5, v, ALU.mult, ALU.add).then_inc(done, 1)
                        dve.wait_ge(done, B)

        def linear():
            with ExitStack() as c:
                s = Space(c)
                two = range(B)
                both = lambda name, shape: [s.sb(f"{name}{b}", shape) for b in two]
                wqkv, wo = s.sb("wqkv", [P, 3 * D]), s.sb("wo", [P, D])
                bqkv, bo = s.sb("bqkv", [P, 3 * D]), s.sb("bo", [1, D])
                gam, bet = s.sb("gam", [P, 2 * D]), s.sb("bet", [P, 2 * D])
                headm, causal, blockm = s.sb("headm", [P, H2]), s.sb("causal", [P, P]), s.sb("blockm", [P, H2 * VA])
                xc, hn, hT = both("xc", [P, D]), both("hn", [P, D]), both("hT", [P, P])
                qk, V = both("qk", [P, 2 * D]), both("V", [P, H2, VA])
                st, mv, sd = both("st", [P, 2, 6]), both("mv", [P, 2, 2]), both("sd", [P, 2])
                xn, ga, gb, ker = both("xn", [P, 2 * D]), both("ga", [P, 2 * D]), both("gb", [P, 2 * D]), both("ker", [P, 2 * D])
                kqT, qm, Am = both("kqT", [P, 2, P]), both("qm", [P, H2, P]), both("Am", [P, H2, P])
                state, cross = both("state", [P, H2 * VA]), both("cross", [P, H2 * VA])
                den, o, oT = both("den", [P, H2]), both("o", [P, D]), both("oT", [P, P])
                R = [s.ps(f"R{b}", [P, 4, 512]) for b in two]
                w_in, setup, chain, xs = s.sem("weights"), s.sem("setup"), s.sem("steps"), s.sem("xc")
                (hn_ready, hT_psum, hT_ready, qkv_psum, var_ready, std_ready, xn_ready, scaled, shifted_, ker_ready, kqT_psum,
                 kqT_ready, qm_ready, a_psum, am_ready, o_psum, cross_psum, state_ready, on_ready, oT_psum, oT_ready,
                 y_psum, x_new) = (s.sem(n) for n in (
                 "hn_ready hT_psum hT_ready qkv_psum var_ready std_ready xn_ready scaled shifted ker_ready kqT_psum "
                 "kqT_ready qm_ready a_psum am_ready o_psum cross_psum state_ready on_ready oT_psum oT_ready "
                 "y_psum x_new").split())
                at = lambda t, b: t * B + b + 1
                layernorm_stats(s, x, mean, rstd)
                with nc.Block() as block:
                    @block.sync
                    def _(sp):
                        row = lambda n: a[n].rearrange("(o n) -> o n", o=1)
                        loads = [(wqkv[:, :], a["L1_attn_Wqkv"]), (wo[:, :], a["L1_attn_Wo"]), (bqkv[:, :], row("L1_attn_bqkv").broadcast_to([P, 3 * D])),
                                 (bo[:, :], row("L1_attn_bo")), (headm[:, :], a["c_headm"]), (causal[:, :], a["c_causal"]), (blockm[:, :], a["c_blockm"])]
                        for k, n in enumerate("qk"):
                            loads += [(gam[:, k * D:(k + 1) * D], row(f"L1_attn_gamma_{n}").broadcast_to([P, D])),
                                      (bet[:, k * D:(k + 1) * D], row(f"L1_attn_beta_{n}").broadcast_to([P, D]))]
                        for dst, src in loads:
                            sp.dma_start(dst, src).then_inc(w_in, 16)
                        sp.wait_ge(w_in, 16 * len(loads))

                    @block.vector
                    def _(dve):
                        for b in two:
                            nc.vector.memset(V[b][:, :, :], 1.0).then_inc(setup, 1)
                            nc.vector.memset(state[b][:, :], 0.0).then_inc(setup, 1)
                        dve.wait_ge(setup, 2 * B)

                with nc.Block() as block:
                    @block.tensor
                    def _(pe):
                        with pe.Fori(0, TB) as t:
                            for b in two:
                                pe.wait_ge(hn_ready, at(t, b))
                                nc.tensor.transpose(R[b][:, 0, 0:P], hn[b][:, :], ident[:, :]).then_inc(hT_psum, 1)
                            for b in two:
                                pe.wait_ge(hT_ready, at(t, b))
                                nc.tensor.matmul(R[b][:, 1, 0:3 * D], hT[b][:, :], wqkv[:, :], start=True, stop=True).then_inc(qkv_psum, 1)
                            for b in two:
                                pe.wait_ge(ker_ready, at(t, b))
                                for k in range(2):
                                    last = nc.tensor.transpose(R[b][:, 2, k * P:(k + 1) * P], ker[b][:, k * D:(k + 1) * D], ident[:, :])
                                last.then_inc(kqT_psum, 1)
                            for b in two:
                                pe.wait_ge(qm_ready, at(t, b))
                                for k in range(4):
                                    last = nc.tensor.matmul(R[b][:, k, :], kqT[b][:, 1, :], qm[b][:, 4 * k:4 * k + 4, :], start=True, stop=True)
                                last.then_inc(a_psum, 1)
                            for b in two:
                                pe.wait_ge(am_ready, at(t, b))
                                nc.tensor.matmul(R[b][:, 0, 0:H2 * VA], kqT[b][:, 0, :], state[b][:, :], start=True, stop=False)
                                for h in range(H2):
                                    last = nc.tensor.matmul(R[b][:, 0, h * VA:(h + 1) * VA], Am[b][:, h, :], V[b][:, h, :], start=False, stop=(h == H2 - 1))
                                last.then_inc(o_psum, 1)
                                nc.tensor.matmul(R[b][:, 1, 0:H2 * VA], ker[b][:, D:], V[b][:, :, :], start=True, stop=True).then_inc(cross_psum, 1)
                            for b in two:
                                pe.wait_ge(on_ready, at(t, b))
                                nc.tensor.transpose(R[b][:, 2, 0:P], o[b][:, :], ident[:, :]).then_inc(oT_psum, 1)
                            for b in two:
                                pe.wait_ge(oT_ready, at(t, b))
                                nc.tensor.matmul(R[b][:, 3, 0:D], oT[b][:, :], wo[:, :], start=True, stop=False)
                                nc.tensor.matmul(R[b][:, 3, 0:D], ones[:, :], bo[:, :], start=False, stop=True).then_inc(y_psum, 1)

                    @block.scalar
                    def _(act):
                        with act.Fori(0, TB) as t:
                            for b in two:
                                act.wait_ge(hT_psum, at(t, b))
                                nc.scalar.copy(hT[b][:, :], R[b][:, 0, 0:P]).then_inc(hT_ready, 1)
                            for b in two:
                                act.wait_ge(var_ready, at(t, b))
                                nc.scalar.activation(sd[b][:, :], mv[b][:, :, 1], ACT.Sqrt, scale=D / (D - 1)).then_inc(std_ready, 1)
                            for b in two:
                                act.wait_ge(shifted_, at(t, b))
                                nc.scalar.activation(ker[b][:, :], gb[b][:, :], ACT.Square).then_inc(ker_ready, 1)
                            for b in two:
                                act.wait_ge(kqT_psum, at(t, b))
                                nc.scalar.copy(kqT[b][:, :, :], R[b][:, 2, 0:2 * P].rearrange("p (k n) -> p k n", k=2)).then_inc(kqT_ready, 1)
                            for b in two:
                                act.wait_ge(oT_psum, at(t, b))
                                nc.scalar.copy(oT[b][:, :], R[b][:, 2, 0:P]).then_inc(oT_ready, 1)

                    @block.gpsimd
                    def _(pool):
                        with pool.Fori(0, TB) as t:
                            for b in two:
                                pool.wait_ge(xn_ready, at(t, b))
                                nc.gpsimd.tensor_tensor(ga[b][:, :], xn[b][:, :], gam[:, :], ALU.mult).then_inc(scaled, 1)
                                pool.wait_ge(scaled, at(t, b))
                                nc.gpsimd.tensor_tensor(gb[b][:, :], ga[b][:, :], bet[:, :], ALU.add).then_inc(shifted_, 1)

                    @block.vector
                    def _(dve):
                        ch = Chain(dve, chain, 18)
                        gate = lambda: nc.vector.memset(gatebuf[:, :], 0.0)
                        with dve.Fori(0, TB) as t:
                            ch.turn(t)
                            for b in two:
                                xt = x[:, bass.ds(t + b * TB, 1), :]
                                ch.link(nc.vector.tensor_tensor(xc[b][:, :], xt, bc(mean[:, bass.ds(t + b * TB, 1)], [P, D]), ALU.subtract))
                                nc.vector.tensor_tensor(hn[b][:, :], xc[b][:, :], bc(rstd[:, bass.ds(t + b * TB, 1)], [P, D]), ALU.mult).then_inc(hn_ready, 1)
                            for b in two:
                                dve.wait_ge(qkv_psum, at(t, b))
                                qkv = R[b][:, 1, 0:3 * D]
                                nc.vector.tensor_tensor(V[b][:, :, 0:D2], qkv[:, 2 * D:].rearrange("p (h d) -> p h d", d=D2),
                                                        bqkv[:, 2 * D:].rearrange("p (h d) -> p h d", d=D2), ALU.add)
                                ch.link(nc.vector.tensor_tensor(qk[b][:, :], qkv[:, 0:2 * D], bqkv[:, 0:2 * D], ALU.add))
                                for k in range(2):
                                    if k == 0:
                                        last = nc.vector.bn_stats(st[b][:, k, :], qk[b][:, k * D:(k + 1) * D])
                                    else:
                                        ch.link(nc.vector.bn_stats(st[b][:, k, :], qk[b][:, k * D:(k + 1) * D]))
                                gate()
                                for k in range(2):
                                    last = nc.vector.bn_aggr(mv[b][:, k, :], st[b][:, k, :])
                                last.then_inc(var_ready, 1)
                            for b in two:
                                dve.wait_ge(std_ready, at(t, b))
                                ch.link(nc.vector.tensor_scalar_add(sd[b][:, :], sd[b][:, :], 1e-6))
                                ch.link(nc.vector.reciprocal(sd[b][:, :], sd[b][:, :]))
                                for k in range(2):
                                    last = nc.vector.tensor_scalar(xn[b][:, k * D:(k + 1) * D], qk[b][:, k * D:(k + 1) * D], mv[b][:, k, 0:1], sd[b][:, k:k + 1],
                                                                   ALU.subtract, ALU.mult)
                                last.then_inc(xn_ready, 1)
                            for b in two:
                                dve.wait_ge(kqT_ready, at(t, b))
                                nc.vector.tensor_tensor(qm[b][:, :, :], bc(kqT[b][:, 0:1, :], [P, H2, P]), bc(headm[:, :, None], [P, H2, P]), ALU.mult).then_inc(qm_ready, 1)
                            for b in two:
                                dve.wait_ge(a_psum, at(t, b))
                                nc.vector.tensor_tensor(Am[b][:, :, :], R[b][:, :, :].rearrange("p k (h n) -> p (k h) n", n=P),
                                                        bc(causal[:, None, :], [P, H2, P]), ALU.mult).then_inc(am_ready, 1)
                            for b in two:
                                dve.wait_ge(o_psum, at(t, b))
                                O = R[b][:, 0, 0:H2 * VA].rearrange("p (h d) -> p h d", d=VA)
                                ch.link(nc.vector.tensor_scalar_add(den[b][:, :], O[:, :, D2], 1e-6))
                                ch.link(nc.vector.reciprocal(den[b][:, :], den[b][:, :]))
                                nc.vector.tensor_tensor(o[b][:, :].rearrange("p (h d) -> p h d", d=D2), O[:, :, 0:D2], bc(den[b][:, :, None], [P, H2, D2]), ALU.mult).then_inc(on_ready, 1)
                            for b in two:
                                dve.wait_ge(cross_psum, at(t, b))
                                ch.link(nc.vector.tensor_tensor(cross[b][:, :], R[b][:, 1, 0:H2 * VA], blockm[:, :], ALU.mult))
                                ch.link(nc.vector.tensor_tensor(state[b][:, :], state[b][:, :], cross[b][:, :], ALU.add))
                            for b in two:
                                dve.wait_ge(y_psum, at(t, b))
                                xt = x[:, bass.ds(t + b * TB, 1), :]
                                nc.vector.tensor_tensor(xt, R[b][:, 3, 0:D], xt, ALU.add).then_inc(x_new, 1)
                        assert ch.k == ch.per, ch.k
                        dve.wait_ge(x_new, NT)

        def attention():
            with ExitStack() as c:
                s = Space(c)
                hT = s.sb("hT", [P, NT * P])
                cosq, sinq, cosk, sink = (s.sb(n, [P, S]) for n in ("cosq", "sinq", "cosk", "sink"))
                dist = s.sb("dist", [P, BIASW])
                slope, amp, sgn = s.sb("slope", [P, H0]), s.sb("amp", [P, H0]), s.sb("sgn", [P, 2])
                O_all = s.sb("O_all", [P, NT, H0 * D0])
                prepare(s, hT, cosq, sinq, cosk, sink, dist, slope, amp, sgn)
                heads(hT, cosq, sinq, cosk, sink, dist, slope, amp, O_all)
                project(O_all)

        def prepare(s, hT, cosq, sinq, cosk, sink, dist, slope, amp, sgn):
            layernorm_stats(s, x, mean, rstd)
            with ExitStack() as c:
                s = Space(c)
                xc, hn = s.sb("xc", [P, NT, D]), s.sb("hn", [P, NT, D])
                freq, ang, turns, r, over = s.sb("freq", [P, 1]), s.sb("ang", [P, S]), s.sb("turns", [P, S]), s.sb("r", [P, S]), s.sb("over", [P, S])
                T4 = [s.ps(f"T{k}", [P, 512]) for k in range(4)]
                w_in, iotas, hn_ready, hT_psum, chain, r_ready, sin_ready = (s.sem(n) for n in ("weights", "iotas", "hn_ready", "hT_psum", "chain", "r_ready", "sin_ready"))
                hT_ready = s.sem("hT_ready")
                PI = 3.1415925
                TWO_PI = 6.283185307179586
                MAGIC = 12582912.0
                C1 = 6.28125
                C2 = 1014 / 2 ** 19
                C3 = TWO_PI - C1 - C2
                with nc.Block() as block:
                    @block.sync
                    def _(sp):
                        nf = D0 // 2
                        for k in range(P // nf):
                            sp.dma_start(freq[k * nf:(k + 1) * nf, :], a["L0_attn_rope_freqs"].rearrange("(p o) -> p o", o=1)).then_inc(w_in, 16)
                        sp.dma_start(slope[:, :], a["L0_attn_bias_a"].rearrange("h a b -> (a b) h").broadcast_to([P, H0])).then_inc(w_in, 16)
                        sp.dma_start(amp[:, :], a["L0_attn_bias_p"].rearrange("h a b -> (a b) h").broadcast_to([P, H0])).then_inc(w_in, 16)
                        sp.dma_start(sgn[:, :], a["c_sgn"]).then_inc(w_in, 16)
                        sp.wait_ge(w_in, 16 * 7)

                    @block.gpsimd
                    def _(pool):
                        nc.gpsimd.iota(ang[:, :], pattern=[[1, S]], base=0, channel_multiplier=0, allow_small_or_imprecise_dtypes=True).then_inc(iotas, 1)
                        nc.gpsimd.iota(dist[:, :], pattern=[[1, BIASW]], base=P - S, channel_multiplier=-1, allow_small_or_imprecise_dtypes=True).then_inc(iotas, 1)
                        pool.wait_ge(iotas, 2)

                    @block.tensor
                    def _(pe):
                        for t in range(NT):
                            if t % 4 == 0:
                                pe.wait_ge(hn_ready, t // 4 + 1)
                            last = nc.tensor.transpose(T4[t // 4][:, (t % 4) * P:(t % 4 + 1) * P], hn[:, t, :], ident[:, :])
                            if t % 4 == 3:
                                last.then_inc(hT_psum, 1)

                    @block.scalar
                    def _(act):
                        for k in range(4):
                            act.wait_ge(hT_psum, k + 1)
                            nc.scalar.copy(hT[:, k * 512:(k + 1) * 512], T4[k][:, :]).then_inc(hT_ready, 1)
                        act.wait_ge(r_ready, 1)
                        nc.scalar.activation(sink[:, :], r[:, :], ACT.Sin).then_inc(sin_ready, 1)
                        act.wait_ge(r_ready, 2)
                        nc.scalar.activation(cosk[:, :], over[:, :], ACT.Sin).then_inc(sin_ready, 1)
                        act.wait_ge(hT_ready, 4)
                        act.wait_ge(sin_ready, 2)

                    @block.vector
                    def _(dve):
                        ch = Chain(dve, chain, 0)
                        for k in range(4):
                            sl = slice(4 * k, 4 * k + 4)
                            ch.link(nc.vector.tensor_tensor(xc[:, sl, :], x[:, sl, :], bc(mean[:, sl, None], [P, 4, D]), ALU.subtract))
                            nc.vector.tensor_tensor(hn[:, sl, :], xc[:, sl, :], bc(rstd[:, sl, None], [P, 4, D]), ALU.mult).then_inc(hn_ready, 1)
                        dve.wait_ge(w_in, 16 * 7)
                        dve.wait_ge(iotas, 2)
                        ch.link(nc.vector.scalar_tensor_tensor(dist[:, :], dist[:, :], -1.0, dist[:, :], ALU.mult, ALU.max))
                        ch.link(nc.vector.tensor_scalar_max(slope[:, :], slope[:, :], 0.01))
                        ch.link(nc.vector.tensor_scalar_max(amp[:, :], amp[:, :], 0.01))
                        ch.link(nc.vector.tensor_scalar(ang[:, :], ang[:, :], freq[:, :], None, ALU.mult))
                        ch.link(nc.vector.tensor_scalar(turns[:, :], ang[:, :], 1 / TWO_PI, MAGIC, ALU.mult, ALU.add))
                        ch.link(nc.vector.tensor_scalar(turns[:, :], turns[:, :], MAGIC, None, ALU.subtract))
                        ch.link(nc.vector.scalar_tensor_tensor(r[:, :], turns[:, :], -C1, ang[:, :], ALU.mult, ALU.add))
                        ch.link(nc.vector.scalar_tensor_tensor(r[:, :], turns[:, :], -C2, r[:, :], ALU.mult, ALU.add))
                        ch.link(nc.vector.scalar_tensor_tensor(r[:, :], turns[:, :], -C3, r[:, :], ALU.mult, ALU.add))

                        def wrap(v, tmp):
                            ch.link(nc.vector.tensor_scalar(tmp[:, :], v[:, :], PI, -TWO_PI, ALU.is_gt, ALU.mult))
                            ch.link(nc.vector.tensor_tensor(v[:, :], v[:, :], tmp[:, :], ALU.add))
                            ch.link(nc.vector.tensor_scalar(tmp[:, :], v[:, :], -PI, TWO_PI, ALU.is_lt, ALU.mult))
                            ch.link(nc.vector.tensor_tensor(v[:, :], v[:, :], tmp[:, :], ALU.add))
                            return nc.vector.tensor_scalar(v[:, :], v[:, :], PI, -PI, ALU.min, ALU.max)
                        wrap(r, turns).then_inc(r_ready, 1)
                        dve.wait_ge(r_ready, 1)
                        ch.link(nc.vector.tensor_scalar_add(over[:, :], r[:, :], TWO_PI / 4))
                        wrap(over, turns).then_inc(r_ready, 1)
                        dve.wait_ge(sin_ready, 2)
                        nc.vector.tensor_scalar(sinq[:, :], sink[:, :], sgn[:, 1:2], None, ALU.mult)
                        ch.link(nc.vector.tensor_scalar(cosq[:, :], cosk[:, :], -1.0 / D0 ** 0.5, None, ALU.mult))
                        ch.link(nc.vector.tensor_scalar(sink[:, :], sink[:, :], sgn[:, 0:1], None, ALU.mult))

        def heads(hT, cosq, sinq, cosk, sink, dist, slope, amp, O_all):
            with ExitStack() as c:
                s = Space(c)
                w = s.sb("w", [P, 5, P])
                ab = s.sb("ab", [P, 4])
                qT, kT = s.sb("qT", [P, NT * P]), s.sb("kT", [P, NT * P])
                m1, m2 = s.sb("m1", [P, 2, 512]), s.sb("m2", [P, 2, 512])
                V = s.sb("V", [P, NT, 2, D0 + 1])
                bias = s.sb("bias", [P, 2, BIASW])
                y, pr, pT = s.sb("y", [P, 2, S]), s.sb("pr", [P, 2, S]), s.sb("pT", [P, 2, TB, P])
                U = 2 * NT
                low, rz = s.sb("low", [P, U]), s.sb("rz", [P, 2])
                Sp = [s.ps(f"S{k}", [P, S]) for k in range(2)]
                Tp = s.ps("Tp", [P, 2, 512])
                Op = [s.ps(f"O{k}", [P, 512]) for k in range(2)]
                (w_in, setup, ab_ready, ln_ready, bias_ready, proj_psum, m_ready, rot_ready, v_psum, v_ready, s_psum, y_ready, exp_ready,
                 ta_psum, tb_psum, ta_ready, tb_ready, o_psum, r_ready, o_ready) = (s.sem(n) for n in (
                 "weights setup ab_ready ln_ready bias_ready proj_psum m_ready rot_ready v_psum v_ready s_psum y_ready exp_ready "
                 "ta_psum tb_psum ta_ready tb_ready o_psum r_ready o_ready").split())
                LAST = U + 3
                tile, head, batch = (lambda v: v // 2), (lambda v: v % 2), (lambda v: v // 2 // TB)

                with nc.Block() as block:
                    @block.vector
                    def _(dve):
                        nc.vector.memset(V[:, :, :, :], 1.0).then_inc(setup, 1)
                        dve.wait_ge(setup, 1)

                with nc.Block() as block:
                    @block.sync
                    def _(sp):
                        wsrc = a["L0_attn_w5"]
                        sp.dma_start(w[:, :, :], wsrc[0]).then_inc(w_in, 16)
                        with sp.Fori(0, PAIRS - 1) as i:
                            sp.wait_ge(v_psum, 4 * i + 4)
                            sp.dma_start(w[:, :, :], wsrc[bass.ds(i + 1, 1)].rearrange("o p k n -> p (o k) n")).then_inc(w_in, 16)

                    @block.tensor
                    def _(pe):
                        with pe.Fori(0, PAIRS) as i:
                            pe.wait_ge(w_in, 16 * i + 16)
                            for j in range(8):
                                if j >= 2:
                                    pe.wait_ge(m_ready, 8 * i + j - 1)
                                for k in range(2):
                                    last = nc.tensor.matmul(Sp[j % 2][:, k * 512:(k + 1) * 512], w[:, 2 * (j % 2) + k, :],
                                                            hT[:, (j // 2) * 512:(j // 2 + 1) * 512], start=True, stop=True)
                                last.then_inc(proj_psum, 1)
                            for k in range(4):
                                if k >= 2:
                                    pe.wait_ge(v_ready, 4 * i + k - 1)
                                for t in range(4):
                                    last = nc.tensor.matmul(Tp[:, k % 2, t * P:(t + 1) * P], hT[:, (4 * k + t) * P:(4 * k + t + 1) * P], w[:, 4, :],
                                                            start=True, stop=True)
                                last.then_inc(v_psum, 1)
                            pe.wait_ge(rot_ready, 8 * i + 8)
                            pe.wait_ge(v_ready, 4 * i + 4)
                            for n in range(LAST):
                                v = n
                                if v < U:
                                    if v >= 2:
                                        pe.wait_ge(y_ready, U * i + v - 1)
                                    r = head(v) * D0
                                    for k in range(2):
                                        last = nc.tensor.matmul(Sp[v % 2][:, k * 512:(k + 1) * 512], qT[r:r + D0, tile(v) * P:(tile(v) + 1) * P],
                                                                kT[r:r + D0, batch(v) * S + k * 512:batch(v) * S + (k + 1) * 512], start=True, stop=True)
                                    last.then_inc(s_psum, 1)
                                v = n - 2
                                if 0 <= v < U:
                                    pe.wait_ge(exp_ready, U * i + v + 1)
                                    for k in range(TB):
                                        if v >= 1 and k == 0:
                                            pe.wait_ge(ta_ready, U * i + v)
                                        if v >= 1 and k == 4:
                                            pe.wait_ge(tb_ready, U * i + v)
                                        last = nc.tensor.transpose(Tp[:, k // 4, (k % 4) * P:(k % 4 + 1) * P], pr[:, v % 2, k * P:(k + 1) * P], ident[:, :])
                                        if k == 3:
                                            last.then_inc(ta_psum, 1)
                                    last.then_inc(tb_psum, 1)
                                v = n - 3
                                if 0 <= v < U:
                                    if v >= 2:
                                        pe.wait_ge(o_ready, U * i + v - 1)
                                    pe.wait_ge(ta_ready, U * i + v + 1)
                                    pe.wait_ge(tb_ready, U * i + v + 1)
                                    for k in range(TB):
                                        last = nc.tensor.matmul(Op[v % 2][:, 0:D0 + 1], pT[:, v % 2, k, :], V[:, batch(v) * TB + k, head(v), :],
                                                                start=(k == 0), stop=(k == TB - 1))
                                    last.then_inc(o_psum, 1)

                    @block.scalar
                    def _(act):
                        with act.Fori(0, PAIRS) as i:
                            act.wait_ge(ab_ready, i + 1)
                            for h in range(2):
                                nc.scalar.activation(bias[:, h, :], dist[:, :], ACT.Ln, bias=1.0, scale=ab[:, h:h + 1]).then_inc(ln_ready, 1)
                            for k in range(4):
                                act.wait_ge(v_psum, 4 * i + k + 1)
                                nc.scalar.copy(V[:, 4 * k:4 * k + 4, :, 0:D0], Tp[:, k % 2, :].rearrange("p (t h d) -> p t h d", t=4, h=2)).then_inc(v_ready, 1)
                            for n in range(LAST):
                                v = n - 2
                                if 0 <= v < U:
                                    act.wait_ge(tb_psum, U * i + v + 1)
                                    nc.scalar.copy(pT[:, v % 2, 4:, :], Tp[:, 1, :].rearrange("p (k n) -> p k n", n=P)).then_inc(tb_ready, 1)
                                v = n
                                if v < U:
                                    act.wait_ge(y_ready, U * i + v + 1)
                                    if v >= 2:
                                        act.wait_ge(tb_psum, U * i + v - 1)
                                    nc.scalar.activation(pr[:, v % 2, :], y[:, v % 2, :], ACT.Exp, bias=low[:, v:v + 1], scale=-1.0).then_inc(exp_ready, 1)

                    @block.gpsimd
                    def _(pool):
                        with pool.Fori(0, PAIRS) as i:
                            for j in range(8):
                                pool.wait_ge(m_ready, 8 * i + j + 1)
                                dst = (qT, kT)[j % 2]
                                nc.gpsimd.tensor_tensor(dst[:, (j // 2) * 512:(j // 2 + 1) * 512], m1[:, j % 2, :], m2[:, j % 2, :], ALU.add).then_inc(rot_ready, 1)

                    @block.vector
                    def _(dve):
                        with dve.Fori(0, PAIRS) as i:
                            nc.vector.tensor_copy(ab[:, 0:2], slope[:, bass.ds(2 * i, 2)])
                            nc.vector.tensor_copy(ab[:, 2:4], amp[:, bass.ds(2 * i, 2)]).then_inc(ab_ready, 1)
                            for j in range(8):
                                cs, sn = ((cosq, sinq), (cosk, sink))[j % 2]
                                pos = slice((j // 2 % 2) * 512, (j // 2 % 2 + 1) * 512)
                                if j >= 2:
                                    dve.wait_ge(rot_ready, 8 * i + j - 1)
                                dve.wait_ge(proj_psum, 8 * i + j + 1)
                                nc.vector.tensor_tensor(m1[:, j % 2, :], Sp[j % 2][:, 0:512], cs[:, pos], ALU.mult)
                                nc.vector.tensor_tensor(m2[:, j % 2, :], Sp[j % 2][:, 512:], sn[:, pos], ALU.mult).then_inc(m_ready, 1)
                            dve.wait_ge(ln_ready, 2 * i + 2)
                            dve.wait_ge(ab_ready, i + 1)
                            for h in range(2):
                                nc.vector.tensor_scalar(bias[:, h, :], bias[:, h, :], ab[:, 2 + h:3 + h], None, ALU.mult).then_inc(bias_ready, 1)
                            dve.wait_ge(bias_ready, 2 * i + 2)
                            for n in range(LAST):
                                v = n
                                if v < U:
                                    dve.wait_ge(s_psum, U * i + v + 1)
                                    if v >= 2:
                                        dve.wait_ge(exp_ready, U * i + v - 1)
                                    nc.vector.memset(gatebuf[:, v % 4:v % 4 + 1], 0.0)
                                    off = S - P - (tile(v) % TB) * P
                                    nc.vector.tensor_tensor_reduce(out=y[:, v % 2, :], in0=Sp[v % 2][:, :], in1=bias[:, head(v), off:off + S], scale=1.0, scalar=3e38,
                                                                   op0=ALU.add, op1=ALU.min, accum_out=low[:, v:v + 1]).then_inc(y_ready, 1)
                                v = n - 2
                                if 0 <= v < U:
                                    dve.wait_ge(ta_psum, U * i + v + 1)
                                    nc.vector.tensor_copy(pT[:, v % 2, 0:4, :], Tp[:, 0, :].rearrange("p (k n) -> p k n", n=P)).then_inc(ta_ready, 1)
                                v = n - 3
                                if 0 <= v < U:
                                    dve.wait_ge(o_psum, U * i + v + 1)
                                    nc.vector.reciprocal(rz[:, v % 2:v % 2 + 1], Op[v % 2][:, D0:D0 + 1]).then_inc(r_ready, 1)
                                    dve.wait_ge(r_ready, U * i + v + 1)
                                    nc.vector.tensor_scalar(O_all[:, tile(v), bass.ds(2 * D0 * i + head(v) * D0, D0)], Op[v % 2][:, 0:D0],
                                                            rz[:, v % 2:v % 2 + 1], None, ALU.mult).then_inc(o_ready, 1)

        def project(O_all):
            with ExitStack() as c:
                s = Space(c)
                KC = H0 * D0 // P
                wo = s.sb("wo", [P, KC, D])
                stage, oT = s.sb("stage", [P, 2, H0 * D0]), s.sb("oT", [P, 2, KC, P])
                Tp = [s.ps(f"T{k}", [P, 2, 512]) for k in range(2)]
                Y = [s.ps(f"Y{k}", [P, 512]) for k in range(2)]
                w_in, staged, t_psum, oT_ready, y_psum, x_new = (s.sem(n) for n in ("weights", "staged", "t_psum", "oT_ready", "y_psum", "x_new"))
                with nc.Block() as block:
                    @block.sync
                    def _(sp):
                        sp.dma_start(wo[:, :, :], a["L0_attn_out_w"].rearrange("(k p) d -> p k d", p=P)).then_inc(w_in, 16)
                        sp.wait_ge(w_in, 16)

                    @block.tensor
                    def _(pe):
                        pe.wait_ge(w_in, 16)
                        with pe.Fori(0, NT // 2) as i:
                            for k in range(2):
                                pe.wait_ge(staged, 2 * i + k + 1)
                                for n in range(KC):
                                    last = nc.tensor.transpose(Tp[k][:, n // 4, (n % 4) * P:(n % 4 + 1) * P], stage[:, k, n * P:(n + 1) * P], ident[:, :])
                                last.then_inc(t_psum, 1)
                            for k in range(2):
                                pe.wait_ge(oT_ready, 2 * i + k + 1)
                                for n in range(KC):
                                    last = nc.tensor.matmul(Y[k][:, 0:D], oT[:, k, n, :], wo[:, n, :], start=(n == 0), stop=(n == KC - 1))
                                last.then_inc(y_psum, 1)

                    @block.scalar
                    def _(act):
                        with act.Fori(0, NT // 2) as i:
                            for k in range(2):
                                act.wait_ge(t_psum, 2 * i + k + 1)
                                nc.scalar.copy(oT[:, k, :, :], Tp[k][:, :, :].rearrange("p a (b n) -> p (a b) n", n=P)).then_inc(oT_ready, 1)

                    @block.vector
                    def _(dve):
                        with dve.Fori(0, NT // 2) as i:
                            for k in range(2):
                                nc.vector.tensor_scalar(stage[:, k, :], O_all[:, bass.ds(2 * i + k, 1), :].rearrange("p o n -> p (o n)"), 1.0, None, ALU.mult).then_inc(staged, 1)
                            for k in range(2):
                                dve.wait_ge(y_psum, 2 * i + k + 1)
                                xt = x[:, bass.ds(2 * i + k, 1), :]
                                nc.vector.tensor_tensor(xt, Y[k][:, 0:D], xt, ALU.add).then_inc(x_new, 1)
                        dve.wait_ge(x_new, NT)

        moe()
        attention()
        W, loads, tables = windowed_weights(g)
        fetched = g.sem("windowed_weights")
        moe(loads, fetched)
        windowed_tables(W, len(loads), fetched, *tables)
        windowed(W)
        linear()
        windowed(W)
        s_out = g.sem("s_out")
        with nc.Block() as block:
            @block.sync
            def _(sp):
                sp.dma_start(out.rearrange("b (t p) d -> p (b t) d", p=P), x[:, :, :]).then_inc(s_out, 16)
                sp.wait_ge(s_out, 16)


def constants():
    import numpy as np
    c = {"c_ident": np.eye(P)}
    r, m = np.arange(P)[:, None, None], np.arange(P)[None, None, :]
    ch = np.arange(EC)[None, :, None]
    c["c_sel"] = (r % E == 2 * ch + m // F) & (r < 3 * E)
    c["c_rank"] = np.tile(E - np.arange(E), (P, 1))
    half = np.arange(0, D1, 2, dtype=np.float32)
    inv = (np.float32(1.0) / np.float32(10000.0) ** (half / np.float32(D1))).astype(np.float32)
    t = np.arange(S, dtype=np.float32)
    ang = (t[:, None] * inv[None, :]).astype(np.float32).astype(np.float64)
    base = (half + np.float32(0.4 * D1)) / np.float32(1.4 * D1)
    scale = base[None, :].astype(np.float64) ** ((t - S // 2) / (WIN // 2))[:, None].astype(np.float64)
    cos, sin = np.cos(ang), np.sin(ang)
    co = np.stack([np.tile(8.0 * cos * scale, 2), np.tile(cos / scale, 2)], 1)
    si = np.stack([np.concatenate([-8.0 * sin * scale, 8.0 * sin * scale], 1), np.concatenate([-sin / scale, sin / scale], 1)], 1)
    c["c_cos"], c["c_sin"] = (v.reshape(TB, P, 2, D1).transpose(1, 0, 2, 3) for v in (co, si))
    q, tt, j = np.arange(P)[:, None, None], np.arange(TB)[None, :, None], np.arange(KEYS)[None, None, :] - WIN
    c["c_mask"] = np.where((j > q) | (q > j + WIN) | (tt * P + j < 0), MASKED, 0.0)
    p = np.arange(P)
    first = p % D0 < D0 // 2
    c["c_sgn"] = np.stack([np.where(first, -1.0, 1.0), np.where(first, 1.0, -1.0) / D0 ** 0.5], 1)
    c["c_headm"] = p[:, None] // D2 == np.arange(H2)[None, :]
    c["c_causal"] = p[:, None] <= p[None, :]
    c["c_blockm"] = p[:, None] // D2 == np.arange(H2 * VA)[None, :] // VA
    return {k: np.ascontiguousarray(v, dtype=np.float32) for k, v in c.items()}


def kernel(**inputs):
    import numpy as _np
    import concourse.bacc as _bacc
    from concourse import mybir as _mybir
    from concourse.bass_utils import run_bass_kernel_spmd as _run

    nc = _bacc.Bacc("TRN2", target_bir_lowering=False, num_devices=1)
    arrays, args = {}, {}
    data = dict(inputs)
    w = _np.asarray(data.pop("L0_attn_qkv_w")).reshape(3, PAIRS, 2, 2, D0 // 2, D)
    q, k, v = w
    data["L0_attn_w5"] = _np.stack([m.reshape(PAIRS, P, D) for m in (q, q[:, :, ::-1], k, k[:, :, ::-1], v)], 1).transpose(0, 3, 1, 2)
    data["L0_attn_out_w"] = _np.ascontiguousarray(_np.asarray(data["L0_attn_out_w"]).T)
    data.update(constants())
    for name, v in data.items():
        v = _np.ascontiguousarray(v)
        arrays[f"in_{name}"] = v
        args[name] = nc.dram_tensor(f"in_{name}", v.shape, _mybir.dt.from_np(v.dtype), kind="ExternalInput").ap()
    out = nc.dram_tensor("out_0_dram", (B, S, D), _mybir.dt.float32, kind="ExternalOutput").ap()
    build(nc, args, out)
    r = _run(nc, [arrays], core_ids=[0])
    return r.results[0]["out_0_dram"]
```

```python
B, S, D = 2, 1024, 128
P = 128
NT = B * S // P
TB = S // P
EPS = 1e-5

E, F, FS = 16, 64, 128
HC = (E * F + FS) // P
EC = E * F // P
BT = 4
NB = NT // BT

H0, D0 = 16, 64
PAIRS = H0 // 2
BIASW = 2 * S - P

DEPTH, H1, D1, WIN = 2, 8, 64, 64
INNER = H1 * D1
KEYS = WIN + P
HID = int(D * 4 * 2 / 3)
HIDC = [(c, min(P, HID - c)) for c in range(0, HID, P)]
MASKED = -1e30

H2 = 16
D2 = D // H2
VA = D2 + 1


def build(nc, a, out):
    import numpy as np
    import concourse.bass as bass
    from concourse import mybir
    from contextlib import ExitStack

    f32, bf16 = mybir.dt.float32, mybir.dt.bfloat16
    ALU, ACT, AX = mybir.AluOpType, mybir.ActivationFunctionType, mybir.AxisListType.X
    names = [0]

    class Space:
        def __init__(self, ctx):
            self.ctx = ctx
            names[0] += 1
            self.n = names[0]
            self.sems = []
            ctx.callback(self.clear)

        def clear(self):
            if self.sems and self.n > 1:
                with nc.Block() as block:
                    @block.sync
                    def _(sp):
                        for sem in self.sems:
                            sp.sem_clear(sem)

        def sb(self, name, shape, dt=f32):
            return self.ctx.enter_context(nc.sbuf_tensor(f"{name}_{self.n}", shape, dt))

        def ps(self, name, shape, dt=f32):
            return self.ctx.enter_context(nc.psum_tensor(f"{name}_{self.n}", shape, dt))

        def sem(self, name):
            handle = self.ctx.enter_context(nc.semaphore(f"{name}_{self.n}"))
            self.sems.append(handle)
            return handle

    class Chain:
        def __init__(self, eng, sem, per):
            self.eng, self.sem, self.per, self.k, self.base = eng, sem, per, 0, 0

        def turn(self, i):
            self.base, self.k = i * self.per, 0

        def link(self, ins):
            ins.then_inc(self.sem, 1)
            self.k += 1
            self.eng.wait_ge(self.sem, self.base + self.k)

    def layernorm_stats(sp, src, dst_mean, dst_rstd, loads=(), loaded=None):
        stats, mv, tmp = sp.sb("stats", [P, NT, 6]), sp.sb("mv", [P, NT, 2]), sp.sb("tmp", [P, NT])
        c, s = sp.sem("ln_chain"), sp.sem("ln_std")
        with nc.Block() as block:
            @block.sync
            def _(sync):
                for dst, src_ in loads:
                    sync.dma_start(dst, src_).then_inc(loaded, 16)

            @block.vector
            def _(dve):
                for t in range(NT):
                    last = nc.vector.bn_stats(stats[:, t, :], src[:, t, :])
                last.then_inc(c, 1)
                dve.wait_ge(c, 1)
                for t in range(NT):
                    last = nc.vector.bn_aggr(mv[:, t, :], stats[:, t, :])
                last.then_inc(c, 1)
                dve.wait_ge(c, 2)
                nc.vector.tensor_copy(dst_mean[:, :], mv[:, :, 0])
                nc.vector.tensor_scalar_add(tmp[:, :], mv[:, :, 1], EPS).then_inc(c, 1)
                dve.wait_ge(s, 1)
                nc.vector.reciprocal(dst_rstd[:, :], tmp[:, :]).then_inc(c, 1)
                dve.wait_ge(c, 4)

            @block.scalar
            def _(act):
                act.wait_ge(c, 3)
                nc.scalar.activation(tmp[:, :], tmp[:, :], ACT.Sqrt).then_inc(s, 1)
                act.wait_ge(s, 1)

    def bc(ap, shape):
        return ap.broadcast_to(shape)

    ctx = ExitStack()
    with ctx:
        g = Space(ctx)
        x = g.sb("x", [P, NT, D])
        mean, rstd = g.sb("mean", [P, NT]), g.sb("rstd", [P, NT])
        ident, identb = g.sb("ident", [P, P]), g.sb("identb", [P, P], bf16)
        ones = g.sb("ones", [1, P])
        gatebuf = g.sb("gatebuf", [P, 4])
        xd = a["L0_attn_x"].rearrange("b (t p) d -> p (b t) d", p=P)
        s_load, s_const = g.sem("load"), g.sem("const")
        with nc.Block() as block:
            @block.sync
            def _(sp):
                sp.dma_start(x[:, :, :], xd).then_inc(s_load, 16)
                sp.dma_start(ident[:, :], a["c_ident"]).then_inc(s_load, 16)
                sp.wait_ge(s_load, 32)

            @block.vector
            def _(dve):
                nc.vector.memset(ones[:, :], 1.0).then_inc(s_const, 1)
                nc.vector.memset(gatebuf[:, :], 0.0).then_inc(s_const, 1)
                dve.wait_ge(s_load, 32)
                nc.vector.tensor_copy(identb[:, :], ident[:, :]).then_inc(s_const, 1)
                dve.wait_ge(s_const, 3)

        def moe(prefetch, fetched, beside):
            with ExitStack() as c:
                s = Space(c)
                wg, wu = s.sb("wg", [P, HC * P]), s.sb("wu", [P, HC * P])
                wd, wr = s.sb("wd", [P, HC, D]), s.sb("wr", [P, E])
                self32, sel = s.sb("self32", [P, EC, P]), s.sb("sel", [P, EC, P], bf16)
                rank = s.sb("rank", [P, E])
                hn, hT = s.sb("hn", [P, BT, D]), s.sb("hT", [P, BT * P])
                xc = s.sb("xc", [P, BT, D])
                sg, hid, act_ = s.sb("sg", [P, 2, BT * P]), s.sb("hid", [P, 2, BT * P]), s.sb("act", [P, HC, BT * P])
                G = [P, BT, E]
                d, e, p, p2, t1, t2, s1, cw, rest = (s.sb(n, G) for n in
                    ("d", "e", "p", "p2", "t1", "t2", "s1", "cw", "rest"))
                m4, r4 = s.sb("m4", [P, BT]), s.sb("r4", [P, BT])
                cw3, cwT = s.sb("cw3", [P, BT, P // E, E], bf16), s.sb("cwT", [P, BT * P], bf16)
                pA = s.ps("pA", [P, BT * P])
                pAb = s.ps("pAb", [P, BT * P], bf16)
                pg, pu, pc = (s.ps(n, [P, 2, BT * P]) for n in ("pg", "pu", "pc"))
                pY = pc[:, 1, :]
                s_hid = s.sem("half_hidden")
                w_in = s.sem("weights"); sel_ok = s.sem("sel_ok")
                hn_ready, hT_psum, hT_ready = s.sem("hn_ready"), s.sem("hT_psum"), s.sem("hT_ready")
                logits, e_in, e_ready, cw_ready, cT_psum, cwT_ready = (s.sem(n) for n in
                    ("logits", "e_in", "e_ready", "cw_ready", "cT_psum", "cwT_ready"))
                gate_psum, up_psum, silu_ready, hid_ready = (s.sem(n) for n in ("gate_psum", "up_psum", "silu_ready", "hid_ready"))
                y_psum, x_new, chain = s.sem("y_psum"), s.sem("x_new"), s.sem("chain")
                loads = [(wr[:, :], a["L0_ffn_Wr"]), (self32[:, :, :], a["c_sel"]), (rank[:, :], a["c_rank"]),
                         (wg[:, 0:E * F].rearrange("p (e f) -> p e f", e=E), a["L0_ffn_Wg"].rearrange("e d f -> d e f")),
                         (wu[:, 0:E * F].rearrange("p (e f) -> p e f", e=E), a["L0_ffn_Wu"].rearrange("e d f -> d e f")),
                         (wg[:, E * F:], a["L0_ffn_Sg"]), (wu[:, E * F:], a["L0_ffn_Su"]),
                         (wd[:, 0:EC, :], a["L0_ffn_Wd"].rearrange("(c two) f d -> (two f) c d", two=2)), (wd[:, EC, :], a["L0_ffn_Sd"])]
                router_in = s.sem("router_in")
                layernorm_stats(s, x, mean, rstd, loads[:3], router_in)
                L = pA[:, 0:BT * E].rearrange("p (t e) -> p t e", e=E)

                with nc.Block() as block:
                    @block.sync
                    def _(sp):
                        for dst, src in loads[3:]:
                            sp.dma_start(dst, src).then_inc(w_in, 16)
                        for dst, src in prefetch:
                            sp.dma_start(dst, src).then_inc(fetched, 16)
                        sp.wait_ge(w_in, 16 * 6)

                    @block.gpsimd
                    def _(pool):
                        beside(pool)

                    def blocks(eng, body):
                        body(0, True)
                        with eng.Fori(1, NB - 1) as i:
                            body(i, True)
                        body(NB - 1, False)

                    @block.tensor
                    def _(pe):
                        def front(i):
                            pe.wait_ge(hn_ready, i + 1)
                            for j in range(BT):
                                last = nc.tensor.transpose(pA[:, j * P:(j + 1) * P], hn[:, j, :], ident[:, :])
                            last.then_inc(hT_psum, 1)
                            if isinstance(i, int) and i == 0:
                                pe.wait_ge(router_in, 16 * 3)
                            pe.wait_ge(hT_ready, i + 1)
                            for j in range(BT):
                                last = nc.tensor.matmul(L[:, j, :], hT[:, j * P:(j + 1) * P], wr[:, :], start=True, stop=True)
                            last.then_inc(logits, 1)

                        def weights(i):
                            pe.wait_ge(cw_ready, i + 1)
                            for j in range(BT):
                                last = nc.tensor.transpose(pAb[:, j * P:(j + 1) * P],
                                                           cw3[:, j, :, :].rearrange("p a b -> p (a b)"), identb[:, :])
                            last.then_inc(cT_psum, 1)

                        def up(i):
                            for c in range(HC):
                                if c >= 2:
                                    pe.wait_ge(silu_ready, i * HC + c - 1)
                                nc.tensor.matmul(pg[:, c % 2, :], wg[:, c * P:(c + 1) * P], hT[:, :], start=True, stop=True).then_inc(gate_psum, 1)
                                if c >= 2:
                                    pe.wait_ge(hid_ready, i * HC + c - 1)
                                last = nc.tensor.matmul(pu[:, c % 2, :], wu[:, c * P:(c + 1) * P], hT[:, :], start=True, stop=True)
                                if c < EC:
                                    if c == 0:
                                        pe.wait_ge(cwT_ready, i + 1)
                                    if c == 1 and not (isinstance(i, int) and i == 0):
                                        pe.wait_ge(x_new, i)
                                    last = nc.tensor.matmul(pc[:, c % 2, :], sel[:, c, :], cwT[:, :], start=True, stop=True)
                                last.then_inc(up_psum, 1)

                        def down(i):
                            pe.wait_ge(hid_ready, i * HC + HC)
                            for j in range(BT):
                                for c in range(HC):
                                    last = nc.tensor.matmul(pY[:, j * D:(j + 1) * D], act_[:, c, j * P:(j + 1) * P], wd[:, c, :],
                                                            start=(c == 0), stop=(c == HC - 1))
                            last.then_inc(y_psum, 1)

                        def body(i, more):
                            weights(i)
                            up(i)
                            if more:
                                front(i + 1)
                            down(i)

                        front(0)
                        pe.wait_ge(w_in, 16 * 6)
                        pe.wait_ge(sel_ok, 2)
                        blocks(pe, body)

                    @block.scalar
                    def _(act):
                        def front(i):
                            act.wait_ge(hT_psum, i + 1)
                            nc.scalar.copy(hT[:, :], pA[:, :]).then_inc(hT_ready, 1)
                            act.wait_ge(e_in, i + 1)
                            nc.scalar.activation(e[:, :, :], d[:, :, :], ACT.Exp).then_inc(e_ready, 1)

                        def body(i, more):
                            for c in range(HC):
                                act.wait_ge(gate_psum, i * HC + c + 1)
                                if c >= 2:
                                    act.wait_ge(hid_ready, i * HC + c - 1)
                                nc.scalar.activation(sg[:, c % 2, :], pg[:, c % 2, :], ACT.Silu).then_inc(silu_ready, 1)
                            if more:
                                front(i + 1)
                        front(0)
                        blocks(act, body)

                    @block.vector
                    def _(dve):
                        nc.vector.memset(cw3[:, :, :, :], 0.0).then_inc(sel_ok, 1)
                        ch = Chain(dve, chain, 22)
                        rk = bc(rank[:, None, :], G)

                        def normalise(i):
                            ch.turn(i)
                            ch.link(nc.vector.tensor_tensor(xc[:, :, :], x[:, bass.ds(i * BT, BT), :], bc(mean[:, bass.ds(i * BT, BT), None], [P, BT, D]), ALU.subtract))
                            nc.vector.tensor_tensor(hn[:, :, :], xc[:, :, :], bc(rstd[:, bass.ds(i * BT, BT), None], [P, BT, D]), ALU.mult).then_inc(hn_ready, 1)

                        def route(i):
                            dve.wait_ge(logits, i + 1)
                            ch.link(nc.vector.tensor_reduce(m4[:, :], L, AX, ALU.max))
                            nc.vector.tensor_tensor(d[:, :, :], L, bc(m4[:, :, None], G), ALU.subtract).then_inc(e_in, 1)
                            dve.wait_ge(e_ready, i + 1)
                            ch.link(nc.vector.reduce_sum(r4[:, :], e[:, :, :], AX))
                            ch.link(nc.vector.reciprocal(m4[:, :], r4[:, :]))
                            ch.link(nc.vector.tensor_tensor(p[:, :, :], e[:, :, :], bc(m4[:, :, None], G), ALU.mult))

                            def pick(src, dst):
                                ch.link(nc.vector.tensor_reduce(m4[:, :], src[:, :, :], AX, ALU.max))
                                ch.link(nc.vector.tensor_tensor(t1[:, :, :], src[:, :, :], bc(m4[:, :, None], G), ALU.is_ge))
                                ch.link(nc.vector.tensor_tensor(t2[:, :, :], t1[:, :, :], rk, ALU.mult))
                                ch.link(nc.vector.tensor_reduce(r4[:, :], t2[:, :, :], AX, ALU.max))
                                ch.link(nc.vector.tensor_tensor(dst[:, :, :], t2[:, :, :], bc(r4[:, :, None], G), ALU.is_equal))
                            pick(p, s1)
                            ch.link(nc.vector.scalar_tensor_tensor(p2[:, :, :], s1[:, :, :], -2.0, p[:, :, :], ALU.mult, ALU.add))
                            pick(p2, d)
                            ch.link(nc.vector.tensor_tensor(t1[:, :, :], s1[:, :, :], d[:, :, :], ALU.add))
                            ch.link(nc.vector.tensor_tensor(cw[:, :, :], t1[:, :, :], p[:, :, :], ALU.mult))
                            ch.link(nc.vector.tensor_copy(cw3[:, :, 0, :], cw[:, :, :]))
                            ch.link(nc.vector.tensor_tensor(rest[:, :, :], cw[:, :, :], cw3[:, :, 0, :], ALU.subtract))
                            ch.link(nc.vector.tensor_copy(cw3[:, :, 1, :], rest[:, :, :]))
                            ch.link(nc.vector.tensor_tensor(t1[:, :, :], rest[:, :, :], cw3[:, :, 1, :], ALU.subtract))
                            nc.vector.tensor_copy(cw3[:, :, 2, :], t1[:, :, :]).then_inc(cw_ready, 1)
                            assert ch.k == ch.per, ch.k

                        def body(i, more):
                            dve.wait_ge(cT_psum, i + 1)
                            nc.vector.tensor_copy(cwT[:, :], pAb[:, :]).then_inc(cwT_ready, 1)
                            if not (isinstance(i, int) and i == 0):
                                output(i - 1)
                            for c in range(HC):
                                dve.wait_ge(up_psum, i * HC + c + 1)
                                dve.wait_ge(silu_ready, i * HC + c + 1)
                                if c < EC:
                                    nc.vector.tensor_tensor(hid[:, c % 2, :], sg[:, c % 2, :], pu[:, c % 2, :], ALU.mult).then_inc(s_hid, 1)
                                    dve.wait_ge(s_hid, i * EC + c + 1)
                                    nc.vector.tensor_tensor(act_[:, c, :], hid[:, c % 2, :], pc[:, c % 2, :], ALU.mult).then_inc(hid_ready, 1)
                                else:
                                    nc.vector.tensor_tensor(act_[:, c, :], sg[:, c % 2, :], pu[:, c % 2, :], ALU.mult).then_inc(hid_ready, 1)
                                if more and c == HC // 2:
                                    normalise(i + 1)
                            if more:
                                route(i + 1)

                        def output(i):
                            dve.wait_ge(y_psum, i + 1)
                            xi = x[:, bass.ds(i * BT, BT), :]
                            nc.vector.scalar_tensor_tensor(xi, pY.rearrange("p (t d) -> p t d", d=D), 0.5, xi, ALU.mult, ALU.add).then_inc(x_new, 1)
                        normalise(0)
                        dve.wait_ge(sel_ok, 1)
                        dve.wait_ge(router_in, 16 * 3)
                        route(0)
                        nc.vector.tensor_copy(sel[:, :, :], self32[:, :, :]).then_inc(sel_ok, 1)
                        blocks(dve, body)
                        output(NB - 1)
                        dve.wait_ge(x_new, NB)

        def windowed_weights(s):
            hf, NC = D1 // 2, len(HIDC)
            W, loads = [], []
            maskf = s.sb("maskf", [P, TB, KEYS])
            mask = s.sb("mask", [P, TB, KEYS], bf16)
            cosf, sinf = s.sb("cosf", [P, TB, 2, D1]), s.sb("sinf", [P, TB, 2, D1])
            loads += [(cosf[:, :, :, :], a["c_cos"]), (sinf[:, :, :, :], a["c_sin"]), (maskf[:, :, :], a["c_mask"])]
            for l in range(DEPTH):
                w = dict(
                    wqkv=s.sb(f"wqkv{l}", [P, 3 * INNER]), wo=s.sb(f"wo{l}", [P, INNER // P, D]),
                    w1=s.sb(f"w1_{l}", [P, 2 * HID]), w2=s.sb(f"w2_{l}", [P, NC, D]),
                    b1a=s.sb(f"b1a{l}", [P, NC]), b1g=s.sb(f"b1g{l}", [P, NC]), b2=s.sb(f"b2_{l}", [1, D]),
                    lg=s.sb(f"lg{l}", [P, 1]), lb=s.sb(f"lb{l}", [P, 1]),
                    qk=s.sb(f"qk{l}", [P, 2, D1]), qks=s.sb(f"qks{l}", [P, 2, D1]),
                    cosT=s.sb(f"cosT{l}", [P, TB, 2, D1]), sinT=s.sb(f"sinT{l}", [P, TB, 2, D1]), mask=mask)
                W.append(w)
                bcast = lambda ap, n: ap.broadcast_to([P, n])
                qs, ks = a["L1_ffn_q_scale"], a["L1_ffn_k_scale"]
                loads += [(w["wqkv"][:, :], a["L1_ffn_wqkv"][l]), (w["wo"][:, :, :], a["L1_ffn_wo"][l].rearrange("(c p) d -> p c d", p=P)),
                          (w["w1"][:, :], a["L1_ffn_w1"][l]), (w["b2"][:, :], a["L1_ffn_b2"][l:l + 1, :]),
                          (w["lg"][:, :], a["L1_ffn_ln_g"][l].rearrange("(p o) -> p o", o=1)), (w["lb"][:, :], a["L1_ffn_ln_b"][l].rearrange("(p o) -> p o", o=1)),
                          (w["qk"][:, 0, :], bcast(qs[l:l + 1, :], D1)), (w["qk"][:, 1, :], bcast(ks[l:l + 1, :], D1)),
                          (w["qks"][:, 0, 0:hf], bcast(qs[l:l + 1, hf:], hf)), (w["qks"][:, 0, hf:], bcast(qs[l:l + 1, 0:hf], hf)),
                          (w["qks"][:, 1, 0:hf], bcast(ks[l:l + 1, hf:], hf)), (w["qks"][:, 1, hf:], bcast(ks[l:l + 1, 0:hf], hf))]
                for k, (r, n) in enumerate(HIDC):
                    loads += [(w["w2"][0:n, k, :], a["L1_ffn_w2"][l, r:r + n, :]),
                              (w["b1a"][0:n, k:k + 1], a["L1_ffn_b1"][l, r:r + n].rearrange("(p o) -> p o", o=1)),
                              (w["b1g"][0:n, k:k + 1], a["L1_ffn_b1"][l, HID + r:HID + r + n].rearrange("(p o) -> p o", o=1))]
            return W, loads, (maskf, mask, cosf, sinf)

        def windowed_tables(pool, s, W, n_loads, fetched, maskf, mask, cosf, sinf):
            done = s.sem("tables")
            pool.wait_ge(fetched, 16 * n_loads)
            for w in W:
                for dst, src, sc in ((w["cosT"], cosf, w["qk"]), (w["sinT"], sinf, w["qks"])):
                    nc.gpsimd.tensor_tensor(dst[:, :, :, :], src[:, :, :, :], bc(sc[:, None, :, :], [P, TB, 2, D1]), ALU.mult).then_inc(done, 1)
            nc.gpsimd.tensor_copy(mask[:, :, :], maskf[:, :, :]).then_inc(done, 1)
            pool.wait_ge(done, 2 * DEPTH + 1)

        def layers(LW, z0, z1, z2):
            with ExitStack() as c:
                s = Space(c)
                NC, HG, HH = len(HIDC), 2, H1 // 2
                mask = LW[0]["mask"]
                zin, zmid, zout = (z0, z2), (z1, z1), (z2, z0)
                two = range(B)
                both = lambda name, shape: [s.sb(f"{name}{b}", shape) for b in two]
                hs1, hT, sq, ra, rb = both("hs1", [P, D]), both("hT", [P, P]), both("sq", [P, 2 * INNER]), both("ra", [P, 2 * INNER]), both("rb", [P, 2 * INNER])
                ss, rn = both("ss", [P, 2 * H1]), both("rn", [P, 2 * H1])
                qT, kT = both("qT", [P, H1 // 2, P]), both("kT", [P, H1 // 2, KEYS])
                V = both("V", [P, TB + 1, H1, D1 + 1])
                VB = both("VB", [P, H1 // 2, 2 * (D1 + 1)])
                grp = lambda name, shape: [s.sb(f"{name}{g_}", shape) for g_ in range(HG)]
                mx, diff, pr, pT = grp("mx", [P, HH]), grp("diff", [P, HH, KEYS]), grp("pr", [P, 2, 3 * P]), grp("pT", [P, 6, P])
                rs, on, oT = s.sb("rs", [P, HG, HH]), s.sb("on", [P, INNER]), s.sb("oT", [P, INNER // P, P])
                hs2, st, mv, rv, hn = both("hs2", [P, D]), s.sb("st", [P, 6]), s.sb("mv", [P, 2]), s.sb("rv", [P, 1]), s.sb("hn", [P, D])
                h2T, gg, uT = s.sb("h2T", [P, P]), s.sb("gg", [P, NC, P]), s.sb("uT", [P, NC, P])
                Q = s.ps("Q", [P, 3, 512])
                M = s.ps("M", [P, 512])
                A = [s.ps(f"A{g_}", [P, 2, 512]) for g_ in range(HG)]
                Sv = [A[g_][:, :, :].rearrange("p k (s n) -> p (k s) n", s=2)[:, :, 0:KEYS] for g_ in range(HG)]
                slot = lambda h: 2 * (h % 2) + (h // 2) % 2
                setup = s.sem("setup")
                hs1_in, hs2_in = [s.sem(f"hs1_in{b}") for b in two], [s.sem(f"hs2_in{b}") for b in two]
                (h1T_psum, hT_ready, qkv_psum, sq_ready, v_ready, ss_ready, norm_ready, rn_ready, ab_ready, rot_sum, rot_ready,
                 kT_psum, qT_psum, qT_ready, kT_ready, s_psum, d_ready, exp_ready, pT_psum, pTa_ready, pTb_ready, o_psum, on_ready,
                 oT_psum, oT_ready, y_psum, zmid_ready, var_ready, std_ready, hn_ready, h2T_psum, h2T_ready, up_psum,
                 gelu_ready, u_ready, y2_psum, zout_ready, chain) = (s.sem(n) for n in (
                 "h1T_psum hT_ready qkv_psum sq_ready v_ready ss_ready norm_ready rn_ready ab_ready rot_sum rot_ready "
                 "kT_psum qT_psum qT_ready kT_ready s_psum d_ready exp_ready pT_psum pTa_ready pTb_ready o_psum on_ready "
                 "oT_psum oT_ready y_psum zmid_ready var_ready std_ready hn_ready h2T_psum h2T_ready up_psum "
                 "gelu_ready u_ready y2_psum zout_ready steps").split())
                at = lambda t, b, l: (l * TB + t) * B + b + 1
                atg = lambda t, b, l, k: HG * ((l * TB + t) * B + b) + k + 1

                last_unit = DEPTH * B * TB

                def steps(eng, body):
                    parts = lambda i: [(n // B % TB, n % B, n // (B * TB)) if 0 <= n < last_unit else None for n in range(i + 1, i - 6, -1)]
                    for i in range(-1, 3 * B):
                        body(*parts(i))
                    for l in range(DEPTH):
                        with eng.Fori(3, TB - 1) as t:
                            body((t, 1, l), (t, 0, l), (t - 1, 1, l), (t - 1, 0, l), (t - 2, 1, l), (t - 2, 0, l), (t - 3, 1, l))
                            body((t + 1, 0, l), (t, 1, l), (t, 0, l), (t - 1, 1, l), (t - 1, 0, l), (t - 2, 1, l), (t - 2, 0, l))
                        done = (l + 1) * B * TB
                        for i in range(done - B, min(done + 3 * B, last_unit + 5)):
                            body(*parts(i))

                with nc.Block() as block:
                    @block.gpsimd
                    def _(pool):
                        for b in two:
                            nc.gpsimd.memset(V[b][:, 0, :, 0:D1], 0.0).then_inc(setup, 1)
                            nc.gpsimd.memset(V[b][:, :, :, D1:], 1.0).then_inc(setup, 1)
                            nc.gpsimd.memset(VB[b][:, :, :], 0.0).then_inc(setup, 1)
                        pool.wait_ge(setup, 6)
                        for b in two:
                            nc.gpsimd.memset(VB[b][0:WIN, :, D1:D1 + 1], 1.0).then_inc(setup, 1)
                            nc.gpsimd.memset(VB[b][WIN:, :, 2 * D1 + 1:], 1.0).then_inc(setup, 1)
                        pool.wait_ge(setup, 10)

                    @block.vector
                    def _(dve):
                        for b in two:
                            nc.vector.memset(kT[b][:, :, :], 0.0).then_inc(rn_ready, 1)
                        dve.wait_ge(rn_ready, 2)
                        dve.sem_clear(rn_ready)

                with nc.Block() as block:
                    def shifted(sp, dst, src, b, t, sem):
                        sp.dma_start(dst[:, 0:D // 2], src[:, b, t + 1, 0:D // 2]).then_inc(sem, 16)
                        sp.dma_start(dst[1:P, D // 2:], src[0:P - 1, b, t + 1, D // 2:]).then_inc(sem, 16)
                        sp.dma_start(dst[0:1, D // 2:], src[P - 1:P, b, t, D // 2:]).then_inc(sem, 16)

                    @block.sync
                    def _(sp):
                        for b in two:
                            shifted(sp, hs1[b], zin[0], b, 0, hs1_in[b])

                        def step(N, X, R, Y, Z, H, W):
                            if Z:
                                t, b, l = Z
                                sp.wait_ge(zmid_ready, at(*Z))
                                shifted(sp, hs2[b], zmid[l], b, t, hs2_in[b])
                            if X:
                                t, b, l = X[0] + 1, X[1], X[2]
                                if isinstance(t, int) and t == TB:
                                    t, l = 0, l + 1
                                if l < DEPTH:
                                    sp.wait_ge(h1T_psum, at(*X))
                                    if l > 0:
                                        sp.wait_ge(zout_ready, at(t, b, l - 1) if isinstance(t, int) else l * TB * B)
                                    shifted(sp, hs1[b], zin[l], b, t, hs1_in[b])
                        steps(sp, step)

                    @block.tensor
                    def _(pe):
                        def transpose_in(t, b, l):
                            pe.wait_ge(hs1_in[b], 48 * (l * TB + t) + 48)
                            if not (isinstance(t, int) and t == l == b == 0):
                                pe.wait_ge(v_ready, at(t, b, l) - 1)
                            nc.tensor.transpose(Q[:, 2, 0:P], hs1[b][:, :], ident[:, :]).then_inc(h1T_psum, 1)

                        def project(t, b, l, k):
                            nc.tensor.matmul(Q[:, k, :], hT[b][:, :], LW[l]["wqkv"][:, k * INNER:(k + 1) * INNER], start=True, stop=True).then_inc(qkv_psum, 1)

                        def transpose_qk(t, b, l):
                            pe.wait_ge(rot_ready, at(t, b, l))
                            for j, psum in ((1, kT_psum), (0, qT_psum)):
                                for k in range(H1 // 2):
                                    last = nc.tensor.transpose(Q[:, j, k * P:(k + 1) * P], ra[b][:, j * INNER + k * P:j * INNER + (k + 1) * P], ident[:, :])
                                last.then_inc(psum, 1)

                        def scores(t, b, l, g_):
                            if g_ == 0:
                                pe.wait_ge(v_ready, at(t, b, l))
                                pe.wait_ge(qT_ready, at(t, b, l))
                                pe.wait_ge(kT_ready, at(t, b, l))
                            elif not (isinstance(t, int) and t == l == b == 0):
                                pe.wait_ge(zmid_ready, at(t, b, l) - 1)
                            for k in range(2):
                                nc.tensor.matmul(Sv[g_][:, 2 * k:2 * k + 2, :], identb[:, :], bc(mask[:, bass.ds(t, 1), :], [P, 2, KEYS]), start=True, stop=False)
                            for h in range(HH * g_, HH * g_ + HH):
                                r = (h % 2) * D1
                                last = nc.tensor.matmul(Sv[g_][:, slot(h), :], qT[b][r:r + D1, h // 2, :], kT[b][r:r + D1, h // 2, :],
                                                        start=False, stop=(slot(h) % 2 == 1))
                            last.then_inc(s_psum, 1)

                        def transpose_p(t, b, l, g_):
                            pe.wait_ge(exp_ready, atg(t, b, l, g_))
                            for j in range(2):
                                for k in range(2):
                                    nc.tensor.transpose(A[g_][:, j, k * P:(k + 1) * P], pr[g_][:, j, k * P:(k + 1) * P], ident[:, :])
                                last = nc.tensor.transpose(A[g_][:, j, 2 * P:3 * P], pr[g_][:, j, 2 * P:3 * P], ident[:, :])
                            last.then_inc(pT_psum, 1)

                        def values(t, b, l, g_):
                            pe.wait_ge(pTa_ready, atg(t, b, l, g_))
                            pe.wait_ge(pTb_ready, atg(t, b, l, g_))
                            for j in range(2):
                                O = A[g_][:, 0, 2 * j * (D1 + 1):2 * (j + 1) * (D1 + 1)]
                                nc.tensor.matmul(O, pT[g_][:, 3 * j + 2, :], VB[b][:, 2 * g_ + j, :], start=True, stop=False)
                                for k in range(2):
                                    last = nc.tensor.matmul(O[:, k * (D1 + 1):(k + 1) * (D1 + 1)], pT[g_][:, 3 * j + k, :],
                                                            V[b][:, t + 1, HH * g_ + 2 * k + j, :], start=False, stop=(k == 1))
                            last.then_inc(o_psum, 1)

                        def out(t, b, l):
                            pe.wait_ge(on_ready, atg(t, b, l, 1))
                            for k in range(INNER // P):
                                last = nc.tensor.transpose(A[0][:, 1, k * P:(k + 1) * P], on[:, k * P:(k + 1) * P], ident[:, :])
                            last.then_inc(oT_psum, 1)

                        def out2(t, b, l):
                            pe.wait_ge(oT_ready, at(t, b, l))
                            for k in range(INNER // P):
                                last = nc.tensor.matmul(A[1][:, 1, 0:D], oT[:, k, :], LW[l]["wo"][:, k, :], start=(k == 0), stop=(k == INNER // P - 1))
                            last.then_inc(y_psum, 1)

                        def transpose_ff(t, b, l):
                            if not (isinstance(t, int) and t == l == b == 0):
                                pe.wait_ge(zout_ready, at(t, b, l) - 1)
                            pe.wait_ge(hn_ready, at(t, b, l))
                            nc.tensor.transpose(M[:, 0:P], hn[:, :], ident[:, :]).then_inc(h2T_psum, 1)

                        def up(t, b, l):
                            pe.wait_ge(h2T_ready, at(t, b, l))
                            for k, (r, n) in enumerate(HIDC):
                                nc.tensor.matmul(Q[0:n, 2, k * P:(k + 1) * P], LW[l]["w1"][:, r:r + n], h2T[:, :], start=True, stop=True)
                                last = nc.tensor.matmul(M[0:n, k * P:(k + 1) * P], LW[l]["w1"][:, HID + r:HID + r + n], h2T[:, :], start=True, stop=True)
                            last.then_inc(up_psum, 1)

                        def down(t, b, l):
                            for k, (r, n) in enumerate(HIDC):
                                nc.tensor.matmul(M[:, 0:D], uT[0:n, k, :], LW[l]["w2"][0:n, k, :], start=(k == 0), stop=False)
                            nc.tensor.matmul(M[:, 0:D], ones[:, :], LW[l]["b2"][:, :], start=False, stop=True).then_inc(y2_psum, 1)

                        def step(N, X, R, Y, Z, H, W):
                            if R:
                                pe.wait_ge(ab_ready, 2 * at(*R))
                                pe.wait_ge(sq_ready, 2 * at(*R))
                            if Y:
                                transpose_qk(*Y)
                            if Z:
                                out2(*Z)
                            if Y:
                                scores(*Y, 0)
                                scores(*Y, 1)
                            if X:
                                pe.wait_ge(hT_ready, at(*X))
                                project(*X, 0)
                                project(*X, 1)
                            if W:
                                pe.wait_ge(u_ready, at(*W))
                            if X:
                                project(*X, 2)
                            if W:
                                down(*W)
                            if Y:
                                transpose_p(*Y, 0)
                                transpose_p(*Y, 1)
                            if N:
                                transpose_in(*N)
                            if Y:
                                values(*Y, 0)
                            if H:
                                transpose_ff(*H)
                            if Y:
                                values(*Y, 1)
                            if X:
                                pe.wait_ge(v_ready, at(*X))
                            if N:
                                pe.wait_ge(hT_ready, at(*N))
                            if H:
                                up(*H)
                            if Y:
                                out(*Y)
                        steps(pe, step)

                    @block.scalar
                    def _(act):
                        def step(N, X, R, Y, Z, H, W):
                            def exp(g_):
                                act.wait_ge(d_ready, atg(*Y, g_))
                                d4 = diff[g_][:, :, :].rearrange("p (j k) n -> p j k n", j=2)
                                nc.scalar.activation(pr[g_][:, :, 0:2 * P].rearrange("p j (k n) -> p j k n", k=2), d4[:, :, :, WIN:], ACT.Exp)
                                nc.scalar.activation(pr[g_][:, :, 2 * P:].rearrange("p j (k n) -> p j k n", k=2), d4[:, :, :, 0:WIN], ACT.Exp).then_inc(exp_ready, 1)

                            def square(j):
                                b = X[1]
                                nc.scalar.activation(sq[b][:, j * INNER:(j + 1) * INNER], Q[:, j, :], ACT.Square).then_inc(sq_ready, 1)

                            def copy_p(g_):
                                act.wait_ge(pT_psum, atg(*Y, g_))
                                nc.scalar.copy(pT[g_][:, 0:3, :], A[g_][:, 0, 0:3 * P].rearrange("p (m n) -> p m n", n=P)).then_inc(pTa_ready, 1)
                            if Y:
                                act.wait_ge(qT_psum, at(*Y))
                                nc.scalar.copy(qT[Y[1]][:, :, :], Q[:, 0, :].rearrange("p (k n) -> p k n", n=P)).then_inc(qT_ready, 1)
                                t, b, l = Y
                                before = V[b][WIN:, bass.ds(t, 1), :, 0:D1].rearrange("p o (g c j) d -> p c (o g) j d", g=HG, c=2, j=2)
                                for k in range(2):
                                    dst = VB[b][k * WIN:(k + 1) * WIN, :, k * (D1 + 1):k * (D1 + 1) + D1].rearrange("p (g j) d -> p g j d", g=HG)
                                    nc.scalar.copy(dst, before[:, k])
                            if R:
                                act.wait_ge(ss_ready, at(*R))
                                nc.scalar.activation(ss[R[1]][:, :], ss[R[1]][:, :], ACT.Sqrt).then_inc(norm_ready, 1)
                            if W:
                                act.wait_ge(up_psum, at(*W))
                                for k, (r, n) in enumerate(HIDC):
                                    last = nc.scalar.activation(gg[0:n, k, :], M[0:n, k * P:(k + 1) * P], ACT.Gelu, bias=LW[W[2]]["b1g"][0:n, k:k + 1])
                                last.then_inc(gelu_ready, 1)
                            if Y:
                                exp(0)
                                exp(1)
                            if X:
                                t, b, l = X
                                act.wait_ge(qkv_psum, 3 * at(t, b, l))
                                nc.scalar.copy(V[b][:, t + 1, :, 0:D1], Q[:, 2, :].rearrange("p (h d) -> p h d", h=H1)).then_inc(v_ready, 1)
                            if Y:
                                copy_p(0)
                            if X:
                                square(1)
                            if Y:
                                copy_p(1)
                            if N:
                                act.wait_ge(h1T_psum, at(*N))
                                nc.scalar.copy(hT[N[1]][:, :], Q[:, 2, 0:P]).then_inc(hT_ready, 1)
                            if X:
                                act.wait_ge(ab_ready, 2 * at(t, b, l) - 1)
                                square(0)
                            if H:
                                act.wait_ge(h2T_psum, at(*H))
                                nc.scalar.activation(h2T[:, :], M[:, 0:P], ACT.Identity, bias=LW[H[2]]["lb"][:, 0:1], scale=LW[H[2]]["lg"][:, 0:1]).then_inc(h2T_ready, 1)
                            if Z:
                                act.wait_ge(var_ready, at(*Z))
                                nc.scalar.activation(rv[:, :], rv[:, :], ACT.Sqrt).then_inc(std_ready, 1)
                            if Y:
                                act.wait_ge(oT_psum, at(*Y))
                                nc.scalar.copy(oT[:, :, :], A[0][:, 1, :].rearrange("p (k n) -> p k n", n=P)).then_inc(oT_ready, 1)
                        steps(act, step)

                    @block.gpsimd
                    def _(pool):
                        def step(N, X, R, Y, Z, H, W):
                            if R:
                                t, b, l = R
                                pool.wait_ge(rn_ready, at(t, b, l))
                                pool.wait_ge(rot_sum, 2 * at(t, b, l))
                                nc.gpsimd.tensor_tensor(ra[b][:, :].rearrange("p (h d) -> p h d", d=D1), rb[b][:, :].rearrange("p (h d) -> p h d", d=D1),
                                                        bc(rn[b][:, :, None], [P, 2 * H1, D1]), ALU.mult).then_inc(rot_ready, 1)
                            if X:
                                t, b, l = X
                                for j in range(2):
                                    half = slice(j * INNER, (j + 1) * INNER)
                                    pool.wait_ge(ab_ready, 2 * at(t, b, l) - 1 + j)
                                    nc.gpsimd.tensor_tensor(rb[b][:, half], ra[b][:, half], rb[b][:, half], ALU.add).then_inc(rot_sum, 1)
                        steps(pool, step)

                    @block.vector
                    def _(dve):
                        hf = D1 // 2
                        LINKS = dict(R=1, Y=5, Z=2, H=1)

                        def step(N, X, R, Y, Z, H, W):
                            before = lambda u: at(*u) - 1 if u else 0 if N else last_unit
                            ch.base, ch.k = LINKS["R"] * before(R) + LINKS["Y"] * before(Y) + LINKS["Z"] * before(Z) + LINKS["H"] * before(H), 0
                            def soften(g_):
                                dve.wait_ge(s_psum, atg(*Y, g_))
                                ch.link(nc.vector.tensor_reduce(mx[g_][:, :], Sv[g_], AX, ALU.max))
                                nc.vector.tensor_tensor(diff[g_][:, :, :], Sv[g_], bc(mx[g_][:, :, None], [P, HH, KEYS]), ALU.subtract).then_inc(d_ready, 1)

                            def copy_p(g_):
                                dve.wait_ge(pT_psum, atg(*Y, g_))
                                nc.vector.tensor_copy(pT[g_][:, 3:, :], A[g_][:, 1, 0:3 * P].rearrange("p (m n) -> p m n", n=P)).then_inc(pTb_ready, 1)

                            def normalise(g_):
                                dve.wait_ge(o_psum, atg(*Y, g_))
                                O = A[g_][:, 0, 0:HH * (D1 + 1)].rearrange("p (h d) -> p h d", d=D1 + 1)
                                ch.link(nc.vector.reciprocal(rs[:, g_, :], O[:, :, D1]))
                                nc.vector.tensor_tensor(on[:, g_ * HH * D1:(g_ + 1) * HH * D1].rearrange("p (k j d) -> p j k d", k=2, j=2),
                                                        O[:, :, 0:D1].rearrange("p (j k) d -> p j k d", j=2),
                                                        bc(rs[:, g_, :, None].rearrange("p (j k) o -> p j k o", j=2), [P, 2, 2, D1]), ALU.mult).then_inc(on_ready, 1)
                            def rotate(j, terms=(0, 1)):
                                t, b, l = X
                                src = Q[:, j, :].rearrange("p (h d) -> p h d", d=D1)
                                d3 = lambda buf: buf[b][:, j * INNER:(j + 1) * INNER].rearrange("p (h d) -> p h d", d=D1)
                                if 0 in terms:
                                    nc.vector.tensor_tensor(d3(ra), src, bc(LW[l]["cosT"][:, bass.ds(t, 1), j, :], [P, H1, D1]), ALU.mult)
                                if 1 not in terms:
                                    return
                                for k in range(2):
                                    last = nc.vector.tensor_tensor(d3(rb)[:, :, k * hf:(k + 1) * hf], src[:, :, (1 - k) * hf:(2 - k) * hf],
                                                                   bc(LW[l]["sinT"][:, bass.ds(t, 1), j, k * hf:(k + 1) * hf], [P, H1, hf]), ALU.mult)
                                last.then_inc(ab_ready, 1)
                            if Y:
                                kb = kT[Y[1]]
                                ch.link(nc.vector.tensor_copy(kb[:, :, 0:WIN], kb[:, :, P:KEYS]))
                                dve.wait_ge(kT_psum, at(*Y))
                                nc.vector.tensor_copy(kb[:, :, WIN:KEYS], Q[:, 1, :].rearrange("p (k n) -> p k n", n=P)).then_inc(kT_ready, 1)
                            if Z:
                                tz, bz, lz = Z
                                dve.wait_ge(y_psum, at(*Z))
                                nc.vector.tensor_tensor(zmid[lz][:, bz, tz + 1, :], A[1][:, 1, 0:D], zin[lz][:, bz, tz + 1, :], ALU.add).then_inc(zmid_ready, 1)
                            if H:
                                dve.wait_ge(std_ready, at(*H))
                                ch.link(nc.vector.reciprocal(rv[:, :], rv[:, :]))
                                nc.vector.tensor_scalar(hn[:, :], hs2[H[1]][:, :], mv[:, 0:1], rv[:, :], ALU.subtract, ALU.mult).then_inc(hn_ready, 1)
                            if Y:
                                soften(0)
                            if W:
                                tw, bw, lw = W
                                dve.wait_ge(gelu_ready, at(*W))
                                for k, (r, n) in enumerate(HIDC):
                                    last = nc.vector.scalar_tensor_tensor(uT[0:n, k, :], Q[0:n, 2, k * P:(k + 1) * P], LW[lw]["b1a"][0:n, k:k + 1],
                                                                          gg[0:n, k, :], ALU.add, ALU.mult)
                                last.then_inc(u_ready, 1)
                            if Y:
                                soften(1)
                            if W:
                                dve.wait_ge(y2_psum, at(*W))
                                nc.vector.tensor_tensor(zout[lw][:, bw, tw + 1, :], M[:, 0:D], zmid[lw][:, bw, tw + 1, :], ALU.add).then_inc(zout_ready, 1)
                            if Z:
                                dve.wait_ge(hs2_in[bz], 48 * (lz * TB + tz) + 48)
                                ch.link(nc.vector.bn_stats(st[:, :], hs2[bz][:, :]))
                                nc.vector.memset(gatebuf[:, 0:1], 0.0)
                                ch.link(nc.vector.bn_aggr(mv[:, :], st[:, :]))
                                nc.vector.tensor_scalar_add(rv[:, :], mv[:, 1:2], EPS).then_inc(var_ready, 1)
                            if Y:
                                copy_p(0)
                            if X:
                                t, b, l = X
                                dve.wait_ge(qkv_psum, 3 * at(t, b, l) - 1)
                                rotate(0, (0,))
                            if Y:
                                copy_p(1)
                            if X:
                                rotate(0, (1,))
                            if R:
                                br = R[1]
                                dve.wait_ge(norm_ready, at(*R))
                                ch.link(nc.vector.tensor_scalar_max(ss[br][:, :], ss[br][:, :], 1e-12))
                                nc.vector.reciprocal(rn[br][:, :], ss[br][:, :]).then_inc(rn_ready, 1)
                            if X:
                                dve.wait_ge(sq_ready, 2 * at(t, b, l) - 1)
                                rotate(1)
                            if Y:
                                normalise(0)
                                normalise(1)
                            if X:
                                dve.wait_ge(sq_ready, 2 * at(t, b, l))
                                nc.vector.reduce_sum(ss[b][:, :], sq[b][:, :].rearrange("p (h d) -> p h d", d=D1), AX).then_inc(ss_ready, 1)
                            links = LINKS["R"] * bool(R) + LINKS["Y"] * bool(Y) + LINKS["Z"] * bool(Z) + LINKS["H"] * bool(H)
                            assert ch.k == links, ch.k

                        ch = Chain(dve, chain, 0)
                        steps(dve, step)

        def windowed(W):
            with ExitStack() as c:
                s = Space(c)
                z0, z1, z2 = (s.sb(n, [P, B, TB + 1, D]) for n in ("z0", "z1", "z2"))
                layernorm_stats(s, x, mean, rstd)
                zs, done = s.sem("z_set"), s.sem("x_new")
                with nc.Block() as block:
                    @block.vector
                    def _(dve):
                        nc.vector.memset(z0[:, :, 0, :], 0.0)
                        nc.vector.memset(z1[:, :, 0, :], 0.0)
                        nc.vector.memset(z2[:, :, 0, :], 0.0)
                        for b in range(B):
                            v = x[:, b * TB:(b + 1) * TB, :]
                            nc.vector.tensor_tensor(z0[:, b, 1:, :], v, bc(mean[:, b * TB:(b + 1) * TB, None], [P, TB, D]), ALU.subtract).then_inc(zs, 1)
                            dve.wait_ge(zs, 2 * b + 1)
                            nc.vector.tensor_tensor(z0[:, b, 1:, :], z0[:, b, 1:, :], bc(rstd[:, b * TB:(b + 1) * TB, None], [P, TB, D]), ALU.mult).then_inc(zs, 1)
                            dve.wait_ge(zs, 2 * b + 2)
                layers(W, z0, z1, z2)
                with nc.Block() as block:
                    @block.vector
                    def _(dve):
                        for b in range(B):
                            v = x[:, b * TB:(b + 1) * TB, :]
                            nc.vector.scalar_tensor_tensor(v, z0[:, b, 1:, :], 0.5, v, ALU.mult, ALU.add).then_inc(done, 1)
                        dve.wait_ge(done, B)

        def linear():
            with ExitStack() as c:
                s = Space(c)
                two = range(B)
                both = lambda name, shape: [s.sb(f"{name}{b}", shape) for b in two]
                wqkv, wo = s.sb("wqkv", [P, 3 * D]), s.sb("wo", [P, D])
                bqkv, bo = s.sb("bqkv", [P, 3 * D]), s.sb("bo", [1, D])
                gam, bet = s.sb("gam", [P, 2 * D]), s.sb("bet", [P, 2 * D])
                headm, causal, blockm = s.sb("headm", [P, H2]), s.sb("causal", [P, P]), s.sb("blockm", [P, H2 * VA])
                xc, hn, hT = both("xc", [P, D]), both("hn", [P, D]), both("hT", [P, P])
                qk, V = both("qk", [P, 2 * D]), both("V", [P, H2, VA])
                st, mv, sd = both("st", [P, 2, 6]), both("mv", [P, 2, 2]), both("sd", [P, 2])
                xn, ga, gb, ker = both("xn", [P, 2 * D]), both("ga", [P, 2 * D]), both("gb", [P, 2 * D]), both("ker", [P, 2 * D])
                kqT, qm, Am = both("kqT", [P, 2, P]), both("qm", [P, H2, P]), both("Am", [P, H2, P])
                state, cross = both("state", [P, H2 * VA]), both("cross", [P, H2 * VA])
                den, o, oT = both("den", [P, H2]), both("o", [P, D]), both("oT", [P, P])
                R = [s.ps(f"R{b}", [P, 4, 512]) for b in two]
                w_in, setup, chain = s.sem("weights"), s.sem("setup"), s.sem("steps")
                (hn_ready, hT_psum, hT_ready, qkv_psum, var_ready, std_ready, xn_ready, scaled, shifted_, ker_ready, kqT_psum,
                 kqT_ready, qm_ready, a_psum, am_ready, o_psum, cross_psum, state_ready, on_ready, oT_psum, oT_ready,
                 y_psum, x_new) = (s.sem(n) for n in (
                 "hn_ready hT_psum hT_ready qkv_psum var_ready std_ready xn_ready scaled shifted ker_ready kqT_psum "
                 "kqT_ready qm_ready a_psum am_ready o_psum cross_psum state_ready on_ready oT_psum oT_ready "
                 "y_psum x_new").split())
                at = lambda t, b: t * B + b + 1
                row = lambda n: a[n].rearrange("(o n) -> o n", o=1)
                loads = [(wqkv[:, :], a["L1_attn_Wqkv"]), (wo[:, :], a["L1_attn_Wo"]), (bqkv[:, :], row("L1_attn_bqkv").broadcast_to([P, 3 * D])),
                         (bo[:, :], row("L1_attn_bo")), (headm[:, :], a["c_headm"]), (causal[:, :], a["c_causal"]), (blockm[:, :], a["c_blockm"])]
                for k, n in enumerate("qk"):
                    loads += [(gam[:, k * D:(k + 1) * D], row(f"L1_attn_gamma_{n}").broadcast_to([P, D])),
                              (bet[:, k * D:(k + 1) * D], row(f"L1_attn_beta_{n}").broadcast_to([P, D]))]
                layernorm_stats(s, x, mean, rstd, loads, w_in)
                with nc.Block() as block:
                    @block.sync
                    def _(sp):
                        sp.wait_ge(w_in, 16 * len(loads))

                    @block.vector
                    def _(dve):
                        for b in two:
                            nc.vector.memset(V[b][:, :, :], 1.0).then_inc(setup, 1)
                            nc.vector.memset(state[b][:, :], 0.0).then_inc(setup, 1)
                        dve.wait_ge(setup, 2 * B)


                def steps(eng, body):
                    last = B * TB
                    parts = lambda i: [(n // B, n % B) if 0 <= n < last else None for n in range(i + 1, i - 3, -1)]
                    for i in range(-1, 2 * B):
                        body(*parts(i))
                    with eng.Fori(2, TB - 1) as t:
                        body((t, 1), (t, 0), (t - 1, 1), (t - 1, 0))
                        body((t + 1, 0), (t, 1), (t, 0), (t - 1, 1))
                    for i in range(last - B, last + 2):
                        body(*parts(i))

                first = lambda u: isinstance(u[0], int) and u[0] == 0
                with nc.Block() as block:
                    @block.tensor
                    def _(pe):
                        def products(unit, half):
                            b = unit[1]
                            for k in range(2 * half, 2 * half + 2):
                                last = nc.tensor.matmul(R[b][:, k, :], kqT[b][:, 1, :], qm[b][:, 4 * k:4 * k + 4, :], start=True, stop=True)
                            last.then_inc(a_psum, 1)

                        def step(N, X, Y, Z):
                            if X:
                                t, b = X
                                pe.wait_ge(hT_ready, at(t, b))
                                nc.tensor.matmul(R[b][:, 1, 0:3 * D], hT[b][:, :], wqkv[:, :], start=True, stop=True).then_inc(qkv_psum, 1)
                            if Y:
                                t, b = Y
                                pe.wait_ge(qm_ready, at(t, b))
                                if not first(Y):
                                    pe.wait_ge(x_new, at(t, b) - 2)
                                products(Y, 0)
                            if Z:
                                t, b = Z
                                pe.wait_ge(on_ready, at(t, b))
                                nc.tensor.transpose(R[b][:, 0, 0:P], o[b][:, :], ident[:, :]).then_inc(oT_psum, 1)
                            if Y:
                                products(Y, 1)
                            if Z:
                                t, b = Z
                                pe.wait_ge(oT_ready, at(t, b))
                                nc.tensor.matmul(R[b][:, 0, P:P + D], oT[b][:, :], wo[:, :], start=True, stop=False)
                                nc.tensor.matmul(R[b][:, 0, P:P + D], ones[:, :], bo[:, :], start=False, stop=True).then_inc(y_psum, 1)
                            if N:
                                t, b = N
                                pe.wait_ge(hn_ready, at(t, b))
                                if Z:
                                    pe.wait_ge(state_ready, at(*Z))
                                nc.tensor.transpose(R[1 - b][:, 3, 0:P], hn[b][:, :], ident[:, :]).then_inc(hT_psum, 1)
                            if X:
                                t, b = X
                                pe.wait_ge(ker_ready, at(t, b))
                                for k in range(2):
                                    last = nc.tensor.transpose(R[b][:, 2, k * P:(k + 1) * P], ker[b][:, k * D:(k + 1) * D], ident[:, :])
                                last.then_inc(kqT_psum, 1)
                            if Y:
                                t, b = Y
                                if not first(Y):
                                    pe.wait_ge(state_ready, at(t, b) - 2)
                                pe.wait_ge(am_ready, 2 * at(t, b) - 1)
                                nc.tensor.matmul(R[b][:, 0, 0:H2 * VA], kqT[b][:, 0, :], state[b][:, :], start=True, stop=False)
                                for h in range(H2):
                                    if h == H2 // 2:
                                        pe.wait_ge(am_ready, 2 * at(t, b))
                                    last = nc.tensor.matmul(R[b][:, 0, h * VA:(h + 1) * VA], Am[b][:, h, :], V[b][:, h, :], start=False, stop=(h == H2 - 1))
                                last.then_inc(o_psum, 1)
                                nc.tensor.matmul(R[b][:, 3, 0:H2 * VA], ker[b][:, D:], V[b][:, :, :], start=True, stop=True).then_inc(cross_psum, 1)
                        steps(pe, step)

                    @block.scalar
                    def _(act):
                        def step(N, X, Y, Z):
                            if X:
                                t, b = X
                                act.wait_ge(var_ready, at(t, b))
                                nc.scalar.activation(sd[b][:, :], mv[b][:, :, 1], ACT.Sqrt, scale=D / (D - 1)).then_inc(std_ready, 1)
                            if Z:
                                t, b = Z
                                act.wait_ge(oT_psum, at(t, b))
                                nc.scalar.copy(oT[b][:, :], R[b][:, 0, 0:P]).then_inc(oT_ready, 1)
                            if X:
                                t, b = X
                                act.wait_ge(shifted_, at(t, b))
                                nc.scalar.activation(ker[b][:, :], gb[b][:, :], ACT.Square).then_inc(ker_ready, 1)
                            if N:
                                t, b = N
                                act.wait_ge(hT_psum, at(t, b))
                                nc.scalar.copy(hT[b][:, :], R[1 - b][:, 3, 0:P]).then_inc(hT_ready, 1)
                            if X:
                                t, b = X
                                act.wait_ge(kqT_psum, at(t, b))
                                nc.scalar.copy(kqT[b][:, :, :], R[b][:, 2, 0:2 * P].rearrange("p (k n) -> p k n", k=2)).then_inc(kqT_ready, 1)
                        steps(act, step)

                    @block.gpsimd
                    def _(pool):
                        def step(N, X, Y, Z):
                            if X:
                                t, b = X
                                pool.wait_ge(xn_ready, at(t, b))
                                nc.gpsimd.tensor_tensor(ga[b][:, :], xn[b][:, :], gam[:, :], ALU.mult).then_inc(scaled, 1)
                                pool.wait_ge(scaled, at(t, b))
                                nc.gpsimd.tensor_tensor(gb[b][:, :], ga[b][:, :], bet[:, :], ALU.add).then_inc(shifted_, 1)
                        steps(pool, step)

                    @block.vector
                    def _(dve):
                        ch = Chain(dve, chain, 0)
                        LINKS = dict(N=1, X=4, Y=3)

                        def step(N, X, Y, Z):
                            before = lambda u: at(*u) - 1 if u else 0 if N else B * TB
                            ch.base, ch.k = LINKS["N"] * before(N) + LINKS["X"] * before(X) + LINKS["Y"] * before(Y), 0
                            if X:
                                t, b = X
                                dve.wait_ge(qkv_psum, at(t, b))
                                qkv = R[b][:, 1, 0:3 * D]
                                nc.vector.tensor_tensor(V[b][:, :, 0:D2], qkv[:, 2 * D:].rearrange("p (h d) -> p h d", d=D2),
                                                        bqkv[:, 2 * D:].rearrange("p (h d) -> p h d", d=D2), ALU.add)
                                ch.link(nc.vector.tensor_tensor(qk[b][:, :], qkv[:, 0:2 * D], bqkv[:, 0:2 * D], ALU.add))
                                nc.vector.bn_stats(st[b][:, 0, :], qk[b][:, 0:D])
                                ch.link(nc.vector.bn_stats(st[b][:, 1, :], qk[b][:, D:]))
                                nc.vector.memset(gatebuf[:, :], 0.0)
                                nc.vector.bn_aggr(mv[b][:, 0, :], st[b][:, 0, :])
                                nc.vector.bn_aggr(mv[b][:, 1, :], st[b][:, 1, :]).then_inc(var_ready, 1)
                            if N:
                                t, b = N
                                xt = x[:, bass.ds(t + b * TB, 1), :].rearrange("p o d -> p (o d)")
                                ch.link(nc.vector.tensor_tensor(xc[b][:, :], xt, bc(mean[:, bass.ds(t + b * TB, 1)], [P, D]), ALU.subtract))
                                nc.vector.tensor_tensor(hn[b][:, :], xc[b][:, :], bc(rstd[:, bass.ds(t + b * TB, 1)], [P, D]), ALU.mult).then_inc(hn_ready, 1)
                            if X:
                                t, b = X
                                dve.wait_ge(std_ready, at(t, b))
                                ch.link(nc.vector.tensor_scalar_add(sd[b][:, :], sd[b][:, :], 1e-6))
                                ch.link(nc.vector.reciprocal(sd[b][:, :], sd[b][:, :]))
                                for k in range(2):
                                    last = nc.vector.tensor_scalar(xn[b][:, k * D:(k + 1) * D], qk[b][:, k * D:(k + 1) * D], mv[b][:, k, 0:1], sd[b][:, k:k + 1],
                                                                   ALU.subtract, ALU.mult)
                                last.then_inc(xn_ready, 1)
                            if Y:
                                t, b = Y
                                for k in range(2):
                                    dve.wait_ge(a_psum, 2 * at(t, b) - 1 + k)
                                    hs = slice(k * H2 // 2, (k + 1) * H2 // 2)
                                    nc.vector.tensor_tensor(Am[b][:, hs, :], R[b][:, 2 * k:2 * k + 2, :].rearrange("p k (h n) -> p (k h) n", n=P),
                                                            bc(causal[:, None, :], [P, H2 // 2, P]), ALU.mult).then_inc(am_ready, 1)
                            if Z:
                                t, b = Z
                                dve.wait_ge(y_psum, at(t, b))
                                xt = x[:, bass.ds(t + b * TB, 1), :].rearrange("p o d -> p (o d)")
                                nc.vector.tensor_tensor(xt, R[b][:, 0, P:P + D], xt, ALU.add).then_inc(x_new, 1)
                            if X:
                                t, b = X
                                dve.wait_ge(kqT_ready, at(t, b))
                                nc.vector.tensor_tensor(qm[b][:, :, :], bc(kqT[b][:, 0:1, :], [P, H2, P]), bc(headm[:, :, None], [P, H2, P]), ALU.mult).then_inc(qm_ready, 1)
                            if Y:
                                t, b = Y
                                dve.wait_ge(o_psum, at(t, b))
                                O = R[b][:, 0, 0:H2 * VA].rearrange("p (h d) -> p h d", d=VA)
                                ch.link(nc.vector.tensor_scalar_add(den[b][:, :], O[:, :, D2], 1e-6))
                                ch.link(nc.vector.reciprocal(den[b][:, :], den[b][:, :]))
                                nc.vector.tensor_tensor(o[b][:, :].rearrange("p (h d) -> p h d", d=D2), O[:, :, 0:D2], bc(den[b][:, :, None], [P, H2, D2]), ALU.mult).then_inc(on_ready, 1)
                                dve.wait_ge(cross_psum, at(t, b))
                                ch.link(nc.vector.tensor_tensor(cross[b][:, :], R[b][:, 3, 0:H2 * VA], blockm[:, :], ALU.mult))
                                nc.vector.tensor_tensor(state[b][:, :], state[b][:, :], cross[b][:, :], ALU.add).then_inc(state_ready, 1)
                            links = LINKS["N"] * bool(N) + LINKS["X"] * bool(X) + LINKS["Y"] * bool(Y)
                            assert ch.k == links, ch.k
                        steps(dve, step)
                        dve.wait_ge(x_new, NT)

        def attention(r, over):
            with ExitStack() as c:
                s = Space(c)
                hT = s.sb("hT", [P, NT * P])
                cosq, sinq, cosk, sink = (s.sb(n, [P, S]) for n in ("cosq", "sinq", "cosk", "sink"))
                dist = s.sb("dist", [P, BIASW])
                slope, amp, sgn = s.sb("slope", [P, H0]), s.sb("amp", [P, H0]), s.sb("sgn", [P, 2])
                O_all = s.sb("O_all", [P, NT, H0 * D0])
                wo = s.sb("wo", [P, H0 * D0 // P, D])
                prepare(s, r, over, hT, cosq, sinq, cosk, sink, dist, slope, amp, sgn, wo)
                heads(hT, cosq, sinq, cosk, sink, dist, slope, amp, O_all)
                project(O_all, wo)

        def prepare(s, r, over, hT, cosq, sinq, cosk, sink, dist, slope, amp, sgn, wo):
            with ExitStack() as c:
                s = Space(c)
                xc, hn = s.sb("xc", [P, NT, D]), s.sb("hn", [P, NT, D])
                T4 = [s.ps(f"T{k}", [P, 512]) for k in range(4)]
                w_in, iotas, hn_ready, hT_psum, chain, sin_ready = (s.sem(n) for n in ("weights", "iotas", "hn_ready", "hT_psum", "chain", "sin_ready"))
                hT_ready = s.sem("hT_ready")
                loads = [(slope[:, :], a["L0_attn_bias_a"].rearrange("h a b -> (a b) h").broadcast_to([P, H0])),
                         (amp[:, :], a["L0_attn_bias_p"].rearrange("h a b -> (a b) h").broadcast_to([P, H0])), (sgn[:, :], a["c_sgn"]),
                         (wo[:, :, :], a["L0_attn_out_w"].rearrange("(k p) d -> p k d", p=P))]
                layernorm_stats(s, x, mean, rstd, loads, w_in)
                with nc.Block() as block:
                    @block.gpsimd
                    def _(pool):
                        nc.gpsimd.iota(dist[:, :], pattern=[[1, BIASW]], base=P - S, channel_multiplier=-1, allow_small_or_imprecise_dtypes=True).then_inc(iotas, 1)
                        pool.wait_ge(iotas, 1)

                    @block.tensor
                    def _(pe):
                        for t in range(NT):
                            if t % 4 == 0:
                                pe.wait_ge(hn_ready, t // 4 + 1)
                            last = nc.tensor.transpose(T4[t // 4][:, (t % 4) * P:(t % 4 + 1) * P], hn[:, t, :], ident[:, :])
                            if t % 4 == 3:
                                last.then_inc(hT_psum, 1)

                    @block.scalar
                    def _(act):
                        nc.scalar.activation(sink[:, :], r[:, :], ACT.Sin).then_inc(sin_ready, 1)
                        nc.scalar.activation(cosk[:, :], over[:, :], ACT.Sin).then_inc(sin_ready, 1)
                        for k in range(4):
                            act.wait_ge(hT_psum, k + 1)
                            nc.scalar.copy(hT[:, k * 512:(k + 1) * 512], T4[k][:, :]).then_inc(hT_ready, 1)
                        act.wait_ge(hT_ready, 4)
                        act.wait_ge(sin_ready, 2)

                    @block.vector
                    def _(dve):
                        ch = Chain(dve, chain, 0)
                        for k in range(4):
                            sl = slice(4 * k, 4 * k + 4)
                            ch.link(nc.vector.tensor_tensor(xc[:, sl, :], x[:, sl, :], bc(mean[:, sl, None], [P, 4, D]), ALU.subtract))
                            nc.vector.tensor_tensor(hn[:, sl, :], xc[:, sl, :], bc(rstd[:, sl, None], [P, 4, D]), ALU.mult).then_inc(hn_ready, 1)
                        dve.wait_ge(w_in, 16 * 4)
                        dve.wait_ge(iotas, 1)
                        ch.link(nc.vector.scalar_tensor_tensor(dist[:, :], dist[:, :], -1.0, dist[:, :], ALU.mult, ALU.max))
                        ch.link(nc.vector.tensor_scalar_max(slope[:, :], slope[:, :], 0.01))
                        ch.link(nc.vector.tensor_scalar_max(amp[:, :], amp[:, :], 0.01))
                        dve.wait_ge(sin_ready, 2)
                        nc.vector.tensor_scalar(sinq[:, :], sink[:, :], sgn[:, 1:2], None, ALU.mult)
                        ch.link(nc.vector.tensor_scalar(cosq[:, :], cosk[:, :], -1.0 / D0 ** 0.5, None, ALU.mult))
                        ch.link(nc.vector.tensor_scalar(sink[:, :], sink[:, :], sgn[:, 0:1], None, ALU.mult))

        def heads(hT, cosq, sinq, cosk, sink, dist, slope, amp, O_all):
            with ExitStack() as c:
                s = Space(c)
                w = s.sb("w", [P, 5, P])
                ab = s.sb("ab", [P, 4])
                qT, kT = s.sb("qT", [P, NT * P]), s.sb("kT", [P, NT * P])
                m1, m2 = s.sb("m1", [P, 2, 512]), s.sb("m2", [P, 2, 512])
                V = s.sb("V", [P, NT, 2, D0 + 1])
                bias = s.sb("bias", [P, 2, BIASW])
                y, pr, pT = s.sb("y", [P, 2, S]), s.sb("pr", [P, 2, S]), s.sb("pT", [P, 2, TB, P])
                U = 2 * NT
                low, rz = s.sb("low", [P, U]), s.sb("rz", [P, 2])
                Sp = [s.ps(f"S{k}", [P, S]) for k in range(2)]
                Tp = s.ps("Tp", [P, 2, 512])
                Op = [s.ps(f"O{k}", [P, 512]) for k in range(2)]
                (w_in, setup, ab_ready, ln_ready, bias_ready, proj_psum, m_ready, rot_ready, v_psum, v_ready, s_psum, y_ready, exp_ready,
                 ta_psum, tb_psum, ta_ready, tb_ready, o_psum, r_ready, o_ready) = (s.sem(n) for n in (
                 "weights setup ab_ready ln_ready bias_ready proj_psum m_ready rot_ready v_psum v_ready s_psum y_ready exp_ready "
                 "ta_psum tb_psum ta_ready tb_ready o_psum r_ready o_ready").split())
                LAST = U + 3
                tile, head, batch = (lambda v: v // 2), (lambda v: v % 2), (lambda v: v // 2 // TB)

                with nc.Block() as block:
                    @block.vector
                    def _(dve):
                        nc.vector.memset(V[:, :, :, D0:], 1.0).then_inc(setup, 1)
                        dve.wait_ge(setup, 1)

                with nc.Block() as block:
                    @block.sync
                    def _(sp):
                        wsrc = a["L0_attn_w5"]
                        sp.dma_start(w[:, :, :], wsrc[0]).then_inc(w_in, 16)
                        with sp.Fori(0, PAIRS - 1) as i:
                            sp.wait_ge(v_psum, 4 * i + 4)
                            sp.dma_start(w[:, :, :], wsrc[bass.ds(i + 1, 1)].rearrange("o p k n -> p (o k) n")).then_inc(w_in, 16)

                    @block.tensor
                    def _(pe):
                        with pe.Fori(0, PAIRS) as i:
                            pe.wait_ge(w_in, 16 * i + 16)
                            for j in range(8):
                                if j >= 2:
                                    pe.wait_ge(m_ready, 8 * i + j - 1)
                                for k in range(2):
                                    last = nc.tensor.matmul(Sp[j % 2][:, k * 512:(k + 1) * 512], w[:, 2 * (j % 2) + k, :],
                                                            hT[:, (j // 2) * 512:(j // 2 + 1) * 512], start=True, stop=True)
                                last.then_inc(proj_psum, 1)
                            for k in range(4):
                                if k >= 2:
                                    pe.wait_ge(v_ready, 4 * i + k - 1)
                                for t in range(4):
                                    last = nc.tensor.matmul(Tp[:, k % 2, t * P:(t + 1) * P], hT[:, (4 * k + t) * P:(4 * k + t + 1) * P], w[:, 4, :],
                                                            start=True, stop=True)
                                last.then_inc(v_psum, 1)
                            pe.wait_ge(rot_ready, 8 * i + 8)
                            pe.wait_ge(v_ready, 4 * i + 4)
                            for n in range(LAST):
                                v = n
                                if v < U:
                                    if v >= 2:
                                        pe.wait_ge(y_ready, U * i + v - 1)
                                    r = head(v) * D0
                                    for k in range(2):
                                        last = nc.tensor.matmul(Sp[v % 2][:, k * 512:(k + 1) * 512], qT[r:r + D0, tile(v) * P:(tile(v) + 1) * P],
                                                                kT[r:r + D0, batch(v) * S + k * 512:batch(v) * S + (k + 1) * 512], start=True, stop=True)
                                    last.then_inc(s_psum, 1)
                                v = n - 2
                                if 0 <= v < U:
                                    pe.wait_ge(exp_ready, U * i + v + 1)
                                    for k in range(TB):
                                        if v >= 1 and k == 0:
                                            pe.wait_ge(ta_ready, U * i + v)
                                        if v >= 1 and k == 4:
                                            pe.wait_ge(tb_ready, U * i + v)
                                        last = nc.tensor.transpose(Tp[:, k // 4, (k % 4) * P:(k % 4 + 1) * P], pr[:, v % 2, k * P:(k + 1) * P], ident[:, :])
                                        if k == 3:
                                            last.then_inc(ta_psum, 1)
                                    last.then_inc(tb_psum, 1)
                                v = n - 3
                                if 0 <= v < U:
                                    if v >= 2:
                                        pe.wait_ge(o_ready, U * i + v - 1)
                                    pe.wait_ge(ta_ready, U * i + v + 1)
                                    pe.wait_ge(tb_ready, U * i + v + 1)
                                    for k in range(TB):
                                        last = nc.tensor.matmul(Op[v % 2][:, 0:D0 + 1], pT[:, v % 2, k, :], V[:, batch(v) * TB + k, head(v), :],
                                                                start=(k == 0), stop=(k == TB - 1))
                                    last.then_inc(o_psum, 1)

                    @block.scalar
                    def _(act):
                        with act.Fori(0, PAIRS) as i:
                            act.wait_ge(ab_ready, i + 1)
                            for h in range(2):
                                nc.scalar.activation(bias[:, h, :], dist[:, :], ACT.Ln, bias=1.0, scale=ab[:, h:h + 1]).then_inc(ln_ready, 1)
                            for k in range(4):
                                act.wait_ge(v_psum, 4 * i + k + 1)
                                nc.scalar.copy(V[:, 4 * k:4 * k + 4, :, 0:D0], Tp[:, k % 2, :].rearrange("p (t h d) -> p t h d", t=4, h=2)).then_inc(v_ready, 1)
                            for n in range(LAST):
                                v = n - 2
                                if 0 <= v < U:
                                    act.wait_ge(tb_psum, U * i + v + 1)
                                    nc.scalar.copy(pT[:, v % 2, 4:, :], Tp[:, 1, :].rearrange("p (k n) -> p k n", n=P)).then_inc(tb_ready, 1)
                                v = n
                                if v < U:
                                    act.wait_ge(y_ready, U * i + v + 1)
                                    if v >= 2:
                                        act.wait_ge(tb_psum, U * i + v - 1)
                                    nc.scalar.activation(pr[:, v % 2, :], y[:, v % 2, :], ACT.Exp, bias=low[:, v:v + 1], scale=-1.0).then_inc(exp_ready, 1)

                    @block.gpsimd
                    def _(pool):
                        with pool.Fori(0, PAIRS) as i:
                            for j in range(8):
                                pool.wait_ge(m_ready, 8 * i + j + 1)
                                dst = (qT, kT)[j % 2]
                                nc.gpsimd.tensor_tensor(dst[:, (j // 2) * 512:(j // 2 + 1) * 512], m1[:, j % 2, :], m2[:, j % 2, :], ALU.add).then_inc(rot_ready, 1)

                    @block.vector
                    def _(dve):
                        with dve.Fori(0, PAIRS) as i:
                            nc.vector.tensor_copy(ab[:, 0:2], slope[:, bass.ds(2 * i, 2)])
                            nc.vector.tensor_copy(ab[:, 2:4], amp[:, bass.ds(2 * i, 2)]).then_inc(ab_ready, 1)
                            for j in range(8):
                                cs, sn = ((cosq, sinq), (cosk, sink))[j % 2]
                                pos = slice((j // 2 % 2) * 512, (j // 2 % 2 + 1) * 512)
                                if j >= 2:
                                    dve.wait_ge(rot_ready, 8 * i + j - 1)
                                dve.wait_ge(proj_psum, 8 * i + j + 1)
                                nc.vector.tensor_tensor(m1[:, j % 2, :], Sp[j % 2][:, 0:512], cs[:, pos], ALU.mult)
                                nc.vector.tensor_tensor(m2[:, j % 2, :], Sp[j % 2][:, 512:], sn[:, pos], ALU.mult).then_inc(m_ready, 1)
                            dve.wait_ge(ln_ready, 2 * i + 2)
                            dve.wait_ge(ab_ready, i + 1)
                            for h in range(2):
                                nc.vector.tensor_scalar(bias[:, h, :], bias[:, h, :], ab[:, 2 + h:3 + h], None, ALU.mult).then_inc(bias_ready, 1)
                            dve.wait_ge(bias_ready, 2 * i + 2)
                            for n in range(LAST):
                                v = n
                                if v < U:
                                    dve.wait_ge(s_psum, U * i + v + 1)
                                    if v >= 2:
                                        dve.wait_ge(exp_ready, U * i + v - 1)
                                    nc.vector.memset(gatebuf[:, v % 4:v % 4 + 1], 0.0)
                                    off = S - P - (tile(v) % TB) * P
                                    nc.vector.tensor_tensor_reduce(out=y[:, v % 2, :], in0=Sp[v % 2][:, :], in1=bias[:, head(v), off:off + S], scale=1.0, scalar=3e38,
                                                                   op0=ALU.add, op1=ALU.min, accum_out=low[:, v:v + 1]).then_inc(y_ready, 1)
                                v = n - 2
                                if 0 <= v < U:
                                    dve.wait_ge(ta_psum, U * i + v + 1)
                                    nc.vector.tensor_copy(pT[:, v % 2, 0:4, :], Tp[:, 0, :].rearrange("p (k n) -> p k n", n=P)).then_inc(ta_ready, 1)
                                v = n - 3
                                if 0 <= v < U:
                                    dve.wait_ge(o_psum, U * i + v + 1)
                                    nc.vector.reciprocal(rz[:, v % 2:v % 2 + 1], Op[v % 2][:, D0:D0 + 1]).then_inc(r_ready, 1)
                                    dve.wait_ge(r_ready, U * i + v + 1)
                                    nc.vector.tensor_scalar(O_all[:, tile(v), bass.ds(2 * D0 * i + head(v) * D0, D0)], Op[v % 2][:, 0:D0],
                                                            rz[:, v % 2:v % 2 + 1], None, ALU.mult).then_inc(o_ready, 1)

        def project(O_all, wo):
            with ExitStack() as c:
                s = Space(c)
                KC = H0 * D0 // P
                stage, oT = s.sb("stage", [P, 2, H0 * D0]), s.sb("oT", [P, 2, KC, P])
                Tp = [s.ps(f"T{k}", [P, 2, 512]) for k in range(2)]
                Y = [s.ps(f"Y{k}", [P, 512]) for k in range(2)]
                staged, t_psum, oT_ready, y_psum, x_new = (s.sem(n) for n in ("staged", "t_psum", "oT_ready", "y_psum", "x_new"))
                with nc.Block() as block:
                    @block.tensor
                    def _(pe):
                        def turn(i):
                            for k in range(2):
                                pe.wait_ge(staged, 2 * i + k + 1)
                                for n in range(KC):
                                    last = nc.tensor.transpose(Tp[k][:, n // 4, (n % 4) * P:(n % 4 + 1) * P], stage[:, k, n * P:(n + 1) * P], ident[:, :])
                                last.then_inc(t_psum, 1)
                            for k in range(2):
                                pe.wait_ge(oT_ready, 2 * i + k + 1)
                                if not isinstance(i, int):
                                    pe.wait_ge(x_new, 2 * i + k - 1)
                                for n in range(KC):
                                    last = nc.tensor.matmul(Y[k][:, 0:D], oT[:, k, n, :], wo[:, n, :], start=(n == 0), stop=(n == KC - 1))
                                last.then_inc(y_psum, 1)
                        turn(0)
                        with pe.Fori(1, NT // 2) as i:
                            turn(i)

                    @block.scalar
                    def _(act):
                        with act.Fori(0, NT // 2) as i:
                            for k in range(2):
                                act.wait_ge(t_psum, 2 * i + k + 1)
                                nc.scalar.copy(oT[:, k, :, :], Tp[k][:, :, :].rearrange("p a (b n) -> p (a b) n", n=P)).then_inc(oT_ready, 1)

                    @block.vector
                    def _(dve):
                        def stage_tiles(i):
                            for k in range(2):
                                nc.vector.tensor_scalar(stage[:, k, :], O_all[:, bass.ds(2 * i + k, 1), :].rearrange("p o n -> p (o n)"), 1.0, None, ALU.mult).then_inc(staged, 1)

                        def add(i):
                            for k in range(2):
                                dve.wait_ge(y_psum, 2 * i + k + 1)
                                xt = x[:, bass.ds(2 * i + k, 1), :]
                                nc.vector.tensor_tensor(xt, Y[k][:, 0:D], xt, ALU.add).then_inc(x_new, 1)
                        stage_tiles(0)
                        with dve.Fori(0, NT // 2 - 1) as i:
                            dve.wait_ge(t_psum, 2 * i + 2)
                            nc.vector.memset(gatebuf[:, 0:1], 0.0)
                            stage_tiles(i + 1)
                            add(i)
                        add(NT // 2 - 1)
                        dve.wait_ge(x_new, NT)

        def rotation_angles(s):
            freq, ang, turns, r, over = s.sb("freq", [P, 1]), s.sb("ang", [P, S]), s.sb("turns", [P, S]), s.sb("r", [P, S]), s.sb("over", [P, S])
            fetched, iota, chain = s.sem("frequencies"), s.sem("positions"), s.sem("angle_steps")
            nf = D0 // 2
            loads = [(freq[k * nf:(k + 1) * nf, :], a["L0_attn_rope_freqs"].rearrange("(p o) -> p o", o=1)) for k in range(P // nf)]
            PI = 3.1415925
            TWO_PI = 6.283185307179586
            MAGIC = 12582912.0
            C1 = 6.28125
            C2 = 1014 / 2 ** 19
            C3 = TWO_PI - C1 - C2

            def make(pool):
                ch = Chain(pool, chain, 0)
                nc.gpsimd.iota(ang[:, :], pattern=[[1, S]], base=0, channel_multiplier=0, allow_small_or_imprecise_dtypes=True).then_inc(iota, 1)
                pool.wait_ge(iota, 1)
                pool.wait_ge(fetched, 16 * len(loads))

                def scalar(dst, src, c1, c2, op1, op2=None):
                    ch.link(nc.gpsimd.tensor_scalar(dst[:, :], src[:, :], c1, c2, op1, op2) if op2 else nc.gpsimd.tensor_scalar(dst[:, :], src[:, :], c1, c2, op1))

                def add(dst, u, v):
                    ch.link(nc.gpsimd.tensor_tensor(dst[:, :], u[:, :], v[:, :], ALU.add))
                scalar(ang, ang, freq[:, :], None, ALU.mult)
                scalar(turns, ang, 1 / TWO_PI, MAGIC, ALU.mult, ALU.add)
                scalar(turns, turns, MAGIC, None, ALU.subtract)
                for k, part in enumerate((C1, C2, C3)):
                    scalar(over, turns, -part, None, ALU.mult)
                    add(r, ang if k == 0 else r, over)

                def wrap(v, below):
                    scalar(turns, v, PI, -TWO_PI, ALU.is_gt, ALU.mult)
                    add(v, v, turns)
                    if below:
                        scalar(turns, v, -PI, TWO_PI, ALU.is_lt, ALU.mult)
                        add(v, v, turns)
                    scalar(v, v, PI, -PI, ALU.min, ALU.max)
                wrap(r, True)
                scalar(over, r, TWO_PI / 4, None, ALU.add)
                wrap(over, False)
            return r, over, loads, fetched, make

        with ExitStack() as c:
            r, over, loads, fetched, make_angles = rotation_angles(Space(c))
            moe(loads, fetched, make_angles)
            attention(r, over)
        W, loads, tables = windowed_weights(g)
        fetched = g.sem("windowed_weights")
        moe(loads, fetched, lambda pool: windowed_tables(pool, g, W, len(loads), fetched, *tables))
        windowed(W)
        linear()
        windowed(W)
        s_out = g.sem("s_out")
        with nc.Block() as block:
            @block.sync
            def _(sp):
                sp.dma_start(out.rearrange("b (t p) d -> p (b t) d", p=P), x[:, :, :]).then_inc(s_out, 16)
                sp.wait_ge(s_out, 16)


def constants():
    import numpy as np
    c = {"c_ident": np.eye(P)}
    r, m = np.arange(P)[:, None, None], np.arange(P)[None, None, :]
    ch = np.arange(EC)[None, :, None]
    c["c_sel"] = (r % E == 2 * ch + m // F) & (r < 3 * E)
    c["c_rank"] = np.tile(E - np.arange(E), (P, 1))
    half = np.arange(0, D1, 2, dtype=np.float32)
    inv = (np.float32(1.0) / np.float32(10000.0) ** (half / np.float32(D1))).astype(np.float32)
    t = np.arange(S, dtype=np.float32)
    ang = (t[:, None] * inv[None, :]).astype(np.float32).astype(np.float64)
    base = (half + np.float32(0.4 * D1)) / np.float32(1.4 * D1)
    scale = base[None, :].astype(np.float64) ** ((t - S // 2) / (WIN // 2))[:, None].astype(np.float64)
    cos, sin = np.cos(ang), np.sin(ang)
    co = np.stack([np.tile(8.0 * cos * scale, 2), np.tile(cos / scale, 2)], 1)
    si = np.stack([np.concatenate([-8.0 * sin * scale, 8.0 * sin * scale], 1), np.concatenate([-sin / scale, sin / scale], 1)], 1)
    c["c_cos"], c["c_sin"] = (v.reshape(TB, P, 2, D1).transpose(1, 0, 2, 3) for v in (co, si))
    q, tt, j = np.arange(P)[:, None, None], np.arange(TB)[None, :, None], np.arange(KEYS)[None, None, :] - WIN
    c["c_mask"] = np.where((j > q) | (q > j + WIN) | (tt * P + j < 0), MASKED, 0.0)
    p = np.arange(P)
    first = p % D0 < D0 // 2
    c["c_sgn"] = np.stack([np.where(first, -1.0, 1.0), np.where(first, 1.0, -1.0) / D0 ** 0.5], 1)
    c["c_headm"] = p[:, None] // D2 == np.arange(H2)[None, :]
    c["c_causal"] = p[:, None] <= p[None, :]
    c["c_blockm"] = p[:, None] // D2 == np.arange(H2 * VA)[None, :] // VA
    return {k: np.ascontiguousarray(v, dtype=np.float32) for k, v in c.items()}


def kernel(**inputs):
    import numpy as _np
    import concourse.bacc as _bacc
    from concourse import mybir as _mybir
    from concourse.bass_utils import run_bass_kernel_spmd as _run

    nc = _bacc.Bacc("TRN2", target_bir_lowering=False, num_devices=1)
    arrays, args = {}, {}
    data = dict(inputs)
    w = _np.asarray(data.pop("L0_attn_qkv_w")).reshape(3, PAIRS, 2, 2, D0 // 2, D)
    q, k, v = w
    data["L0_attn_w5"] = _np.stack([m.reshape(PAIRS, P, D) for m in (q, q[:, :, ::-1], k, k[:, :, ::-1], v)], 1).transpose(0, 3, 1, 2)
    data["L0_attn_out_w"] = _np.ascontiguousarray(_np.asarray(data["L0_attn_out_w"]).T)
    data.update(constants())
    for name, v in data.items():
        v = _np.ascontiguousarray(v)
        arrays[f"in_{name}"] = v
        args[name] = nc.dram_tensor(f"in_{name}", v.shape, _mybir.dt.from_np(v.dtype), kind="ExternalInput").ap()
    out = nc.dram_tensor("out_0_dram", (B, S, D), _mybir.dt.float32, kind="ExternalOutput").ap()
    build(nc, args, out)
    r = _run(nc, [arrays], core_ids=[0])
    return r.results[0]["out_0_dram"]
```
